# Optimizing a Trainium2 kernel written in Bass

```python
import numpy as np
import jax
import jax.numpy as jnp

def _softmax(x, axis=-1):
    return jax.nn.softmax(x, axis=axis)

def _gelu(x):
    return jax.nn.gelu(x, approximate=True)

def _silu(x):
    return jax.nn.silu(x)

def _sigmoid(x):
    return jax.nn.sigmoid(x)

def _layernorm(x, axis=-1, eps=1e-05):
    m = jnp.mean(x, axis=axis, keepdims=True)
    v = jnp.var(x, axis=axis, keepdims=True)
    return (x - m) / jnp.sqrt(v + eps)

def _scatter_add(tgt, idx, src, axis=0):
    return tgt.at[idx].add(src)

def _segment_sum(src, seg, n):
    return jax.ops.segment_sum(src, seg, n)
kernel_name = 'mk_lm_tower_d2_tok_ids512_r4_7a8bae'

def setup_inputs(seed: int=0):
    np.random.seed(seed)
    _w = jnp.asarray

    def _rec_inputs():
        import jax
        import jax.numpy as jnp
        _rk = jax.random.key(seed)
        x = jax.random.randint(jax.random.fold_in(_rk, 1), (64, 128), 0, 12564, jnp.int32)
        return x
    x = _rec_inputs()

    def _L0_tok_setup():
        import jax, jax.numpy as jnp
        import numpy as np
        VOCAB = 50257
        EMBED = 128
        key = jax.random.key(seed)
        k1, k2 = jax.random.split(key)
        x = jax.random.randint(k1, (8, 512), 0, VOCAB, dtype=jnp.int64 if jax.config.jax_enable_x64 else jnp.int32)
        w = jax.random.normal(k2, (VOCAB, EMBED), dtype=jnp.float32)
        return {'x': x, 'w': w}
    _L0_tok_all = _L0_tok_setup()
    _L0_tok_in = {k: v for k, v in _L0_tok_all.items() if k in ('w',)}
    del _L0_tok_all

    def _L0_attn_setup():
        import jax, jax.numpy as jnp
        import numpy as np
        B, T, D, K, V = (4, 1024, 128, 128, 128)
        key = jax.random.key(seed)
        ks = jax.random.split(key, 7)
        w = lambda k, shp: jax.random.normal(k, shp, dtype=jnp.float32) * 0.02
        return {'minibatch': jax.random.normal(ks[0], (B, T, D), dtype=jnp.float32), 'Wk': w(ks[1], (D, K)), 'bk': jnp.zeros((K,), jnp.float32), 'Wq': w(ks[2], (D, K)), 'bq': jnp.zeros((K,), jnp.float32), 'Wv': w(ks[3], (D, V)), 'bv': jnp.zeros((V,), jnp.float32)}
    _L0_attn_all = _L0_attn_setup()
    _L0_attn_in = {k: v for k, v in _L0_attn_all.items() if k in ('Wk', 'bk', 'Wq', 'bq', 'Wv', 'bv')}
    del _L0_attn_all

    def _L0_ffn_setup():
        import jax, jax.numpy as jnp
        import numpy as np
        G = 4
        EPG = 4
        E = 16
        KG = 2
        K = 2
        GTP = 0.9
        TP = 0.9
        SCALE = 1.0 / float(np.sqrt(G))

        def _routing_weights(xf, Wr, br, Wgate, bgate):
            N = xf.shape[0]
            gp = jax.nn.softmax(xf @ Wr + br, axis=-1)
            order = jnp.argsort(-gp, axis=-1)
            sp_k = jnp.take_along_axis(gp, order, axis=-1)[:, :KG]
            idx_k = order[:, :KG]
            act = jnp.cumsum(sp_k, axis=-1) <= GTP
            act = act.at[:, 0].set(True)
            mp = sp_k * act
            rn = mp / (jnp.sum(mp, axis=-1, keepdims=True) + 1e-09)
            w_group = jnp.zeros((N, G), xf.dtype).at[jnp.arange(N)[:, None], idx_k].set(rn)
            ep = jax.nn.softmax(jnp.einsum('nd,gde->nge', xf, Wgate) + bgate, axis=-1)
            eorder = jnp.argsort(-ep, axis=-1)
            esp = jnp.take_along_axis(ep, eorder, axis=-1)[:, :, :K]
            eidx = eorder[:, :, :K]
            eact = jnp.cumsum(esp, axis=-1) <= TP
            eact = eact.at[:, :, 0].set(True)
            emp = esp * eact
            ern = emp / (jnp.sum(emp, axis=-1, keepdims=True) + 1e-09)
            w_exp = jnp.zeros((N, G, EPG), xf.dtype).at[jnp.arange(N)[:, None, None], jnp.arange(G)[None, :, None], eidx].set(ern)
            return (w_group[:, :, None] * w_exp * SCALE).reshape(N, E)
        key = jax.random.key(seed)
        ks = jax.random.split(key, 6)
        B, T, D, H = (2, 256, 128, 512)
        x = jax.random.normal(ks[0], (B, T, D), jnp.float32)
        Wr = jax.random.normal(ks[1], (D, G), jnp.float32) * 0.02
        br = jnp.zeros((G,), jnp.float32)
        Wgate = jax.random.normal(ks[2], (G, D, EPG), jnp.float32) * 0.02
        bgate = jnp.zeros((G, EPG), jnp.float32)
        W1 = jax.random.normal(ks[3], (E, D, H), jnp.float32) * 0.02
        W3 = jax.random.normal(ks[4], (E, D, H), jnp.float32) * 0.02
        W2 = jax.random.normal(ks[5], (E, H, D), jnp.float32) * 0.02
        return {'x': x, 'Wr': Wr, 'br': br, 'Wgate': Wgate, 'bgate': bgate, 'W1': W1, 'W3': W3, 'W2': W2}
    _L0_ffn_all = _L0_ffn_setup()
    _L0_ffn_in = {k: v for k, v in _L0_ffn_all.items() if k in ('Wr', 'br', 'Wgate', 'bgate', 'W1', 'W3', 'W2')}
    del _L0_ffn_all

    def _L1_attn_setup():
        import jax, jax.numpy as jnp
        import numpy as np
        N_HEAD = 8
        D_MODEL = 128
        D_HEAD = D_MODEL // N_HEAD
        QLEN = 512
        BSZ = 4
        LN_EPS = 1e-05

        def _layer_norm(x, gamma, beta):
            mu = jnp.mean(x, axis=-1, keepdims=True)
            var = jnp.mean(jnp.square(x - mu), axis=-1, keepdims=True)
            return (x - mu) * jax.lax.rsqrt(var + LN_EPS) * gamma + beta

        def _pos_emb(qlen, d_model, dtype):
            pos_seq = jnp.arange(qlen - 1, -1, -1, dtype=dtype)
            inv_freq = 1.0 / 10000.0 ** (jnp.arange(0, d_model, 2, dtype=dtype) / d_model)
            sinusoid = pos_seq[:, None] * inv_freq[None, :]
            return jnp.concatenate([jnp.sin(sinusoid), jnp.cos(sinusoid)], axis=-1)

        def _rel_shift(x):
            q, r, b, n = x.shape
            x_padded = jnp.pad(x, ((0, 0), (1, 0), (0, 0), (0, 0)))
            x_padded = x_padded.reshape(r + 1, q, b, n)
            return x_padded[1:].reshape(q, r, b, n)
        key = jax.random.key(seed)
        ks = jax.random.split(key, 6)
        s = 0.02
        return {'w': jax.random.normal(ks[0], (QLEN, BSZ, D_MODEL), dtype=jnp.float32), 'Wqkv': jax.random.normal(ks[1], (3 * D_MODEL, D_MODEL), dtype=jnp.float32) * s, 'Wr': jax.random.normal(ks[2], (D_MODEL, D_MODEL), dtype=jnp.float32) * s, 'Wo': jax.random.normal(ks[3], (D_MODEL, D_MODEL), dtype=jnp.float32) * s, 'ln_gamma': jnp.ones((D_MODEL,), dtype=jnp.float32), 'ln_beta': jnp.zeros((D_MODEL,), dtype=jnp.float32), 'r_w_bias': jax.random.normal(ks[4], (N_HEAD, D_HEAD), dtype=jnp.float32) * s, 'r_r_bias': jax.random.normal(ks[5], (N_HEAD, D_HEAD), dtype=jnp.float32) * s}
    _L1_attn_all = _L1_attn_setup()
    _L1_attn_in = {k: v for k, v in _L1_attn_all.items() if k in ('Wqkv', 'Wr', 'Wo', 'ln_gamma', 'ln_beta', 'r_w_bias', 'r_r_bias')}
    del _L1_attn_all

    def _L1_ffn_setup():
        import jax, jax.numpy as jnp
        import numpy as np
        D_MODEL = 128
        D_FF = 512
        N_EXPERTS = 64
        K_ACTIVE = 2
        N_HASHES = 4
        LAYER_ID = 0
        SALT = 0.0
        BUCKET_SCALE = 8.0
        CAPACITY_FACTOR = 1.25
        key = jax.random.key(seed)
        k0, k1, k2, k3 = jax.random.split(key, 4)
        B, S = (4, 512)
        hidden_states = jax.random.normal(k0, (B, S, D_MODEL), dtype=jnp.float32)
        W_hash = jax.random.normal(k1, (N_HASHES, D_MODEL), dtype=jnp.float32) / np.float32(np.sqrt(D_MODEL))
        W1 = jax.random.normal(k2, (N_EXPERTS, D_MODEL, D_FF), dtype=jnp.float32) * np.float32(1.0 / np.sqrt(D_MODEL))
        b1 = jnp.zeros((N_EXPERTS, D_FF), dtype=jnp.float32)
        W2 = jax.random.normal(k3, (N_EXPERTS, D_FF, D_MODEL), dtype=jnp.float32) * np.float32(1.0 / np.sqrt(D_FF))
        b2 = jnp.zeros((N_EXPERTS, D_MODEL), dtype=jnp.float32)
        return {'hidden_states': hidden_states, 'W_hash': W_hash, 'W1': W1, 'b1': b1, 'W2': W2, 'b2': b2}
    _L1_ffn_all = _L1_ffn_setup()
    _L1_ffn_in = {k: v for k, v in _L1_ffn_all.items() if k in ('W_hash', 'W1', 'b1', 'W2', 'b2')}
    del _L1_ffn_all
    return {'x': x, 'L0_tok_w': _L0_tok_in['w'], 'L0_attn_Wk': _L0_attn_in['Wk'], 'L0_attn_bk': _L0_attn_in['bk'], 'L0_attn_Wq': _L0_attn_in['Wq'], 'L0_attn_bq': _L0_attn_in['bq'], 'L0_attn_Wv': _L0_attn_in['Wv'], 'L0_attn_bv': _L0_attn_in['bv'], 'L0_ffn_Wr': _L0_ffn_in['Wr'], 'L0_ffn_br': _L0_ffn_in['br'], 'L0_ffn_Wgate': _L0_ffn_in['Wgate'], 'L0_ffn_bgate': _L0_ffn_in['bgate'], 'L0_ffn_W1': _L0_ffn_in['W1'], 'L0_ffn_W3': _L0_ffn_in['W3'], 'L0_ffn_W2': _L0_ffn_in['W2'], 'L1_attn_Wqkv': _L1_attn_in['Wqkv'], 'L1_attn_Wr': _L1_attn_in['Wr'], 'L1_attn_Wo': _L1_attn_in['Wo'], 'L1_attn_ln_gamma': _L1_attn_in['ln_gamma'], 'L1_attn_ln_beta': _L1_attn_in['ln_beta'], 'L1_attn_r_w_bias': _L1_attn_in['r_w_bias'], 'L1_attn_r_r_bias': _L1_attn_in['r_r_bias'], 'L1_ffn_W_hash': _L1_ffn_in['W_hash'], 'L1_ffn_W1': _L1_ffn_in['W1'], 'L1_ffn_b1': _L1_ffn_in['b1'], 'L1_ffn_W2': _L1_ffn_in['W2'], 'L1_ffn_b2': _L1_ffn_in['b2']}

def reference(x, L0_tok_w, L0_attn_Wk, L0_attn_bk, L0_attn_Wq, L0_attn_bq, L0_attn_Wv, L0_attn_bv, L0_ffn_Wr, L0_ffn_br, L0_ffn_Wgate, L0_ffn_bgate, L0_ffn_W1, L0_ffn_W3, L0_ffn_W2, L1_attn_Wqkv, L1_attn_Wr, L1_attn_Wo, L1_attn_ln_gamma, L1_attn_ln_beta, L1_attn_r_w_bias, L1_attn_r_r_bias, L1_ffn_W_hash, L1_ffn_W1, L1_ffn_b1, L1_ffn_W2, L1_ffn_b2):
    import jax
    import jax.numpy as jnp

    def _L0_tok_ref(x, w):
        import jax, jax.numpy as jnp
        import numpy as np
        VOCAB = 50257
        EMBED = 128
        return jnp.take(w, x, axis=0)

    def _L0_attn_ref(minibatch, Wk, bk, Wq, bq, Wv, bv):
        import jax, jax.numpy as jnp
        import numpy as np
        B, T, D, K, V = (4, 1024, 128, 128, 128)
        keys = minibatch @ Wk + bk
        queries = minibatch @ Wq + bq
        values = minibatch @ Wv + bv
        logits = jnp.einsum('btk,bsk->bts', queries, keys)
        t = logits.shape[1]
        mask = jnp.triu(jnp.ones((t, t), dtype=bool), k=1)
        logits = jnp.where(mask[None, :, :], -jnp.inf, logits)
        sqrt_k = jnp.asarray(np.sqrt(K), dtype=logits.dtype)
        probs = jax.nn.softmax(logits, axis=1) / sqrt_k
        read = jnp.einsum('bts,bsv->btv', probs, values)
        return minibatch + read

    def _L0_ffn_ref(x, Wr, br, Wgate, bgate, W1, W3, W2):
        import jax, jax.numpy as jnp
        import numpy as np
        G = 4
        EPG = 4
        E = 16
        KG = 2
        K = 2
        GTP = 0.9
        TP = 0.9
        SCALE = 1.0 / float(np.sqrt(G))

        def _routing_weights(xf, Wr, br, Wgate, bgate):
            N = xf.shape[0]
            gp = jax.nn.softmax(xf @ Wr + br, axis=-1)
            order = jnp.argsort(-gp, axis=-1)
            sp_k = jnp.take_along_axis(gp, order, axis=-1)[:, :KG]
            idx_k = order[:, :KG]
            act = jnp.cumsum(sp_k, axis=-1) <= GTP
            act = act.at[:, 0].set(True)
            mp = sp_k * act
            rn = mp / (jnp.sum(mp, axis=-1, keepdims=True) + 1e-09)
            w_group = jnp.zeros((N, G), xf.dtype).at[jnp.arange(N)[:, None], idx_k].set(rn)
            ep = jax.nn.softmax(jnp.einsum('nd,gde->nge', xf, Wgate) + bgate, axis=-1)
            eorder = jnp.argsort(-ep, axis=-1)
            esp = jnp.take_along_axis(ep, eorder, axis=-1)[:, :, :K]
            eidx = eorder[:, :, :K]
            eact = jnp.cumsum(esp, axis=-1) <= TP
            eact = eact.at[:, :, 0].set(True)
            emp = esp * eact
            ern = emp / (jnp.sum(emp, axis=-1, keepdims=True) + 1e-09)
            w_exp = jnp.zeros((N, G, EPG), xf.dtype).at[jnp.arange(N)[:, None, None], jnp.arange(G)[None, :, None], eidx].set(ern)
            return (w_group[:, :, None] * w_exp * SCALE).reshape(N, E)
        B, T, D = x.shape
        xf = x.reshape(-1, D)
        tw = _routing_weights(xf, Wr, br, Wgate, bgate)
        out = jnp.zeros_like(xf)
        for e in range(E):
            h = jax.nn.silu(xf @ W1[e]) * (xf @ W3[e])
            out = out + tw[:, e:e + 1] * (h @ W2[e])
        return out.reshape(B, T, D)

    def _L1_attn_ref(w, Wqkv, Wr, Wo, ln_gamma, ln_beta, r_w_bias, r_r_bias):
        import jax, jax.numpy as jnp
        import numpy as np
        N_HEAD = 8
        D_MODEL = 128
        D_HEAD = D_MODEL // N_HEAD
        QLEN = 512
        BSZ = 4
        LN_EPS = 1e-05

        def _layer_norm(x, gamma, beta):
            mu = jnp.mean(x, axis=-1, keepdims=True)
            var = jnp.mean(jnp.square(x - mu), axis=-1, keepdims=True)
            return (x - mu) * jax.lax.rsqrt(var + LN_EPS) * gamma + beta

        def _pos_emb(qlen, d_model, dtype):
            pos_seq = jnp.arange(qlen - 1, -1, -1, dtype=dtype)
            inv_freq = 1.0 / 10000.0 ** (jnp.arange(0, d_model, 2, dtype=dtype) / d_model)
            sinusoid = pos_seq[:, None] * inv_freq[None, :]
            return jnp.concatenate([jnp.sin(sinusoid), jnp.cos(sinusoid)], axis=-1)

        def _rel_shift(x):
            q, r, b, n = x.shape
            x_padded = jnp.pad(x, ((0, 0), (1, 0), (0, 0), (0, 0)))
            x_padded = x_padded.reshape(r + 1, q, b, n)
            return x_padded[1:].reshape(q, r, b, n)
        qlen, bsz, d_model = w.shape
        scale = 1.0 / D_HEAD ** 0.5
        r = _pos_emb(qlen, d_model, w.dtype)
        wn = _layer_norm(w, ln_gamma, ln_beta)
        heads = jnp.einsum('ibd,ed->ibe', wn, Wqkv)
        q_h, k_h, v_h = jnp.split(heads, 3, axis=-1)
        q_h = q_h.reshape(qlen, bsz, N_HEAD, D_HEAD)
        k_h = k_h.reshape(qlen, bsz, N_HEAD, D_HEAD)
        v_h = v_h.reshape(qlen, bsz, N_HEAD, D_HEAD)
        r_k = jnp.einsum('rd,ed->re', r, Wr).reshape(qlen, N_HEAD, D_HEAD)
        AC = jnp.einsum('ibnd,jbnd->ijbn', q_h + r_w_bias, k_h)
        BD = _rel_shift(jnp.einsum('ibnd,jnd->ijbn', q_h + r_r_bias, r_k))
        attn_score = (AC + BD) * scale
        attn_prob = jax.nn.softmax(attn_score, axis=1)
        attn_vec = jnp.einsum('ijbn,jbnd->ibnd', attn_prob, v_h)
        attn_vec = attn_vec.reshape(qlen, bsz, N_HEAD * D_HEAD)
        attn_out = jnp.einsum('ibe,de->ibd', attn_vec, Wo)
        return w + attn_out

    def _L1_ffn_ref(hidden_states, W_hash, W1, b1, W2, b2):
        import jax, jax.numpy as jnp
        import numpy as np
        D_MODEL = 128
        D_FF = 512
        N_EXPERTS = 64
        K_ACTIVE = 2
        N_HASHES = 4
        LAYER_ID = 0
        SALT = 0.0
        BUCKET_SCALE = 8.0
        CAPACITY_FACTOR = 1.25
        B, S, D = hidden_states.shape
        T = B * S
        x = hidden_states.reshape(T, D)
        scores = x @ W_hash.T
        buckets = jnp.mod(jnp.floor(scores * BUCKET_SCALE + SALT).astype(jnp.int32) + LAYER_ID, N_EXPERTS)
        selected = buckets[:, :K_ACTIVE]
        flat_e = selected.reshape(-1)
        C = int(np.ceil(T * K_ACTIVE / N_EXPERTS * CAPACITY_FACTOR))
        oh = jax.nn.one_hot(flat_e, N_EXPERTS, dtype=jnp.int32)
        pos = jnp.sum((jnp.cumsum(oh, axis=0) - 1) * oh, axis=1)
        valid = pos < C
        pos_c = jnp.clip(pos, 0, C - 1)
        x_rep = jnp.repeat(x, K_ACTIVE, axis=0)
        buf = jnp.zeros((N_EXPERTS, C, D), dtype=x.dtype).at[flat_e, pos_c].add(jnp.where(valid[:, None], x_rep, 0.0))
        h = jax.nn.gelu(jnp.einsum('ecd,edf->ecf', buf, W1) + b1[:, None, :], approximate=False)
        y = jnp.einsum('ecf,efd->ecd', h, W2) + b2[:, None, :]
        out_pairs = jnp.where(valid[:, None], y[flat_e, pos_c], 0.0)
        out = out_pairs.reshape(T, K_ACTIVE, D).mean(axis=1)
        return out.reshape(B, S, D)
    h = _L0_tok_ref(x, L0_tok_w)
    h = h + _L0_attn_ref(_layernorm(h, axis=-1), L0_attn_Wk, L0_attn_bk, L0_attn_Wq, L0_attn_bq, L0_attn_Wv, L0_attn_bv)
    h = h + _L0_ffn_ref(_layernorm(h, axis=-1), L0_ffn_Wr, L0_ffn_br, L0_ffn_Wgate, L0_ffn_bgate, L0_ffn_W1, L0_ffn_W3, L0_ffn_W2)
    h = h + _L1_attn_ref(_layernorm(h, axis=-1), L1_attn_Wqkv, L1_attn_Wr, L1_attn_Wo, L1_attn_ln_gamma, L1_attn_ln_beta, L1_attn_r_w_bias, L1_attn_r_r_bias)
    h = h + _L1_ffn_ref(_layernorm(h, axis=-1), L1_ffn_W_hash, L1_ffn_W1, L1_ffn_b1, L1_ffn_W2, L1_ffn_b2)
    return h

_drawn_inputs = setup_inputs


def setup_inputs(seed=0):
    import zlib

    import numpy as np

    out = dict(_drawn_inputs(seed))
    spreads = {'L0_attn_bk': (0.0, 0.435),
     'L0_attn_bq': (0.0, 0.8),
     'L0_attn_bv': (0.0, 0.1),
     'L0_ffn_br': (0.0, 0.63),
     'L0_ffn_bgate': (0.0, 0.656),
     'L1_attn_ln_gamma': (1.0, 0.6),
     'L1_attn_ln_beta': (0.0, 0.548),
     'L1_ffn_b1': (0.0, 0.64),
     'L1_ffn_b2': (0.0, 0.422)}
    factors = {'L0_attn_Wk': 4.354,
     'L0_attn_Wq': 3.246,
     'L0_attn_Wv': 3.319,
     'L0_ffn_Wr': 5.13,
     'L0_ffn_Wgate': 4.208,
     'L0_ffn_W1': 3.716,
     'L0_ffn_W3': 3.825,
     'L0_ffn_W2': 3.81,
     'L1_attn_Wqkv': 3.201,
     'L1_attn_Wr': 8.0,
     'L1_attn_Wo': 2.935,
     'L1_attn_r_w_bias': 8.0,
     'L1_attn_r_r_bias': 8.0}
    for name, (base, spread) in spreads.items():
        noise = np.random.default_rng([zlib.crc32(name.encode()), seed]).standard_normal(out[name].shape)
        drawn = base * np.exp(spread * noise) if base else spread * noise
        out[name] = jnp.asarray(drawn.astype(out[name].dtype))
    for name, factor in factors.items():
        out[name] = (out[name] * factor).astype(out[name].dtype)
    return out
```

```python
from contextlib import ExitStack

import numpy as np
import concourse.bass as bass
from concourse import mybir

F32 = mybir.dt.float32
BF16 = mybir.dt.bfloat16
I32 = mybir.dt.int32
ALU = mybir.AluOpType
ACT = mybir.ActivationFunctionType
AX = mybir.AxisListType

P = 128
D = 128
TILES = 64
TOKENS = TILES * P
QUAD = 4
PAIRS_OF_QUADS = TILES // QUAD // 2
HID = 512
E0, G0, EPG0 = 16, 4, 4
PICKS0 = 4
BLOCKS0 = TOKENS * PICKS0 // P + E0
E1, CAP1, PICKS1 = 64, 320, 2
SLOTS1 = E1 * CAP1
HEADS, DH = 8, 16
EPS = 1e-5
MASKED = -1e30
SEED = 2


def made(n):
    return n + SEED + 1


def freed(n, bufs):
    return n + SEED + 1 - bufs


def bc(ap, dim, shape):
    return ap.unsqueeze(dim).to_broadcast(shape)


def turn(eng, tally):
    eng.sem_inc(tally, 1)


class Chain:

    def __init__(self, eng, sem):
        self.eng, self.sem, self.n = eng, sem, 0

    def __call__(self, ins):
        self.n += 1
        ins.then_inc(self.sem, 1)
        self.eng.wait_ge(self.sem, self.n)


def positions():
    seq = np.arange(TILES - 1, -1, -1, dtype=np.float32)
    freq = np.float32(1.0) / np.float32(10000.0) ** (np.arange(0, D, 2, dtype=np.float32) / np.float32(D))
    angle = (seq[:, None] * freq[None, :]).astype(np.float32)
    return np.ascontiguousarray(np.concatenate([np.sin(angle), np.cos(angle)], axis=-1).T.astype(np.float32))


TRANSPOSED = ("x", "L1_attn_Wqkv", "L1_attn_Wr", "L1_attn_Wo", "L1_ffn_W_hash")


def layout(inputs):
    laid = {n: np.ascontiguousarray(a.T if n in TRANSPOSED else a) for n, a in inputs.items()}
    b1 = inputs["L1_ffn_b1"].reshape(E1, HID // P, P)
    laid["L1_ffn_b1"] = np.ascontiguousarray(b1.transpose(2, 0, 1))
    laid["positions"] = positions()
    return laid


class Signals:

    def __init__(self, nc, ctx):
        self.nc, self.ctx, self.of_stage = nc, ctx, []

    def __call__(self, names, dma=""):
        own = {n: self.nc.alloc_semaphore(n) for n in names.split()}
        self.of_stage += own.values()
        return own | {n: self.ctx.enter_context(self.nc.semaphore(n)) for n in dma.split()}

    def end_stage(self):
        self.nc.clear_and_free_semaphores(self.of_stage)
        self.of_stage = []
        self.nc.all_engine_barrier()


def tower(nc, A, out, stop=None):
    ctx = ExitStack()

    sems = Signals(nc, ctx)

    def dram(name, shape, dt=F32):
        return nc.dram_tensor(name, shape, dt, kind="Internal").ap()

    XN1 = dram("XN1", (TOKENS, D))
    XS0 = dram("XS0", (BLOCKS0 * P, D))
    YS0 = dram("YS0", (BLOCKS0 * P, D))
    BD = dram("BD", (P, TILES + 1, HEADS * TILES))
    XN3 = dram("XN3", (TOKENS, D))
    XS1 = dram("XS1", (SLOTS1, D))
    YS1 = dram("YS1", (SLOTS1, D))

    with ctx:
        def keep(name, shape, dt=F32):
            return ctx.enter_context(nc.sbuf_tensor(name, shape, dt))

        ps = [ctx.enter_context(nc.psum_tensor(f"ps{i}", [P, 512], F32)) for i in range(8)]
        H = keep("H", [P, TILES, D])
        score = keep("score", [P, TILES, PICKS1])
        ident = keep("ident", [P, P])
        before = keep("before", [P, P], BF16)
        ones = keep("ones", [P, P], BF16)

        with ExitStack() as c0:
            def sb0(name, shape, dt=F32):
                return c0.enter_context(nc.sbuf_tensor(name, shape, dt))
            slot0 = sb0("slot0", [P, TILES, PICKS0], I32)
            weight0 = sb0("weight0", [P, TILES, PICKS0])
            with ExitStack() as c_w:
                def sbw(name, shape, dt=F32):
                    return c_w.enter_context(nc.sbuf_tensor(name, shape, dt))
                block_expert = sbw("block_expert", [1, BLOCKS0], I32)
                w1 = sbw("w1", [P, E0, HID])
                w3 = sbw("w3", [P, E0, HID])
                w2 = sbw("w2", [P, E0, HID // P, D])
                with nc.sbuf_tensor("logit", [P, TILES, 1 + G0, EPG0], F32) as logit:
                    layer0_attention(nc, A, sems, ps, H, ident, before, ones, logit, w1, w3, w2, XN1, XS0, XS1)
                    sems.end_stage()
                    if stop == "A":
                        return
                    layer0_routing(nc, sems, ps, before, ones, logit, slot0, weight0, block_expert)
                    sems.end_stage()
                if stop == "B":
                    return
                scatter_rows(nc, sems, "s0_", slot0, PICKS0, XN1, XS0, BLOCKS0 * P - 1)
                sems.end_stage()
                layer0_experts(nc, sems, ps, ident, block_expert, w1, w3, w2, XS0, YS0)
                sems.end_stage()
                if stop == "C":
                    return
            wnT = sb0("wnT", [P, P, TILES])
            layer0_combine(nc, A, sems, ps, H, ident, slot0, weight0, wnT, YS0, BD)
            sems.end_stage()
            if stop == "D":
                return
            readT = sb0("readT", [P, P, TILES])
            layer1_attention(nc, A, sems, ps, ident, wnT, readT, BD)
            sems.end_stage()
            layer1_project(nc, A, sems, ps, H, ident, readT, score, XN3)
            sems.end_stage()
            if stop == "E":
                return
        with ExitStack() as c1:
            slot_in = c1.enter_context(nc.sbuf_tensor("slot_in", [P, TILES, PICKS1], I32))
            slot_out = c1.enter_context(nc.sbuf_tensor("slot_out", [P, TILES, PICKS1], I32))
            share = c1.enter_context(nc.sbuf_tensor("share", [P, TILES, PICKS1], F32))
            layer1_routing(nc, sems, ps, before, ones, score, slot_in, slot_out, share)
            sems.end_stage()
            scatter_rows(nc, sems, "s1_", slot_in, PICKS1, XN3, XS1, SLOTS1 - 1)
            sems.end_stage()
            layer1_experts(nc, A, sems, ps, ident, XS1, YS1)
            sems.end_stage()
            layer1_combine(nc, sems, H, slot_out, share, YS1, out)
            sems.end_stage()


def layer0_attention(nc, A, sems, ps, H, ident, before, ones, logit, w1, w3, w2, XN1, XS0, XS1):
    ctx = ExitStack()
    with ctx:
        def sb(name, shape, dt=F32):
            return ctx.enter_context(nc.sbuf_tensor(name, shape, dt))
        zeros = sb("zeros", [P, 1024])
        causal = sb("causal", [P, P])
        power = sb("power", [P, QUAD])
        xidx = sb("xidx", [P, TILES], I32)
        wq, wk, wv = sb("wq", [P, D]), sb("wk", [P, D]), sb("wv", [P, D])
        bq, bk, bv = sb("bq", [P, 1]), sb("bk", [P, 1]), sb("bv", [P, D])
        wr = sb("wr", [P, 1 + G0, EPG0])
        br = sb("br", [P, 1 + G0, EPG0])
        idx4 = sb("idx4", [P, 2, QUAD], I32)
        h0 = sb("h0", [P, 2, QUAD, D])
        st = sb("st", [P, 2, QUAD, 6])
        mv = sb("mv", [P, 2, QUAD, 2])
        ve = sb("ve", [P, 2, QUAD])
        rstd = sb("rstd", [P, 2, QUAD])
        xn = sb("xn", [P, 2, QUAD, D])
        hx = sb("hx", [P, 2, QUAD, D])
        xT = sb("xT", [P, 2, QUAD * P])
        qT = sb("qT", [P, 2, QUAD * P])
        kT = sb("kT", [P, 2, QUAD * P])
        v = sb("v", [P, 2, QUAD, D])
        lm = sb("lm", [P, 2, QUAD, P])
        nmx = sb("nmx", [P, 2, QUAD])
        prob = sb("prob", [P, 2, QUAD, P])
        psum = sb("psum", [P, 2, QUAD])
        rsum = sb("rsum", [P, 2, QUAD])
        vs = sb("vs", [P, 2, QUAD, D])
        st1 = sb("st1", [P, 2, QUAD, 6])
        mv1 = sb("mv1", [P, 2, QUAD, 2])
        ve1 = sb("ve1", [P, 2, QUAD])
        rstd1 = sb("rstd1", [P, 2, QUAD])
        xn1 = sb("xn1", [P, 2, QUAD, D])
        x1T = sb("x1T", [P, 2, QUAD * P])
        pT, pQ, pK, pV, pL, pR, pT1, pG = ps
        s = sems("a_const a_eye a_idx a_stats a_mv a_ve a_rstd a_xn a_hx a_pT a_xT a_pQ a_pK a_pV a_qT a_kT "
                 "a_v a_pL a_lm a_max a_prob a_rsum a_vs a_pR a_h1 a_stats1 a_mv1 a_ve1 a_rstd1 a_xn1 "
                 "a_stored a_pT1 a_x1T a_pG a_logit a_zero a_p2 a_turn a_poolturn",
                 dma="a_load a_xload a_zeroed a_expw a_gather0 a_gather1 a_store0 a_store1")
        gather = [s["a_gather0"], s["a_gather1"]]
        store = [s["a_store0"], s["a_store1"]]
        n_load = 10
        XN1v = XN1.rearrange("(i t) d -> t i d", t=P)
        z0 = XS0.rearrange("(p r) d -> p (r d)", p=P)
        z1 = XS1.rearrange("(p r) d -> p (r d)", p=P)
        n_zero = (z0.shape[1] + z1.shape[1]) // 1024
        blk = ctx.enter_context(nc.Block())

        @blk.sync
        def _(sp):
            sp.dma_start(xidx[:], A["x"]).then_inc(s["a_xload"], 16)
            for dst, src in ((wq[:], A["L0_attn_Wq"]), (wk[:], A["L0_attn_Wk"]), (wv[:], A["L0_attn_Wv"]),
                             (bq[:], A["L0_attn_bq"].unsqueeze(1)), (bk[:], A["L0_attn_bk"].unsqueeze(1)),
                             (bv[:], A["L0_attn_bv"].partition_broadcast(P)),
                             (wr[:, 0, :], A["L0_ffn_Wr"]),
                             (wr[:, 1:, :], A["L0_ffn_Wgate"].rearrange("g d e -> d g e")),
                             (br[:, 0, :], A["L0_ffn_br"].partition_broadcast(P)),
                             (br[:, 1:, :], A["L0_ffn_bgate"].partition_broadcast(P))):
                sp.dma_start(dst, src).then_inc(s["a_load"], 16)
            sp.wait_ge(s["a_zero"], 1)
            with sp.Fori(0, z0.shape[1] // 1024) as i:
                sp.dma_start(z0[:, bass.ts(i, 1024)], zeros[:]).then_inc(s["a_zeroed"], 16)
            with sp.Fori(0, z1.shape[1] // 1024) as i:
                sp.dma_start(z1[:, bass.ts(i, 1024)], zeros[:]).then_inc(s["a_zeroed"], 16)
            with sp.Fori(0, E0) as e:
                sp.dma_start(w1[:, e, :], A["L0_ffn_W1"][e]).then_inc(s["a_expw"], 16)
                sp.dma_start(w3[:, e, :], A["L0_ffn_W3"][e]).then_inc(s["a_expw"], 16)
                sp.dma_start(w2[:, e, :, :], A["L0_ffn_W2"][e].rearrange("(c p) d -> p c d", p=P)).then_inc(s["a_expw"], 16)
            sp.sem_inc(s["a_stored"], SEED)
            with sp.Fori(0, PAIRS_OF_QUADS) as i:
                for p in range(2):
                    sp.wait_ge(s["a_xn1"], made(2 * i + p))
                    sp.dma_start(XN1v[:, bass.ds((2 * i + p) * QUAD, QUAD), :], xn1[:, p]).then_inc(store[p], 16)
                for p in range(2):
                    sp.wait_ge(store[p], 16 * i + 16)
                    sp.sem_inc(s["a_stored"], 1)
            sp.wait_ge(s["a_zeroed"], 16 * n_zero)
            sp.wait_ge(s["a_expw"], 48 * E0)

        @blk.gpsimd
        def _(pool):
            for name in ("a_idx", "a_rstd", "a_rstd1", "a_hx"):
                pool.sem_inc(s[name], SEED)
            nc.gpsimd.memset(zeros[:], 0.0).then_inc(s["a_zero"], 1)
            nc.gpsimd.memset(ident[:], 0.0)
            nc.gpsimd.memset(causal[:], 0.0)
            nc.gpsimd.memset(ones[:], 1.0)
            nc.gpsimd.memset(before[:], 1.0)
            nc.gpsimd.memset(power[:], -0.5).then_inc(s["a_eye"], 1)
            pool.wait_ge(s["a_eye"], 1)
            nc.gpsimd.affine_select(out=ident[:], in_=ident[:], compare_op=ALU.not_equal, fill=1.0, base=0,
                                    pattern=[[-1, P]], channel_multiplier=1)
            nc.gpsimd.affine_select(out=causal[:], in_=causal[:], compare_op=ALU.is_ge, fill=MASKED, base=0,
                                    pattern=[[1, P]], channel_multiplier=-1)
            nc.gpsimd.affine_select(out=before[:], in_=before[:], compare_op=ALU.is_gt, fill=0.0, base=0,
                                    pattern=[[1, P]], channel_multiplier=-1).then_inc(s["a_const"], 1)
            pool.wait_ge(s["a_const"], 1)
            pool.wait_ge(s["a_xload"], 16)

            def fetch(n, p):
                pool.wait_ge(s["a_h1"], freed(n, 2))
                nc.gpsimd.tensor_copy(idx4[:, p, :], xidx[:, bass.ds(n * QUAD, QUAD)]).then_inc(s["a_idx"], 1)
                pool.wait_ge(s["a_idx"], made(n))
                turn(pool, s["a_poolturn"])
                for j in range(QUAD):
                    nc.gpsimd.indirect_dma_start(
                        out=h0[:, p, j, :], out_offset=None, in_=A["L0_tok_w"],
                        in_offset=bass.IndirectOffsetOnAxis(ap=idx4[:, p, j:j + 1], axis=0)).then_inc(gather[p], 16)
            with pool.Fori(0, PAIRS_OF_QUADS) as i:
                for p in range(2):
                    fetch(2 * i + p, p)
                for p in range(2):
                    pool.wait_ge(s["a_ve"], made(2 * i + p))
                    nc.gpsimd.tensor_tensor(rstd[:, p, :], ve[:, p, :], power[:], ALU.pow).then_inc(s["a_rstd"], 1)
                for p in range(2):
                    pool.wait_ge(s["a_xn"], made(2 * i + p))
                    nc.gpsimd.tensor_tensor(hx[:, p], h0[:, p], xn[:, p], ALU.add).then_inc(s["a_hx"], 1)
                for p in range(2):
                    pool.wait_ge(s["a_ve1"], made(2 * i + p))
                    nc.gpsimd.tensor_tensor(rstd1[:, p, :], ve1[:, p, :], power[:], ALU.pow).then_inc(s["a_rstd1"], 1)

        @blk.vector
        def _(dve):
            for name in ("a_stats a_mv a_ve a_xn a_v a_lm a_max a_rsum a_vs a_p2 a_h1 a_stats1 a_mv1 a_ve1 a_xn1 "
                         "a_logit").split():
                dve.sem_inc(s[name], SEED)
            dve.wait_ge(s["a_load"], 16 * n_load)
            dve.wait_ge(s["a_const"], 1)

            def normalise(n, p, x_of, st, mv, ve, rstd, to, tag, to_free):
                turn(dve, s["a_turn"])
                for j in range(QUAD):
                    last = nc.vector.bn_stats(st[:, p, j, :], x_of(j))
                last.then_inc(s["a_stats" + tag], 1)
                dve.wait_ge(s["a_stats" + tag], made(n))
                turn(dve, s["a_turn"])
                for j in range(QUAD):
                    last = nc.vector.bn_aggr(mv[:, p, j, :], st[:, p, j, :])
                last.then_inc(s["a_mv" + tag], 1)
                dve.wait_ge(s["a_mv" + tag], made(n))
                nc.vector.tensor_scalar_add(ve[:, p, :], mv[:, p, :, 1], EPS).then_inc(s["a_ve" + tag], 1)

            def scale(n, p, x_of, mv, rstd, to, tag):
                dve.wait_ge(s["a_rstd" + tag], made(n))
                for j in range(QUAD):
                    last = nc.vector.tensor_scalar(to[:, p, j, :], x_of(j), mv[:, p, j, 0:1], rstd[:, p, j:j + 1],
                                                   ALU.subtract, ALU.mult)
                last.then_inc(s["a_xn" + tag], 1)

            with dve.Fori(0, PAIRS_OF_QUADS) as i:
                ns = [2 * i, 2 * i + 1]
                for p, n in enumerate(ns):
                    dve.wait_ge(gather[p], 16 * QUAD * (i + 1))
                    normalise(n, p, lambda j: h0[:, p, j, :], st, mv, ve, rstd, xn, "", None)
                for p, n in enumerate(ns):
                    dve.wait_ge(s["a_pT"], freed(n, 2))
                    scale(n, p, lambda j: h0[:, p, j, :], mv, rstd, xn, "")
                for p, n in enumerate(ns):
                    dve.wait_ge(s["a_pV"], made(n))
                    nc.vector.tensor_tensor(v[:, p], pV[:].rearrange("p (j d) -> p j d", j=QUAD),
                                            bc(bv[:], 1, [P, QUAD, D]), ALU.add).then_inc(s["a_v"], 1)
                for p, n in enumerate(ns):
                    dve.wait_ge(s["a_pL"], made(n))
                    nc.vector.tensor_tensor(lm[:, p], pL[:].rearrange("p (j t) -> p j t", j=QUAD),
                                            bc(causal[:], 1, [P, QUAD, P]), ALU.add).then_inc(s["a_lm"], 1)
                    dve.wait_ge(s["a_lm"], made(n))
                    nc.vector.tensor_reduce(nmx[:, p, :], lm[:, p], AX.X, ALU.max, negate=True).then_inc(s["a_max"], 1)
                for p, n in enumerate(ns):
                    dve.wait_ge(s["a_prob"], made(n))
                    nc.vector.tensor_scalar_mul(psum[:, p, :], psum[:, p, :], float(np.sqrt(P))).then_inc(s["a_p2"], 1)
                    dve.wait_ge(s["a_p2"], made(n))
                    nc.vector.reciprocal(rsum[:, p, :], psum[:, p, :]).then_inc(s["a_rsum"], 1)
                    dve.wait_ge(s["a_rsum"], made(n))
                    nc.vector.tensor_tensor(vs[:, p], v[:, p], bc(rsum[:, p, :], 2, [P, QUAD, D]),
                                            ALU.mult).then_inc(s["a_vs"], 1)
                for p, n in enumerate(ns):
                    dve.wait_ge(s["a_pR"], made(n))
                    dve.wait_ge(s["a_hx"], made(n))
                    nc.vector.tensor_tensor(H[:, bass.ds(n * QUAD, QUAD), :],
                                            pR[:].rearrange("p (j d) -> p j d", j=QUAD), hx[:, p],
                                            ALU.add).then_inc(s["a_h1"], 1)
                    dve.wait_ge(s["a_h1"], made(n))
                    normalise(n, p, lambda j: H[:, bass.ds(n * QUAD + j, 1), :].rearrange("p o d -> p (o d)"),
                              st1, mv1, ve1, rstd1, xn1, "1", None)
                for p, n in enumerate(ns):
                    dve.wait_ge(s["a_stored"], freed(n, 2))
                    dve.wait_ge(s["a_pT1"], freed(n, 2))
                    scale(n, p, lambda j: H[:, bass.ds(n * QUAD + j, 1), :].rearrange("p o d -> p (o d)"),
                          mv1, rstd1, xn1, "1")
                for p, n in enumerate(ns):
                    dve.wait_ge(s["a_pG"], made(n))
                    nc.vector.tensor_tensor(
                        logit[:, bass.ds(n * QUAD, QUAD), :, :].rearrange("p i g e -> p i (g e)"),
                        pG[:, 0:QUAD * 20].rearrange("p (i c) -> p i c", i=QUAD),
                        bc(br[:].rearrange("p g e -> p (g e)"), 1, [P, QUAD, 20]), ALU.add).then_inc(s["a_logit"], 1)

        @blk.tensor
        def _(pe):
            for name in "a_pT a_pQ a_pK a_pV a_pL a_pR a_pT1 a_pG".split():
                pe.sem_inc(s[name], SEED)
            pe.wait_ge(s["a_load"], 16 * n_load)
            pe.wait_ge(s["a_const"], 1)
            with pe.Fori(0, PAIRS_OF_QUADS) as i:
                ns = [2 * i, 2 * i + 1]
                for p, n in enumerate(ns):
                    pe.wait_ge(s["a_xn"], made(n))
                    pe.wait_ge(s["a_xT"], freed(n, 1))
                    for j in range(QUAD):
                        last = nc.tensor.transpose(pT[:, bass.ts(j, P)], xn[:, p, j, :], ident[:])
                    last.then_inc(s["a_pT"], 1)
                for p, n in enumerate(ns):
                    pe.wait_ge(s["a_xT"], made(n))
                    pe.wait_ge(s["a_qT"], freed(n, 1))
                    nc.tensor.matmul(pQ[:], wq[:], xT[:, p, :], start=True, stop=True).then_inc(s["a_pQ"], 1)
                    pe.wait_ge(s["a_kT"], freed(n, 1))
                    nc.tensor.matmul(pK[:], wk[:], xT[:, p, :], start=True, stop=True).then_inc(s["a_pK"], 1)
                    pe.wait_ge(s["a_v"], freed(n, 1))
                    for j in range(QUAD):
                        last = nc.tensor.matmul(pV[:, bass.ts(j, D)], xT[:, p, bass.ts(j, P)], wv[:], start=True, stop=True)
                    last.then_inc(s["a_pV"], 1)
                for p, n in enumerate(ns):
                    pe.wait_ge(s["a_kT"], made(n))
                    pe.wait_ge(s["a_qT"], made(n))
                    pe.wait_ge(s["a_lm"], freed(n, 1))
                    for j in range(QUAD):
                        last = nc.tensor.matmul(pL[:, bass.ts(j, P)], kT[:, p, bass.ts(j, P)], qT[:, p, bass.ts(j, P)],
                                                start=True, stop=True)
                    last.then_inc(s["a_pL"], 1)
                for p, n in enumerate(ns):
                    pe.wait_ge(s["a_prob"], made(n))
                    pe.wait_ge(s["a_vs"], made(n))
                    pe.wait_ge(s["a_h1"], freed(n, 1))
                    for j in range(QUAD):
                        last = nc.tensor.matmul(pR[:, bass.ts(j, D)], prob[:, p, j, :], vs[:, p, j, :],
                                                start=True, stop=True)
                    last.then_inc(s["a_pR"], 1)
                for p, n in enumerate(ns):
                    pe.wait_ge(s["a_xn1"], made(n))
                    pe.wait_ge(s["a_x1T"], freed(n, 1))
                    for j in range(QUAD):
                        last = nc.tensor.transpose(pT1[:, bass.ts(j, P)], xn1[:, p, j, :], ident[:])
                    last.then_inc(s["a_pT1"], 1)
                for p, n in enumerate(ns):
                    pe.wait_ge(s["a_x1T"], made(n))
                    pe.wait_ge(s["a_logit"], freed(n, 1))
                    for j in range(QUAD):
                        last = nc.tensor.matmul(pG[:, j * 20:j * 20 + 20], x1T[:, p, bass.ts(j, P)],
                                                wr[:].rearrange("p g e -> p (g e)"), start=True, stop=True)
                    last.then_inc(s["a_pG"], 1)

        @blk.scalar
        def _(act):
            for name in "a_xT a_qT a_kT a_prob a_x1T".split():
                act.sem_inc(s[name], SEED)
            act.wait_ge(s["a_load"], 16 * n_load)
            act.wait_ge(s["a_zero"], 1)
            nc.scalar.activation(prob[:, 0, 0, 0:1], zeros[:, 0:1], ACT.Exp)
            with act.Fori(0, PAIRS_OF_QUADS) as i:
                ns = [2 * i, 2 * i + 1]
                for p, n in enumerate(ns):
                    act.wait_ge(s["a_pT"], made(n))
                    act.wait_ge(s["a_pV"], freed(n, 2))
                    nc.scalar.copy(xT[:, p, :], pT[:]).then_inc(s["a_xT"], 1)
                for p, n in enumerate(ns):
                    act.wait_ge(s["a_pL"], freed(n, 2))
                    act.wait_ge(s["a_pQ"], made(n))
                    nc.scalar.activation(qT[:, p, :], pQ[:], ACT.Identity, bias=bq[:, 0:1]).then_inc(s["a_qT"], 1)
                    act.wait_ge(s["a_pK"], made(n))
                    nc.scalar.activation(kT[:, p, :], pK[:], ACT.Identity, bias=bk[:, 0:1]).then_inc(s["a_kT"], 1)
                for p, n in enumerate(ns):
                    act.wait_ge(s["a_max"], made(n))
                    act.wait_ge(s["a_pR"], freed(n, 2))
                    act.wait_ge(s["a_rsum"], freed(n, 2))
                    for j in range(QUAD):
                        last = nc.scalar.activation(prob[:, p, j, :], lm[:, p, j, :], ACT.Exp, bias=nmx[:, p, j:j + 1],
                                                    accum_out=psum[:, p, j:j + 1])
                    last.then_inc(s["a_prob"], 1)
                for p, n in enumerate(ns):
                    act.wait_ge(s["a_pT1"], made(n))
                    act.wait_ge(s["a_pG"], freed(n, 2))
                    nc.scalar.copy(x1T[:, p, :], pT1[:]).then_inc(s["a_x1T"], 1)


def layer0_routing(nc, sems, ps, before, ones, logit, slot0, weight0, block_expert):
    ctx = ExitStack()
    GROUPS = TILES * (1 + G0)
    with ctx:
        def sb(name, shape, dt=F32):
            return ctx.enter_context(nc.sbuf_tensor(name, shape, dt))
        prob = sb("r_prob", [P, TILES, 1 + G0, EPG0])
        rank = sb("r_rank", [P, TILES, 1 + G0, EPG0])
        first = sb("r_first", [P, TILES, 1 + G0, EPG0])
        second = sb("r_second", [P, TILES, 1 + G0, EPG0])
        work = sb("r_work", [P, TILES, 1 + G0, EPG0])
        pair = sb("r_pair", [P, 6, GROUPS])
        small = [sb(f"r_small{k}", [P, TILES, 1 + G0]) for k in range(5)]
        picks = sb("r_picks", [P, E0, TILES], BF16)
        total = sb("r_total", [P, E0, TILES])
        row = sb("r_row", [P, E0, TILES])
        fresh = sb("r_fresh", [P, E0, TILES])
        count_i = sb("r_count_i", [P, E0], I32)
        blocks = sb("r_blocks", [P, E0])
        block_end = sb("r_block_end", [P, E0])
        block_at = sb("r_block_at", [P, E0])
        index = sb("r_index", [1, BLOCKS0])
        reached = sb("r_reached", [1, BLOCKS0, E0], BF16)
        expert_f = sb("r_expert_f", [1, BLOCKS0])
        pick_w = sb("r_pick_w", [P, TILES])
        s = sems("r_dve r_max r_exp r_picks r_counted r_const")
        blk = ctx.enter_context(nc.Block())

        @blk.gpsimd
        def _(pool):
            nc.gpsimd.memset(fresh[:], 1.0).then_inc(s["r_const"], 1)
            pool.wait_ge(s["r_const"], 1)
            nc.gpsimd.memset(fresh[:, :, 0:1], 0.0)
            nc.gpsimd.iota(index[:], pattern=[[1, BLOCKS0]], base=0, channel_multiplier=0,
                           allow_small_or_imprecise_dtypes=True).then_inc(s["r_const"], 1)

        @blk.scalar
        def _(act):
            act.wait_ge(s["r_max"], 1)
            nc.scalar.activation(prob[:], work[:], ACT.Exp).then_inc(s["r_exp"], 1)

        @blk.tensor
        def _(pe):
            pe.wait_ge(s["r_picks"], 1)
            flat = picks[:].rearrange("p e i -> p (e i)")
            for c in range(2):
                nc.tensor.matmul(ps[c][:], before[:], flat[:, bass.ts(c, 512)], start=True, stop=True)
            for c in range(2):
                last = nc.tensor.matmul(ps[2 + c][:], ones[:], flat[:, bass.ts(c, 512)], start=True, stop=True)
            last.then_inc(s["r_counted"], 1)

        @blk.vector
        def _(dve):
            V = nc.vector
            step = Chain(dve, s["r_dve"])
            flat5 = "p i g e -> p (i g) e"
            group = [P, GROUPS, EPG0]

            def small_(k):
                return small[k][:].rearrange("p i g -> p (i g)")
            step(V.tensor_reduce(small_(0), logit[:].rearrange(flat5), AX.X, ALU.max))
            V.tensor_tensor(work[:].rearrange(flat5), logit[:].rearrange(flat5), bc(small_(0), 2, group),
                            ALU.subtract).then_inc(s["r_max"], 1)
            dve.wait_ge(s["r_exp"], 1)
            step(V.tensor_reduce(small_(0), prob[:].rearrange(flat5), AX.X, ALU.add))
            step(V.reciprocal(small_(1), small_(0)))
            step(V.tensor_tensor(prob[:].rearrange(flat5), prob[:].rearrange(flat5), bc(small_(1), 2, group), ALU.mult))
            pr, rk = prob[:].rearrange(flat5), rank[:].rearrange(flat5)
            pairs = [(a, b) for a in range(EPG0) for b in range(a + 1, EPG0)]
            for k, (a, b) in enumerate(pairs):
                last = V.tensor_tensor(pair[:, k, :], pr[:, :, a], pr[:, :, b], ALU.is_ge)
            step(last)
            for e in range(EPG0):
                losing = [k for k, (a, b) in enumerate(pairs) if b == e]
                winning = [k for k, (a, b) in enumerate(pairs) if a == e]
                if winning:
                    step(V.tensor_scalar(rk[:, :, e], pair[:, winning[0], :], -1.0, float(len(winning)), ALU.mult, ALU.add))
                    for k in winning[1:]:
                        step(V.tensor_tensor(rk[:, :, e], rk[:, :, e], pair[:, k, :], ALU.subtract))
                else:
                    step(V.tensor_copy(rk[:, :, e], pair[:, losing.pop(0), :]))
                for k in losing:
                    step(V.tensor_tensor(rk[:, :, e], rk[:, :, e], pair[:, k, :], ALU.add))
            V.tensor_scalar(first[:], rank[:], 0.0, None, ALU.is_equal)
            step(V.tensor_scalar(second[:], rank[:], 1.0, None, ALU.is_equal))
            step(V.tensor_tensor(work[:], prob[:], first[:], ALU.mult))
            step(V.tensor_reduce(small_(0), work[:].rearrange(flat5), AX.X, ALU.add))
            step(V.tensor_tensor(work[:], prob[:], second[:], ALU.mult))
            step(V.tensor_reduce(small_(1), work[:].rearrange(flat5), AX.X, ALU.add))
            step(V.tensor_tensor(small[2][:], small[0][:], small[1][:], ALU.add))
            step(V.tensor_scalar(small[2][:], small[2][:], 0.9, None, ALU.is_le))
            step(V.tensor_tensor(small[1][:], small[1][:], small[2][:], ALU.mult))
            step(V.tensor_tensor(small[2][:], small[0][:], small[1][:], ALU.add))
            step(V.tensor_scalar_add(small[2][:], small[2][:], 1e-9))
            step(V.reciprocal(small[3][:], small[2][:]))
            step(V.tensor_tensor(small[0][:], small[0][:], small[3][:], ALU.mult))
            step(V.tensor_tensor(small[1][:], small[1][:], small[3][:], ALU.mult))
            step(V.tensor_tensor(work[:], first[:], second[:], ALU.add))
            step(V.tensor_tensor(picks[:].rearrange("p (g e) i -> p i g e", g=G0), work[:, :, 1:, :],
                                 bc(work[:, :, 0, :], 3, [P, TILES, G0, EPG0]), ALU.mult))
            dve.sem_inc(s["r_picks"], 1)
            dve.wait_ge(s["r_counted"], 1)
            dve.wait_ge(s["r_const"], 2)
            for c in range(2):
                last = V.tensor_copy(total[:].rearrange("p e i -> p (e i)")[:, bass.ts(c, 512)], ps[2 + c][:])
            step(last)
            step(V.tensor_tensor_scan(row[:].rearrange("p e i -> p (e i)"), fresh[:].rearrange("p e i -> p (e i)"),
                                      total[:].rearrange("p e i -> p (e i)"), 0.0, ALU.mult, ALU.add))
            step(V.tensor_scalar_add(count_i[:], row[:, :, TILES - 1], float(P - 1)))
            step(V.tensor_single_scalar(count_i[:], count_i[:], 7, ALU.arith_shift_right))
            step(V.tensor_copy(blocks[:], count_i[:]))
            step(V.memset(block_at[:], 1.0))
            step(V.tensor_tensor_scan(block_end[:], block_at[:], blocks[:], 0.0, ALU.mult, ALU.add))
            step(V.tensor_tensor(block_at[:], block_end[:], blocks[:], ALU.subtract))
            step(V.tensor_tensor(reached[:], bc(index[:], 2, [1, BLOCKS0, E0]),
                                 bc(block_end[0:1, :], 1, [1, BLOCKS0, E0]), ALU.is_ge))
            step(V.tensor_reduce(expert_f[:], reached[:], AX.X, ALU.add))
            step(V.tensor_scalar(block_expert[:], expert_f[:], float(E0 - 1), None, ALU.min))
            step(V.tensor_tensor(row[:], row[:], total[:], ALU.subtract))
            for c in range(2):
                part = row[:].rearrange("p e i -> p (e i)")[:, bass.ts(c, 512)]
                step(V.tensor_tensor(part, part, ps[c][:], ALU.add))
            step(V.tensor_scalar_mul(block_at[:], block_at[:], float(P)))
            step(V.tensor_tensor(row[:], row[:], bc(block_at[:], 2, [P, E0, TILES]), ALU.add))
            row_v = row[:].rearrange("p (g e) i -> p i g e", g=G0)
            pick16 = work[:].rearrange("p i g e -> p (i g e)")[:, 0:TILES * E0].rearrange("p (i g e) -> p i g e", i=TILES, g=G0)
            for a, of_group in enumerate((first, second)):
                for b, of_expert in enumerate((first, second)):
                    k = 2 * a + b
                    step(V.tensor_tensor(pick16, of_expert[:, :, 1:, :],
                                         bc(of_group[:, :, 0, :], 3, [P, TILES, G0, EPG0]), ALU.mult))
                    step(V.tensor_tensor(pick16, pick16, row_v, ALU.mult))
                    step(V.tensor_reduce(pick_w[:], pick16, AX.XY, ALU.add))
                    step(V.tensor_copy(slot0[:, :, k], pick_w[:]))
                    four = small[4][:, :, 0:G0]
                    step(V.tensor_tensor(four, of_group[:, :, 0, :], small[b][:, :, 1:], ALU.mult))
                    step(V.tensor_reduce(pick_w[:], four, AX.X, ALU.add))
                    step(V.tensor_tensor(pick_w[:], pick_w[:], small[a][:, :, 0], ALU.mult))
                    step(V.tensor_scalar_mul(weight0[:, :, k], pick_w[:], float(G0) ** -0.5))


def scatter_rows(nc, sems, tag, slot, picks, rows, sorted_rows, bound):
    ctx = ExitStack()
    RING = 4
    with ctx:
        data = ctx.enter_context(nc.sbuf_tensor(tag + "data", [P, RING, D], F32))
        idx = ctx.enter_context(nc.sbuf_tensor(tag + "idx", [P, RING, picks], I32))
        s = sems(" ".join(tag + x for x in ("free", "indexed", "turns")),
                 dma=" ".join(f"{tag}{x}{r}" for x in ("landed", "sent") for r in range(RING)))
        free, indexed, turns = (s[tag + x] for x in ("free", "indexed", "turns"))
        landed = [s[f"{tag}landed{r}"] for r in range(RING)]
        sent = [s[f"{tag}sent{r}"] for r in range(RING)]
        blk = ctx.enter_context(nc.Block())
        src = rows.rearrange("(i t) d -> i t d", t=P)

        @blk.sync
        def _(sp):
            with sp.Fori(0, TILES // RING) as i:
                for r in range(RING):
                    sp.wait_ge(free, i * RING + r + 1)
                    sp.dma_start(data[:, r, :], src[i * RING + r]).then_inc(landed[r], 16)

        @blk.gpsimd
        def _(pool):
            pool.sem_inc(free, RING)
            with pool.Fori(0, TILES // RING) as i:
                nc.gpsimd.tensor_copy(idx[:], slot[:, bass.ds(i * RING, RING), :]).then_inc(indexed, 1)
                pool.wait_ge(indexed, i + 1)
                turn(pool, turns)
                for r in range(RING):
                    pool.wait_ge(landed[r], 16 * i + 16)
                    turn(pool, turns)
                    for k in range(picks):
                        nc.gpsimd.indirect_dma_start(
                            out=sorted_rows, out_offset=bass.IndirectOffsetOnAxis(ap=idx[:, r, k:k + 1], axis=0),
                            in_=data[:, r, :], in_offset=None, bounds_check=bound,
                            oob_is_err=False).then_inc(sent[r], 16)
                for r in range(RING):
                    pool.wait_ge(sent[r], 16 * picks * (i + 1))
                    pool.sem_inc(free, 1)


def layer0_experts(nc, sems, ps, ident, block_expert, w1, w3, w2, XS0, YS0):
    ctx = ExitStack()
    CH = HID // P
    with ctx:
        def sb(name, shape, dt=F32):
            return ctx.enter_context(nc.sbuf_tensor(name, shape, dt))
        x = sb("e_x", [P, 2, D])
        xT = sb("e_xT", [P, 2, P])
        gate = sb("e_gate", [P, 2, HID])
        g = sb("e_g", [P, 2, HID])
        gT = sb("e_gT", [P, 2, CH, P])
        y = sb("e_y", [P, 2, D])
        s = sems("e_pT e_xT e_p1 e_p3 e_gate e_g e_pg e_gT e_py e_y e_stored",
                 dma="e_x0 e_x1 e_out0 e_out1")
        landed, out = [s["e_x0"], s["e_x1"]], [s["e_out0"], s["e_out1"]]
        pT, py = ps[0], ps[1]
        p1, p3, pg = [ps[2], ps[3]], [ps[4], ps[5]], [ps[6], ps[7]]
        xv = XS0.rearrange("(j t) d -> j t d", t=P)
        yv = YS0.rearrange("(j t) d -> j t d", t=P)
        blk = ctx.enter_context(nc.Block())

        @blk.sync
        def _(sp):
            with sp.Fori(0, BLOCKS0 // 2) as i:
                for p in range(2):
                    n = 2 * i + p
                    sp.wait_ge(s["e_pT"], freed(n, 2))
                    sp.dma_start(x[:, p, :], xv[n]).then_inc(landed[p], 16)

        @blk.gpsimd
        def _(pool):
            pool.sem_inc(s["e_stored"], SEED)
            with pool.Fori(0, BLOCKS0 // 2) as i:
                for p in range(2):
                    pool.wait_ge(s["e_y"], made(2 * i + p))
                    pool.dma_start(yv[2 * i + p], y[:, p, :]).then_inc(out[p], 16)
                for p in range(2):
                    pool.wait_ge(out[p], 16 * i + 16)
                    pool.sem_inc(s["e_stored"], 1)

        @blk.tensor
        def _(pe):
            for name in "e_pT e_p1 e_p3 e_pg e_py".split():
                pe.sem_inc(s[name], SEED)
            with pe.Fori(0, BLOCKS0 // 2) as i:
                ns = [2 * i, 2 * i + 1]
                expert = []
                for p, n in enumerate(ns):
                    expert.append(pe.value_load(block_expert[0:1, bass.ds(n, 1)], min_val=0, max_val=E0 - 1))
                for p, n in enumerate(ns):
                    pe.wait_ge(landed[p], 16 * i + 16)
                    pe.wait_ge(s["e_xT"], freed(n, 1))
                    nc.tensor.transpose(pT[:, 0:P], x[:, p, :], ident[:]).then_inc(s["e_pT"], 1)
                for p, n in enumerate(ns):
                    pe.wait_ge(s["e_xT"], made(n))
                    pe.wait_ge(s["e_gate"], freed(n, 2))
                    nc.tensor.matmul(p1[p][:], xT[:, p, :], w1[:, bass.ds(expert[p], 1), :].rearrange("p o h -> p (o h)"),
                                     start=True, stop=True).then_inc(s["e_p1"], 1)
                    pe.wait_ge(s["e_g"], freed(n, 2))
                    nc.tensor.matmul(p3[p][:], xT[:, p, :], w3[:, bass.ds(expert[p], 1), :].rearrange("p o h -> p (o h)"),
                                     start=True, stop=True).then_inc(s["e_p3"], 1)
                for p, n in enumerate(ns):
                    pe.wait_ge(s["e_g"], made(n))
                    pe.wait_ge(s["e_gT"], freed(n, 2))
                    for c in range(CH):
                        last = nc.tensor.transpose(pg[p][:, bass.ts(c, P)], g[:, p, bass.ts(c, P)], ident[:])
                    last.then_inc(s["e_pg"], 1)
                for p, n in enumerate(ns):
                    pe.wait_ge(s["e_gT"], made(n))
                    pe.wait_ge(s["e_y"], freed(n, 1))
                    for c in range(CH):
                        last = nc.tensor.matmul(
                            py[:, 0:D], gT[:, p, c, :],
                            w2[:, bass.ds(expert[p], 1), c, :].rearrange("p o d -> p (o d)"),
                            start=(c == 0), stop=(c == CH - 1))
                    last.then_inc(s["e_py"], 1)

        @blk.scalar
        def _(act):
            for name in "e_xT e_gate e_gT".split():
                act.sem_inc(s[name], SEED)
            nc.scalar.activation(gT[:, 0, 0, 0:1], ident[:, 0:1], ACT.Silu)
            with act.Fori(0, BLOCKS0 // 2) as i:
                ns = [2 * i, 2 * i + 1]
                for p, n in enumerate(ns):
                    act.wait_ge(s["e_pT"], made(n))
                    act.wait_ge(s["e_p3"], freed(n, 2))
                    nc.scalar.copy(xT[:, p, :], pT[:, 0:P]).then_inc(s["e_xT"], 1)
                for p, n in enumerate(ns):
                    act.wait_ge(s["e_p1"], made(n))
                    act.wait_ge(s["e_g"], freed(n, 2))
                    nc.scalar.activation(gate[:, p, :], p1[p][:], ACT.Silu).then_inc(s["e_gate"], 1)
                for p, n in enumerate(ns):
                    act.wait_ge(s["e_pg"], made(n))
                    act.wait_ge(s["e_py"], freed(n, 2))
                    nc.scalar.copy(gT[:, p].rearrange("p c t -> p (c t)"), pg[p][:]).then_inc(s["e_gT"], 1)

        @blk.vector
        def _(dve):
            for name in "e_g e_y".split():
                dve.sem_inc(s[name], SEED)
            with dve.Fori(0, BLOCKS0 // 2) as i:
                ns = [2 * i, 2 * i + 1]
                for p, n in enumerate(ns):
                    dve.wait_ge(s["e_gate"], made(n))
                    dve.wait_ge(s["e_p3"], made(n))
                    dve.wait_ge(s["e_pg"], freed(n, 2))
                    nc.vector.tensor_tensor(g[:, p, :], gate[:, p, :], p3[p][:], ALU.mult).then_inc(s["e_g"], 1)
                for p, n in enumerate(ns):
                    dve.wait_ge(s["e_py"], made(n))
                    dve.wait_ge(s["e_stored"], freed(n, 2))
                    nc.vector.tensor_copy(y[:, p, :], py[:, 0:D]).then_inc(s["e_y"], 1)


def layer0_combine(nc, A, sems, ps, H, ident, slot0, weight0, wnT, YS0, BD):
    ctx = ExitStack()
    with ctx:
        def sb(name, shape, dt=F32):
            return ctx.enter_context(nc.sbuf_tensor(name, shape, dt))
        power = sb("d_power", [P, QUAD])
        gamma, beta, rbias = sb("d_gamma", [P, 1]), sb("d_beta", [P, 1]), sb("d_rbias", [P, 1])
        wq, wr = sb("d_wq", [P, D]), sb("d_wr", [P, D])
        angles = sb("d_angles", [P, TILES])
        headmask = sb("d_headmask", [P, HEADS])
        rk = sb("d_rk", [P, TILES])
        window = sb("d_window", [P, 2, HEADS, 2 * TILES])
        idx = sb("d_idx", [P, 2, QUAD, PICKS0], I32)
        got = sb("d_got", [P, 2, QUAD, PICKS0, D])
        wt = sb("d_wt", [P, 2, QUAD, PICKS0])
        acc = sb("d_acc", [P, 2, QUAD, D])
        st, mv, ve, rstd = (sb("d_st", [P, 2, QUAD, 6]), sb("d_mv", [P, 2, QUAD, 2]), sb("d_ve", [P, 2, QUAD]),
                            sb("d_rstd", [P, 2, QUAD]))
        st2, mv2, ve2, rstd2 = (sb("d_st2", [P, 2, QUAD, 6]), sb("d_mv2", [P, 2, QUAD, 2]),
                                sb("d_ve2", [P, 2, QUAD]), sb("d_rstd2", [P, 2, QUAD]))
        w = sb("d_w", [P, 2, QUAD, D])
        wn = sb("d_wn", [P, 2, QUAD, D])
        wT = sb("d_wT", [P, 2, QUAD, P])
        q = sb("d_q", [P, 2, QUAD, P])
        pos = sb("d_pos", [P, 2, HEADS * TILES])
        s = sems("d_const d_const2 d_rk d_rks d_window d_idx d_acc d_acck d_st d_mv d_ve d_rstd d_w d_st2 "
                 "d_mv2 d_ve2 d_rstd2 d_wn d_pT d_wT d_wnT d_h d_pQ d_q d_pB d_pos d_kept d_turn d_poolturn "
                 "d_peturn",
                 dma="d_load d_got0 d_got1 d_out0 d_out1")
        got_in, kept = [s["d_got0"], s["d_got1"]], [s["d_out0"], s["d_out1"]]
        pT, pQ, pB, pR = ps[0], ps[1], [ps[2], ps[3]], ps[4]
        n_load = 6
        blk = ctx.enter_context(nc.Block())

        @blk.sync
        def _(sp):
            for dst, src in ((gamma[:], A["L1_attn_ln_gamma"].unsqueeze(1)), (beta[:], A["L1_attn_ln_beta"].unsqueeze(1)),
                             (rbias[:], A["L1_attn_r_r_bias"].rearrange("n (d o) -> (n d) o", o=1)),
                             (wq[:], A["L1_attn_Wqkv"][:, 0:D]), (wr[:], A["L1_attn_Wr"]), (angles[:], A["positions"])):
                sp.dma_start(dst, src).then_inc(s["d_load"], 16)
            sp.sem_inc(s["d_kept"], SEED)
            with sp.Fori(0, TILES // 2) as i:
                for p in range(2):
                    sp.wait_ge(s["d_pos"], made(2 * i + p))
                    sp.dma_start(BD[:, bass.ds(2 * i + p, 1), :].rearrange("b o c -> b (o c)"), pos[:, p, :]).then_inc(kept[p], 16)
                for p in range(2):
                    sp.wait_ge(kept[p], 16 * i + 16)
                    sp.sem_inc(s["d_kept"], 1)
            sp.wait_ge(s["d_pos"], made(TILES))
            sp.dma_start(BD[:, TILES, :], pos[:, 0, :]).then_inc(kept[0], 16)
            sp.wait_ge(kept[0], 16 * (TILES // 2 + 1))

        @blk.gpsimd
        def _(pool):
            for name in "d_idx d_rstd d_rstd2 d_h d_wnT".split():
                pool.sem_inc(s[name], SEED)
            nc.gpsimd.memset(power[:], -0.5)
            nc.gpsimd.memset(window[:], 0.0)
            nc.gpsimd.memset(q[:], 0.0)
            nc.gpsimd.memset(headmask[:], 1.0).then_inc(s["d_const"], 1)
            pool.wait_ge(s["d_const"], 1)
            nc.gpsimd.affine_select(out=headmask[:], in_=headmask[:], compare_op=ALU.is_ge, fill=0.0, base=0,
                                    pattern=[[-DH, HEADS]], channel_multiplier=1).then_inc(s["d_const"], 1)
            pool.wait_ge(s["d_const"], 2)
            nc.gpsimd.affine_select(out=headmask[:], in_=headmask[:], compare_op=ALU.is_ge, fill=0.0, base=DH - 1,
                                    pattern=[[DH, HEADS]], channel_multiplier=-1).then_inc(s["d_const"], 1)
            with pool.Fori(0, PAIRS_OF_QUADS) as i:
                ns = [2 * i, 2 * i + 1]
                for p, n in enumerate(ns):
                    pool.wait_ge(s["d_acc"], freed(n, 2))
                    turn(pool, s["d_poolturn"])
                    nc.gpsimd.tensor_copy(idx[:, p], slot0[:, bass.ds(n * QUAD, QUAD), :]).then_inc(s["d_idx"], 1)
                    pool.wait_ge(s["d_idx"], made(n))
                    turn(pool, s["d_poolturn"])
                    for j in range(QUAD):
                        for k in range(PICKS0):
                            nc.gpsimd.indirect_dma_start(
                                out=got[:, p, j, k, :], out_offset=None, in_=YS0,
                                in_offset=bass.IndirectOffsetOnAxis(ap=idx[:, p, j, k:k + 1], axis=0)).then_inc(got_in[p], 16)
                for p, n in enumerate(ns):
                    pool.wait_ge(s["d_ve"], made(n))
                    nc.gpsimd.tensor_tensor(rstd[:, p, :], ve[:, p, :], power[:], ALU.pow).then_inc(s["d_rstd"], 1)
                for p, n in enumerate(ns):
                    pool.wait_ge(s["d_w"], made(n))
                    turn(pool, s["d_poolturn"])
                    nc.gpsimd.tensor_tensor(H[:, bass.ds(n * QUAD, QUAD), :], acc[:, p], w[:, p],
                                            ALU.add).then_inc(s["d_h"], 1)
                for p, n in enumerate(ns):
                    pool.wait_ge(s["d_ve2"], made(n))
                    nc.gpsimd.tensor_tensor(rstd2[:, p, :], ve2[:, p, :], power[:], ALU.pow).then_inc(s["d_rstd2"], 1)
                for p, n in enumerate(ns):
                    pool.wait_ge(s["d_wT"], made(n))
                    turn(pool, s["d_poolturn"])
                    nc.gpsimd.tensor_copy(wnT[:, :, bass.ds(n * QUAD, QUAD)],
                                          wT[:, p].rearrange("d i b -> d b i")).then_inc(s["d_wnT"], 1)

        @blk.vector
        def _(dve):
            for name in "d_acc d_acck d_st d_mv d_ve d_w d_st2 d_mv2 d_ve2 d_wn d_pos".split():
                dve.sem_inc(s[name], SEED)
            dve.wait_ge(s["d_const"], 3)
            dve.wait_ge(s["d_rk"], 1)
            nc.vector.tensor_copy(rk[:], pR[:, 0:TILES]).then_inc(s["d_rks"], 1)
            dve.wait_ge(s["d_rks"], 1)
            for k, at in ((0, 0), (1, TILES + 1)):
                width = min(TILES, 2 * TILES - at)
                nc.vector.tensor_tensor(window[:, k, :, at:at + width], bc(rk[:, 0:width], 1, [P, HEADS, width]),
                                        bc(headmask[:], 2, [P, HEADS, width]), ALU.mult).then_inc(s["d_window"], 1)

            def stats(n, p, x, st, mv, ve, tag):
                turn(dve, s["d_turn"])
                for j in range(QUAD):
                    last = nc.vector.bn_stats(st[:, p, j, :], x[:, p, j, :])
                last.then_inc(s["d_st" + tag], 1)
                dve.wait_ge(s["d_st" + tag], made(n))
                turn(dve, s["d_turn"])
                for j in range(QUAD):
                    last = nc.vector.bn_aggr(mv[:, p, j, :], st[:, p, j, :])
                last.then_inc(s["d_mv" + tag], 1)
                dve.wait_ge(s["d_mv" + tag], made(n))
                nc.vector.tensor_scalar_add(ve[:, p, :], mv[:, p, :, 1], EPS).then_inc(s["d_ve" + tag], 1)

            with dve.Fori(0, PAIRS_OF_QUADS) as i:
                ns = [2 * i, 2 * i + 1]
                for p, n in enumerate(ns):
                    dve.wait_ge(s["d_h"], freed(n, 2))
                    nc.vector.tensor_copy(wt[:, p], weight0[:, bass.ds(n * QUAD, QUAD), :])
                    nc.vector.tensor_copy(acc[:, p], H[:, bass.ds(n * QUAD, QUAD), :]).then_inc(s["d_acck"], 1)
                    dve.wait_ge(got_in[p], 16 * QUAD * PICKS0 * (i + 1))
                    for k in range(PICKS0):
                        dve.wait_ge(s["d_acck"], SEED + PICKS0 * n + k + 1)
                        for j in range(QUAD):
                            last = nc.vector.scalar_tensor_tensor(acc[:, p, j, :], got[:, p, j, k, :], wt[:, p, j, k:k + 1],
                                                                  acc[:, p, j, :], ALU.mult, ALU.add)
                        last.then_inc(s["d_acck"] if k < PICKS0 - 1 else s["d_acc"], 1)
                    dve.wait_ge(s["d_acc"], made(n))
                    stats(n, p, acc, st, mv, ve, "")
                for p, n in enumerate(ns):
                    dve.wait_ge(s["d_rstd"], made(n))
                    for j in range(QUAD):
                        last = nc.vector.tensor_scalar(w[:, p, j, :], acc[:, p, j, :], mv[:, p, j, 0:1], rstd[:, p, j:j + 1],
                                                       ALU.subtract, ALU.mult)
                    last.then_inc(s["d_w"], 1)
                    dve.wait_ge(s["d_w"], made(n))
                    stats(n, p, w, st2, mv2, ve2, "2")
                for p, n in enumerate(ns):
                    dve.wait_ge(s["d_rstd2"], made(n))
                    dve.wait_ge(s["d_pT"], freed(n, 2))
                    for j in range(QUAD):
                        last = nc.vector.tensor_scalar(wn[:, p, j, :], w[:, p, j, :], mv2[:, p, j, 0:1], rstd2[:, p, j:j + 1],
                                                       ALU.subtract, ALU.mult)
                    last.then_inc(s["d_wn"], 1)
                for p, n in enumerate(ns):
                    for j in range(QUAD):
                        m = n * QUAD + j
                        dve.wait_ge(s["d_pB"], made(m))
                        dve.wait_ge(s["d_kept"], freed(m, 2))
                        nc.vector.tensor_copy(pos[:, j % 2, :], pB[j % 2][:]).then_inc(s["d_pos"], 1)
            dve.wait_ge(s["d_pB"], made(TILES))
            dve.wait_ge(s["d_kept"], freed(TILES, 2))
            nc.vector.tensor_copy(pos[:, 0, :], pB[0][:]).then_inc(s["d_pos"], 1)

        @blk.tensor
        def _(pe):
            for name in "d_pT d_pQ d_pB".split():
                pe.sem_inc(s[name], SEED)
            pe.wait_ge(s["d_load"], 16 * n_load)
            nc.tensor.matmul(pR[:, 0:TILES], wr[:], angles[:], start=True, stop=True).then_inc(s["d_rk"], 1)
            pe.wait_ge(s["d_window"], 2)
            with pe.Fori(0, PAIRS_OF_QUADS) as i:
                ns = [2 * i, 2 * i + 1]
                for p, n in enumerate(ns):
                    pe.wait_ge(s["d_wn"], made(n))
                    pe.wait_ge(s["d_wT"], freed(n, 1))
                    for j in range(QUAD):
                        last = nc.tensor.transpose(pT[:, bass.ts(j, P)], wn[:, p, j, :], ident[:])
                    last.then_inc(s["d_pT"], 1)
                for p, n in enumerate(ns):
                    pe.wait_ge(s["d_wT"], made(n))
                    pe.wait_ge(s["d_q"], freed(n, 1))
                    nc.tensor.matmul(pQ[:], wq[:], wT[:, p].rearrange("d i b -> d (i b)"),
                                     start=True, stop=True).then_inc(s["d_pQ"], 1)
                for p, n in enumerate(ns):
                    pe.wait_ge(s["d_q"], made(n))
                    for j in range(QUAD):
                        m = n * QUAD + j
                        pe.wait_ge(s["d_pos"], freed(m, 2))
                        turn(pe, s["d_peturn"])
                        prev = q[:, p, j - 1, :] if j else q[:, 1 - p, QUAD - 1, :]
                        nc.tensor.matmul(pB[j % 2][:], prev, window[:, 0, :, bass.ds(TILES - m, TILES)],
                                         start=True, stop=False)
                        nc.tensor.matmul(pB[j % 2][:], q[:, p, j, :], window[:, 1, :, bass.ds(TILES - m, TILES)],
                                         start=False, stop=True).then_inc(s["d_pB"], 1)
            pe.wait_ge(s["d_pos"], freed(TILES, 2))
            nc.tensor.matmul(pB[0][:], q[:, 1, QUAD - 1, :], window[:, 0, :, 0:TILES],
                             start=True, stop=True).then_inc(s["d_pB"], 1)

        @blk.scalar
        def _(act):
            for name in "d_wT d_q".split():
                act.sem_inc(s[name], SEED)
            act.wait_ge(s["d_load"], 16 * n_load)
            act.wait_ge(s["d_const"], 3)
            with act.Fori(0, PAIRS_OF_QUADS) as i:
                ns = [2 * i, 2 * i + 1]
                for p, n in enumerate(ns):
                    act.wait_ge(s["d_pT"], made(n))
                    act.wait_ge(s["d_pQ"], freed(n, 2))
                    act.wait_ge(s["d_wnT"], freed(n, 2))
                    nc.scalar.activation(wT[:, p].rearrange("d i b -> d (i b)"), pT[:], ACT.Identity, bias=beta[:, 0:1],
                                         scale=gamma[:, 0:1]).then_inc(s["d_wT"], 1)
                for p, n in enumerate(ns):
                    act.wait_ge(s["d_pQ"], made(n))
                    if p:
                        act.wait_ge(s["d_pB"], made(2 * i * QUAD))
                    nc.scalar.activation(q[:, p].rearrange("d i b -> d (i b)"), pQ[:], ACT.Identity,
                                         bias=rbias[:, 0:1]).then_inc(s["d_q"], 1)


def layer1_attention(nc, A, sems, ps, ident, wnT, readT, BD):
    ctx = ExitStack()
    OCT = 8
    with ctx:
        def sb(name, shape, dt=F32):
            return ctx.enter_context(nc.sbuf_tensor(name, shape, dt))
        wq, wk, wv = sb("f_wq", [P, D]), sb("f_wk", [P, D]), sb("f_wv", [P, D])
        wbias = sb("f_wbias", [P, 1])
        headmask = sb("f_headmask", [P, HEADS])
        halfmask = sb("f_halfmask", [P, 2])
        q = sb("f_q", [P, OCT, TILES])
        kk = sb("f_k", [P, OCT, TILES])
        x = sb("f_x", [P, OCT, 2, TILES])
        kh = sb("f_kh", [P, 2, 2, HEADS, TILES])
        vh = sb("f_vh", [P, 2, 2, HEADS // 2, 2, DH])
        bd = sb("f_bd", [P, 2, HEADS, TILES])
        S = sb("f_S", [P, 2, HEADS, TILES])
        mx = sb("f_mx", [P, 2, HEADS])
        E = sb("f_E", [P, 2, HEADS, TILES])
        den = sb("f_den", [P, 2, HEADS])
        rden = sb("f_rden", [P, 2, HEADS])
        ET = sb("f_ET", [P, 2, HEADS // 2, P])
        O = sb("f_O", [P, 2, D])
        s = sems("f_const f_pQ f_pK f_q f_k f_x f_kh f_pV f_vh f_pS f_S f_mx f_sub f_E f_den f_rden f_pE "
                 "f_ET f_pO f_O f_pOT f_read f_turn f_poolturn",
                 dma="f_load f_bd0 f_bd1")
        bd_in = [s["f_bd0"], s["f_bd1"]]
        pQ, pK, pV, pS, pE, pO = ps[0], ps[1], ps[2], [ps[3], ps[4]], ps[5], ps[6]
        pOT = ps[7]
        n_load = 4
        GROUPS = P // OCT
        PAIRS = OCT // 2
        blk = ctx.enter_context(nc.Block())

        @blk.sync
        def _(sp):
            for dst, src in ((wq[:], A["L1_attn_Wqkv"][:, 0:D]), (wk[:], A["L1_attn_Wqkv"][:, D:2 * D]),
                             (wv[:], A["L1_attn_Wqkv"][:, 2 * D:3 * D]),
                             (wbias[:], A["L1_attn_r_w_bias"].rearrange("n (d o) -> (n d) o", o=1))):
                sp.dma_start(dst, src).then_inc(s["f_load"], 16)
            with sp.Fori(0, GROUPS) as g:
                for r in range(PAIRS):
                    m, p = PAIRS * g + r, r % 2
                    sp.wait_ge(s["f_S"], freed(m, 2))
                    for h in range(2):
                        sp.dma_start(bd[h * TILES:(h + 1) * TILES, p].rearrange("i n j -> i (n j)"),
                                     BD[bass.ds(2 * m + h, 1), 1:, :].rearrange("o i c -> (o i) c")).then_inc(bd_in[p], 16)

        @blk.gpsimd
        def _(pool):
            for name in "f_kh f_sub".split():
                pool.sem_inc(s[name], SEED)
            nc.gpsimd.memset(headmask[:], 1.0)
            nc.gpsimd.memset(halfmask[:], 1.0).then_inc(s["f_const"], 1)
            pool.wait_ge(s["f_const"], 1)
            nc.gpsimd.affine_select(out=headmask[:], in_=headmask[:], compare_op=ALU.is_ge, fill=0.0, base=0,
                                    pattern=[[-DH, HEADS]], channel_multiplier=1)
            nc.gpsimd.affine_select(out=halfmask[:], in_=halfmask[:], compare_op=ALU.is_ge, fill=0.0, base=0,
                                    pattern=[[-TILES, 2]], channel_multiplier=1).then_inc(s["f_const"], 1)
            pool.wait_ge(s["f_const"], 2)
            nc.gpsimd.affine_select(out=headmask[:], in_=headmask[:], compare_op=ALU.is_ge, fill=0.0, base=DH - 1,
                                    pattern=[[DH, HEADS]], channel_multiplier=-1)
            nc.gpsimd.affine_select(out=halfmask[:], in_=halfmask[:], compare_op=ALU.is_ge, fill=0.0, base=TILES - 1,
                                    pattern=[[TILES, 2]], channel_multiplier=-1).then_inc(s["f_const"], 1)
            pool.wait_ge(s["f_const"], 3)
            with pool.Fori(0, GROUPS) as g:
                for r0 in range(0, PAIRS, 2):
                    for r in (r0, r0 + 1):
                        m, p = PAIRS * g + r, r % 2
                        if r == 0:
                            pool.wait_ge(s["f_k"], made(g))
                        pool.wait_ge(s["f_pS"], freed(m, 2))
                        for h in range(2):
                            last = nc.gpsimd.tensor_tensor(kh[:, p, h], bc(kk[:, 2 * r + h, :], 1, [P, HEADS, TILES]),
                                                           bc(headmask[:], 2, [P, HEADS, TILES]), ALU.mult)
                        last.then_inc(s["f_kh"], 1)
                    for r in (r0, r0 + 1):
                        m, p = PAIRS * g + r, r % 2
                        pool.wait_ge(s["f_mx"], made(m))
                        nc.gpsimd.tensor_tensor(S[:, p], S[:, p], bc(mx[:, p, :], 2, [P, HEADS, TILES]),
                                                ALU.subtract).then_inc(s["f_sub"], 1)

        @blk.scalar
        def _(act):
            for name in "f_q f_k f_x f_E f_ET".split():
                act.sem_inc(s[name], SEED)
            act.wait_ge(s["f_load"], 16 * n_load)
            act.wait_ge(s["f_const"], 3)
            nc.scalar.activation(E[:, 0, 0, 0:1], ident[:, 0:1], ACT.Exp)
            with act.Fori(0, GROUPS) as g:
                act.wait_ge(s["f_pV"], freed(2 * g, 1))
                cols = wnT[:, bass.ds(g * OCT, OCT), :]
                nc.scalar.copy(x[:, :, 0, :], cols)
                nc.scalar.copy(x[:, :, 1, :], cols).then_inc(s["f_x"], 1)
                act.wait_ge(s["f_pQ"], made(g))
                act.wait_ge(s["f_pS"], freed(PAIRS * g, 1))
                nc.scalar.activation(q[:].rearrange("d b i -> d (b i)"), pQ[:], ACT.Identity,
                                     bias=wbias[:, 0:1]).then_inc(s["f_q"], 1)
                act.wait_ge(s["f_pK"], made(g))
                act.wait_ge(s["f_kh"], freed(PAIRS * g, 1))
                nc.scalar.copy(kk[:].rearrange("d b i -> d (b i)"), pK[:]).then_inc(s["f_k"], 1)
                for r0 in range(0, PAIRS, 2):
                    for r in (r0, r0 + 1):
                        m, p = PAIRS * g + r, r % 2
                        act.wait_ge(s["f_sub"], made(m))
                        act.wait_ge(s["f_pE"], freed(m, 2))
                        act.wait_ge(s["f_den"], freed(m, 2))
                        nc.scalar.activation(E[:, p], S[:, p], ACT.Exp, scale=DH ** -0.5).then_inc(s["f_E"], 1)
                    for r in (r0, r0 + 1):
                        m, p = PAIRS * g + r, r % 2
                        act.wait_ge(s["f_pE"], made(m))
                        act.wait_ge(s["f_pO"], freed(m, 2))
                        nc.scalar.copy(ET[:, p].rearrange("p c t -> p (c t)"), pE[:]).then_inc(s["f_ET"], 1)

        @blk.vector
        def _(dve):
            for name in "f_vh f_S f_mx f_den f_rden f_O f_read".split():
                dve.sem_inc(s[name], SEED)
            dve.wait_ge(s["f_const"], 3)
            with dve.Fori(0, GROUPS) as g:
                for r0 in range(0, PAIRS, 2):
                    for r in (r0, r0 + 1):
                        m, p = PAIRS * g + r, r % 2
                        dve.wait_ge(s["f_pV"], made(m))
                        dve.wait_ge(s["f_pO"], freed(m, 2))
                        nc.vector.tensor_tensor(vh[:, p].rearrange("p b c h d -> p (b c) h d"),
                                                pV[:, 0:2 * D].rearrange("p (c h d) -> p c h d", h=2, d=DH),
                                                halfmask[:].unsqueeze(1).unsqueeze(3).to_broadcast([P, HEADS, 2, DH]),
                                                ALU.mult).then_inc(s["f_vh"], 1)
                    for r in (r0, r0 + 1):
                        m, p = PAIRS * g + r, r % 2
                        dve.wait_ge(s["f_pS"], made(m))
                        dve.wait_ge(bd_in[p], 32 * (PAIRS // 2 * g + r // 2 + 1))
                        dve.wait_ge(s["f_E"], freed(m, 2))
                        nc.vector.tensor_tensor(S[:, p].rearrange("p n j -> p (n j)"), pS[p][:],
                                                bd[:, p].rearrange("p n j -> p (n j)"), ALU.add).then_inc(s["f_S"], 1)
                        dve.wait_ge(s["f_S"], made(m))
                        dve.wait_ge(s["f_sub"], freed(m, 2))
                        nc.vector.tensor_reduce(mx[:, p, :], S[:, p], AX.X, ALU.max).then_inc(s["f_mx"], 1)
                    for r in (r0, r0 + 1):
                        m, p = PAIRS * g + r, r % 2
                        dve.wait_ge(s["f_E"], made(m))
                        nc.vector.tensor_reduce(den[:, p, :], E[:, p], AX.X, ALU.add).then_inc(s["f_den"], 1)
                        dve.wait_ge(s["f_den"], made(m))
                        nc.vector.reciprocal(rden[:, p, :], den[:, p, :]).then_inc(s["f_rden"], 1)
                    for r in (r0, r0 + 1):
                        m, p = PAIRS * g + r, r % 2
                        dve.wait_ge(s["f_pO"], made(m))
                        dve.wait_ge(s["f_pOT"], freed(m, 2))
                        dve.wait_ge(s["f_rden"], made(m))
                        nc.vector.tensor_tensor(O[:, p].rearrange("p (n d) -> p n d", n=HEADS),
                                                pO[:, 0:D].rearrange("p (n d) -> p n d", n=HEADS),
                                                bc(rden[:, p, :], 2, [P, HEADS, DH]), ALU.mult).then_inc(s["f_O"], 1)
                    for r in (r0, r0 + 1):
                        m, p = PAIRS * g + r, r % 2
                        dve.wait_ge(s["f_pOT"], made(m))
                        nc.vector.tensor_copy(readT[:, bass.ds(2 * m, 2), :].rearrange("p b i -> p (b i)"),
                                              pOT[:, 0:P]).then_inc(s["f_read"], 1)

        @blk.tensor
        def _(pe):
            for name in "f_pQ f_pK f_pV f_pS f_pE f_pO f_pOT".split():
                pe.sem_inc(s[name], SEED)
            pe.wait_ge(s["f_load"], 16 * n_load)
            with pe.Fori(0, GROUPS) as g:
                cols = wnT[:, bass.ds(g * OCT, OCT), :].rearrange("d b i -> d (b i)")
                pe.wait_ge(s["f_q"], freed(g, 1))
                nc.tensor.matmul(pQ[:], wq[:], cols, start=True, stop=True).then_inc(s["f_pQ"], 1)
                pe.wait_ge(s["f_k"], freed(g, 1))
                nc.tensor.matmul(pK[:], wk[:], cols, start=True, stop=True).then_inc(s["f_pK"], 1)
                for r0 in range(0, PAIRS, 2):
                    for r in (r0, r0 + 1):
                        m, p = PAIRS * g + r, r % 2
                        pe.wait_ge(s["f_x"], made(g))
                        pe.wait_ge(s["f_vh"], freed(m, 1))
                        for h in range(2):
                            last = nc.tensor.matmul(pV[:, h * D:(h + 1) * D], x[:, 2 * r + h].rearrange("d a i -> d (a i)"),
                                                    wv[:], start=True, stop=True)
                        last.then_inc(s["f_pV"], 1)
                    for r in (r0, r0 + 1):
                        m, p = PAIRS * g + r, r % 2
                        pe.wait_ge(s["f_q"], made(g))
                        pe.wait_ge(s["f_kh"], made(m))
                        pe.wait_ge(s["f_S"], freed(m, 2))
                        for h in range(2):
                            last = nc.tensor.matmul(pS[p][h * TILES:(h + 1) * TILES, :], q[:, 2 * r + h, :],
                                                    kh[:, p, h].rearrange("d n j -> d (n j)"), start=True, stop=True)
                        last.then_inc(s["f_pS"], 1)
                    for r in (r0, r0 + 1):
                        m, p = PAIRS * g + r, r % 2
                        pe.wait_ge(s["f_E"], made(m))
                        pe.wait_ge(s["f_ET"], freed(m, 1))
                        for c in range(HEADS // 2):
                            last = nc.tensor.transpose(pE[:, bass.ts(c, P)],
                                                       E[:, p, 2 * c:2 * c + 2, :].rearrange("p n j -> p (n j)"), ident[:])
                        last.then_inc(s["f_pE"], 1)
                    for r in (r0, r0 + 1):
                        m, p = PAIRS * g + r, r % 2
                        pe.wait_ge(s["f_ET"], made(m))
                        pe.wait_ge(s["f_vh"], made(m))
                        pe.wait_ge(s["f_O"], freed(m, 1))
                        for h in range(2):
                            for c in range(HEADS // 2):
                                last = nc.tensor.matmul(pO[h * TILES:(h + 1) * TILES, c * 2 * DH:(c + 1) * 2 * DH],
                                                        ET[:, p, c, h * TILES:(h + 1) * TILES],
                                                        vh[:, p, h, c].rearrange("p h d -> p (h d)"), start=True, stop=True)
                        last.then_inc(s["f_pO"], 1)
                    for r in (r0, r0 + 1):
                        m, p = PAIRS * g + r, r % 2
                        pe.wait_ge(s["f_O"], made(m))
                        pe.wait_ge(s["f_read"], freed(m, 1))
                        nc.tensor.transpose(pOT[:, 0:P], O[:, p, :], ident[:]).then_inc(s["f_pOT"], 1)


def layer1_project(nc, A, sems, ps, H, ident, readT, score, XN3):
    ctx = ExitStack()
    with ctx:
        def sb(name, shape, dt=F32):
            return ctx.enter_context(nc.sbuf_tensor(name, shape, dt))
        power = sb("g_power", [P, QUAD])
        wo = sb("g_wo", [P, D])
        wh = sb("g_wh", [P, PICKS1])
        r = sb("g_r", [P, 2, QUAD, P])
        st, mv, ve, rstd = (sb("g_st", [P, 2, QUAD, 6]), sb("g_mv", [P, 2, QUAD, 2]), sb("g_ve", [P, 2, QUAD]),
                            sb("g_rstd", [P, 2, QUAD]))
        h = sb("g_h", [P, 2, QUAD, D])
        xn = sb("g_xn", [P, 2, QUAD, D])
        xT = sb("g_xT", [P, 2, QUAD * P])
        s = sems("g_const g_r g_pA g_h g_hk g_st g_mv g_ve g_rstd g_xn g_pT g_xT g_pG g_score g_stored "
                 "g_turn",
                 dma="g_load g_store0 g_store1")
        store = [s["g_store0"], s["g_store1"]]
        pA, pT, pG = [ps[0], ps[1]], ps[2], ps[3]
        XN3v = XN3.rearrange("(i t) d -> t i d", t=P)
        blk = ctx.enter_context(nc.Block())

        @blk.sync
        def _(sp):
            sp.dma_start(wo[:], A["L1_attn_Wo"]).then_inc(s["g_load"], 16)
            sp.dma_start(wh[:], A["L1_ffn_W_hash"][:, 0:PICKS1]).then_inc(s["g_load"], 16)
            sp.sem_inc(s["g_stored"], SEED)
            with sp.Fori(0, PAIRS_OF_QUADS) as i:
                for p in range(2):
                    sp.wait_ge(s["g_xn"], made(2 * i + p))
                    sp.dma_start(XN3v[:, bass.ds((2 * i + p) * QUAD, QUAD), :], xn[:, p]).then_inc(store[p], 16)
                for p in range(2):
                    sp.wait_ge(store[p], 16 * i + 16)
                    sp.sem_inc(s["g_stored"], 1)

        @blk.gpsimd
        def _(pool):
            pool.sem_inc(s["g_rstd"], SEED)
            pool.sem_inc(s["g_hk"], SEED)
            nc.gpsimd.memset(power[:], -0.5).then_inc(s["g_const"], 1)
            pool.wait_ge(s["g_const"], 1)
            with pool.Fori(0, PAIRS_OF_QUADS) as i:
                for p in range(2):
                    pool.wait_ge(s["g_ve"], made(2 * i + p))
                    nc.gpsimd.tensor_tensor(rstd[:, p, :], ve[:, p, :], power[:], ALU.pow).then_inc(s["g_rstd"], 1)
                for p in range(2):
                    nc.gpsimd.tensor_copy(H[:, bass.ds((2 * i + p) * QUAD, QUAD), :], h[:, p]).then_inc(s["g_hk"], 1)

        @blk.scalar
        def _(act):
            for name in "g_r g_xT".split():
                act.sem_inc(s[name], SEED)
            with act.Fori(0, PAIRS_OF_QUADS) as i:
                ns = [2 * i, 2 * i + 1]
                for p, n in enumerate(ns):
                    act.wait_ge(s["g_pA"], freed(n, 2))
                    nc.scalar.copy(r[:, p], readT[:, :, bass.ds(n * QUAD, QUAD)].rearrange("e b i -> e i b")).then_inc(s["g_r"], 1)
                for p, n in enumerate(ns):
                    act.wait_ge(s["g_pT"], made(n))
                    act.wait_ge(s["g_pG"], freed(n, 2))
                    nc.scalar.copy(xT[:, p, :], pT[:]).then_inc(s["g_xT"], 1)

        @blk.vector
        def _(dve):
            for name in "g_h g_st g_mv g_ve g_xn g_score".split():
                dve.sem_inc(s[name], SEED)
            with dve.Fori(0, PAIRS_OF_QUADS) as i:
                ns = [2 * i, 2 * i + 1]
                for p, n in enumerate(ns):
                    dve.wait_ge(s["g_pA"], made(n))
                    dve.wait_ge(s["g_hk"], freed(n, 2))
                    nc.vector.tensor_tensor(h[:, p], pA[p][:].rearrange("p (j d) -> p j d", j=QUAD),
                                            H[:, bass.ds(n * QUAD, QUAD), :], ALU.add).then_inc(s["g_h"], 1)
                    dve.wait_ge(s["g_h"], made(n))
                    turn(dve, s["g_turn"])
                    for j in range(QUAD):
                        last = nc.vector.bn_stats(st[:, p, j, :], h[:, p, j, :])
                    last.then_inc(s["g_st"], 1)
                    dve.wait_ge(s["g_st"], made(n))
                    turn(dve, s["g_turn"])
                    for j in range(QUAD):
                        last = nc.vector.bn_aggr(mv[:, p, j, :], st[:, p, j, :])
                    last.then_inc(s["g_mv"], 1)
                    dve.wait_ge(s["g_mv"], made(n))
                    nc.vector.tensor_scalar_add(ve[:, p, :], mv[:, p, :, 1], EPS).then_inc(s["g_ve"], 1)
                for p, n in enumerate(ns):
                    dve.wait_ge(s["g_rstd"], made(n))
                    dve.wait_ge(s["g_stored"], freed(n, 2))
                    dve.wait_ge(s["g_pT"], freed(n, 2))
                    for j in range(QUAD):
                        last = nc.vector.tensor_scalar(xn[:, p, j, :], h[:, p, j, :], mv[:, p, j, 0:1], rstd[:, p, j:j + 1],
                                                       ALU.subtract, ALU.mult)
                    last.then_inc(s["g_xn"], 1)
                for p, n in enumerate(ns):
                    dve.wait_ge(s["g_pG"], made(n))
                    nc.vector.tensor_copy(score[:, bass.ds(n * QUAD, QUAD), :],
                                          pG[:, 0:QUAD * PICKS1].rearrange("p (j c) -> p j c", j=QUAD)).then_inc(s["g_score"], 1)

        @blk.tensor
        def _(pe):
            for name in "g_pA g_pT g_pG".split():
                pe.sem_inc(s[name], SEED)
            pe.wait_ge(s["g_load"], 32)
            with pe.Fori(0, PAIRS_OF_QUADS) as i:
                ns = [2 * i, 2 * i + 1]
                for p, n in enumerate(ns):
                    pe.wait_ge(s["g_r"], made(n))
                    pe.wait_ge(s["g_h"], freed(n, 2))
                    for j in range(QUAD):
                        last = nc.tensor.matmul(pA[p][:, bass.ts(j, D)], r[:, p, j, :], wo[:], start=True, stop=True)
                    last.then_inc(s["g_pA"], 1)
                for p, n in enumerate(ns):
                    pe.wait_ge(s["g_xn"], made(n))
                    pe.wait_ge(s["g_xT"], freed(n, 1))
                    for j in range(QUAD):
                        last = nc.tensor.transpose(pT[:, bass.ts(j, P)], xn[:, p, j, :], ident[:])
                    last.then_inc(s["g_pT"], 1)
                for p, n in enumerate(ns):
                    pe.wait_ge(s["g_xT"], made(n))
                    pe.wait_ge(s["g_score"], freed(n, 1))
                    for j in range(QUAD):
                        last = nc.tensor.matmul(pG[:, j * PICKS1:(j + 1) * PICKS1], xT[:, p, bass.ts(j, P)], wh[:],
                                                start=True, stop=True)
                    last.then_inc(s["g_pG"], 1)


def layer1_routing(nc, sems, ps, before, ones, score, slot_in, slot_out, share):
    ctx = ExitStack()
    BEYOND = float(1 << 20)
    BANKS = E1 * TILES // 512
    with ctx:
        def sb(name, shape, dt=F32):
            return ctx.enter_context(nc.sbuf_tensor(name, shape, dt))
        y = sb("h_y", [P, TILES, PICKS1])
        low = sb("h_low", [P, TILES, PICKS1])
        low_i = sb("h_low_i", [P, TILES, PICKS1], I32)
        over = sb("h_over", [P, TILES, PICKS1])
        bucket = sb("h_bucket", [P, TILES, PICKS1])
        expert = sb("h_expert", [P, E1])
        hot = sb("h_hot", [P, PICKS1, E1, TILES], BF16)
        count = sb("h_count", [P, E1, TILES], BF16)
        fresh = sb("h_fresh", [P, E1, TILES], BF16)
        total = sb("h_total", [P, E1, TILES])
        place = sb("h_place", [P, E1, TILES])
        work = sb("h_work", [P, E1, TILES])
        at = sb("h_at", [P, TILES, PICKS1])
        s = sems("h_dve h_const h_count h_before h_taken h_totals")
        blk = ctx.enter_context(nc.Block())

        @blk.gpsimd
        def _(pool):
            nc.gpsimd.memset(fresh[:], 1.0).then_inc(s["h_const"], 1)
            pool.wait_ge(s["h_const"], 1)
            nc.gpsimd.memset(fresh[:, :, 0:1], 0.0)
            nc.gpsimd.iota(expert[:], pattern=[[1, E1]], base=0, channel_multiplier=0,
                           allow_small_or_imprecise_dtypes=True).then_inc(s["h_const"], 1)

        @blk.tensor
        def _(pe):
            flat = count[:].rearrange("p e i -> p (e i)")
            pe.wait_ge(s["h_count"], 1)
            for c in range(BANKS):
                last = nc.tensor.matmul(ps[c][:], before[:], flat[:, bass.ts(c, 512)], start=True, stop=True)
            last.then_inc(s["h_before"], 1)
            pe.wait_ge(s["h_taken"], 1)
            for c in range(BANKS):
                last = nc.tensor.matmul(ps[c][:], ones[:], flat[:, bass.ts(c, 512)], start=True, stop=True)
            last.then_inc(s["h_totals"], 1)

        @blk.scalar
        def _(act):
            act.wait_ge(s["h_before"], 1)
            for c in range(BANKS):
                last = nc.scalar.copy(work[:].rearrange("p e i -> p (e i)")[:, bass.ts(c, 512)], ps[c][:])
            last.then_inc(s["h_taken"], 1)

        @blk.vector
        def _(dve):
            V = nc.vector
            step = Chain(dve, s["h_dve"])

            def floor(to, of):
                step(V.tensor_copy(low_i[:], of))
                step(V.tensor_copy(low[:], low_i[:]))
                step(V.tensor_tensor(over[:], low[:], of, ALU.is_gt))
                step(V.tensor_tensor(to, low[:], over[:], ALU.subtract))
            step(V.tensor_scalar_mul(y[:], score[:], 8.0))
            floor(bucket[:], y[:])
            step(V.tensor_scalar_mul(y[:], bucket[:], 1.0 / E1))
            floor(at[:], y[:])
            step(V.scalar_tensor_tensor(bucket[:], at[:], -float(E1), bucket[:], ALU.mult, ALU.add))
            dve.wait_ge(s["h_const"], 2)
            for k in range(PICKS1):
                step(V.tensor_tensor(hot[:, k], bc(bucket[:, :, k], 1, [P, E1, TILES]),
                                     bc(expert[:], 2, [P, E1, TILES]), ALU.is_equal))
            V.tensor_tensor(count[:], hot[:, 0], hot[:, 1], ALU.add).then_inc(s["h_count"], 1)
            dve.wait_ge(s["h_totals"], 1)
            for c in range(BANKS):
                last = V.tensor_copy(total[:].rearrange("p e i -> p (e i)")[:, bass.ts(c, 512)], ps[c][:])
            step(last)
            step(V.tensor_tensor_scan(place[:].rearrange("p e i -> p (e i)"), fresh[:].rearrange("p e i -> p (e i)"),
                                      total[:].rearrange("p e i -> p (e i)"), 0.0, ALU.mult, ALU.add))
            step(V.tensor_tensor(place[:], place[:], total[:], ALU.subtract))
            dve.wait_ge(s["h_taken"], 1)
            step(V.tensor_tensor(place[:], place[:], work[:], ALU.add))
            for k in range(PICKS1):
                step(V.tensor_tensor(work[:], place[:], hot[:, k], ALU.mult))
                step(V.tensor_reduce(at[:, :, k], work[:].rearrange("p e i -> p i e"), AX.X, ALU.add))
            step(V.tensor_tensor(over[:, :, 0], bucket[:, :, 0], bucket[:, :, 1], ALU.is_equal))
            step(V.tensor_tensor(at[:, :, 1], at[:, :, 1], over[:, :, 0], ALU.add))
            step(V.tensor_scalar(over[:], at[:], float(CAP1), None, ALU.is_ge))
            step(V.tensor_scalar(share[:], over[:], -1.0 / PICKS1, 1.0 / PICKS1, ALU.mult, ALU.add))
            step(V.scalar_tensor_tensor(y[:], bucket[:], float(CAP1), at[:], ALU.mult, ALU.add))
            step(V.scalar_tensor_tensor(slot_in[:], over[:], BEYOND, y[:], ALU.mult, ALU.add))
            step(V.tensor_scalar(at[:], at[:], float(CAP1 - 1), None, ALU.min))
            step(V.scalar_tensor_tensor(slot_out[:], bucket[:], float(CAP1), at[:], ALU.mult, ALU.add))


def layer1_experts(nc, A, sems, ps, ident, XS1, YS1):
    ctx = ExitStack()
    CH = HID // P
    PARTS = [(0, P), (P, P), (2 * P, CAP1 - 2 * P)]
    with ctx:
        def sb(name, shape, dt=F32):
            return ctx.enter_context(nc.sbuf_tensor(name, shape, dt))
        w1 = sb("i_w1", [P, 2, HID])
        w2 = sb("i_w2", [P, 2, CH, D])
        b1 = sb("i_b1", [P, E1, CH])
        b2 = sb("i_b2", [P, 2, D])
        x = sb("i_x", [P, 2, 3, D])
        xT = sb("i_xT", [P, 2, CAP1])
        h = sb("i_h", [P, 2, CH, CAP1])
        y = sb("i_y", [P, 2, 3, D])
        warm = sb("i_warm", [P, 1])
        s = sems("i_pT i_xT i_p1 i_h i_pY i_y i_stored",
                 dma="i_b1 i_w0 i_w1 i_out0 i_out1")
        landed, out = [s["i_w0"], s["i_w1"]], [s["i_out0"], s["i_out1"]]
        pT, p1, pY = [ps[0], ps[1]], ps[2:6], [ps[6], ps[7]]
        n_dma = 5
        blk = ctx.enter_context(nc.Block())

        @blk.sync
        def _(sp):
            sp.dma_start(b1[:], A["L1_ffn_b1"]).then_inc(s["i_b1"], 16)
            with sp.Fori(0, E1 // 2) as i:
                for p in range(2):
                    e = 2 * i + p
                    sp.wait_ge(s["i_y"], freed(e, 2))
                    sp.dma_start(w1[:, p, :], A["L1_ffn_W1"][e]).then_inc(landed[p], 16)
                    sp.dma_start(w2[:, p], A["L1_ffn_W2"][e].rearrange("(c p) d -> p c d", p=P)).then_inc(landed[p], 16)
                    sp.dma_start(b2[:, p, :], A["L1_ffn_b2"][e].partition_broadcast(P)).then_inc(landed[p], 16)
                    sp.dma_start(x[:, p, 0:2, :], XS1[bass.ds(e * CAP1, 2 * P), :].rearrange("(c t) d -> t c d", t=P)).then_inc(landed[p], 16)
                    sp.dma_start(x[0:CAP1 - 2 * P, p, 2, :], XS1[bass.ds(e * CAP1 + 2 * P, CAP1 - 2 * P), :]).then_inc(landed[p], 16)

        @blk.gpsimd
        def _(pool):
            pool.sem_inc(s["i_stored"], SEED)
            with pool.Fori(0, E1 // 2) as i:
                for p in range(2):
                    e = 2 * i + p
                    pool.wait_ge(s["i_y"], made(e))
                    pool.dma_start(YS1[bass.ds(e * CAP1, 2 * P), :].rearrange("(c t) d -> t c d", t=P),
                                   y[:, p, 0:2, :]).then_inc(out[p], 16)
                    pool.dma_start(YS1[bass.ds(e * CAP1 + 2 * P, CAP1 - 2 * P), :],
                                   y[0:CAP1 - 2 * P, p, 2, :]).then_inc(out[p], 16)
                for p in range(2):
                    pool.wait_ge(out[p], 32 * i + 32)
                    pool.sem_inc(s["i_stored"], 1)

        @blk.scalar
        def _(act):
            act.sem_inc(s["i_h"], CH)
            act.wait_ge(s["i_b1"], 16)
            nc.scalar.activation(warm[:], ident[:, 0:1], ACT.Gelu)
            with act.Fori(0, E1 // 2) as i:
                for p in range(2):
                    e = 2 * i + p
                    for c in range(CH):
                        m = e * CH + c
                        act.wait_ge(s["i_p1"], made(m))
                        if c == 0:
                            act.wait_ge(s["i_pY"], freed(e, 2))
                        nc.scalar.activation(h[:, p, c, :], p1[c][:, 0:CAP1], ACT.Gelu,
                                             bias=b1[:, bass.ds(e, 1), c]).then_inc(s["i_h"], 1)

        @blk.vector
        def _(dve):
            for name in "i_y".split():
                dve.sem_inc(s[name], SEED)
            dve.sem_inc(s["i_xT"], SEED)
            with dve.Fori(0, E1 // 2) as i:
                for p in range(2):
                    e = 2 * i + p
                    dve.wait_ge(s["i_pT"], made(e))
                    dve.wait_ge(s["i_pY"], freed(e, 2))
                    nc.vector.tensor_copy(xT[:, p, :], pT[p][:, 0:CAP1]).then_inc(s["i_xT"], 1)
                for p in range(2):
                    e = 2 * i + p
                    dve.wait_ge(s["i_pY"], made(e))
                    dve.wait_ge(s["i_stored"], freed(e, 2))
                    nc.vector.tensor_tensor(y[:, p, 0:2, :], pY[p][:, 0:2 * D].rearrange("p (c d) -> p c d", c=2),
                                            bc(b2[:, p, :], 1, [P, 2, D]), ALU.add)
                    nc.vector.tensor_tensor(y[0:CAP1 - 2 * P, p, 2, :], pY[p][0:CAP1 - 2 * P, 2 * D:3 * D],
                                            b2[0:CAP1 - 2 * P, p, :], ALU.add).then_inc(s["i_y"], 1)

        @blk.tensor
        def _(pe):
            for name in "i_pT i_p1 i_pY".split():
                pe.sem_inc(s[name], SEED)
            with pe.Fori(0, E1 // 2) as i:
                for p in range(2):
                    pe.wait_ge(landed[p], 16 * n_dma * (i + 1))
                    for t, (_, rows) in enumerate(PARTS):
                        last = nc.tensor.transpose(pT[p][:, t * P:t * P + rows], x[0:rows, p, t, :], ident[0:rows, 0:rows])
                    last.then_inc(s["i_pT"], 1)
                for p in range(2):
                    e = 2 * i + p
                    pe.wait_ge(s["i_xT"], made(e))
                    for c in range(CH):
                        m = e * CH + c
                        pe.wait_ge(s["i_h"], m + 1)
                        nc.tensor.matmul(p1[c][:, 0:CAP1], w1[:, p, bass.ts(c, P)], xT[:, p, :],
                                         start=True, stop=True).then_inc(s["i_p1"], 1)
                for p in range(2):
                    e = 2 * i + p
                    pe.wait_ge(s["i_h"], CH * (e + 2))
                    pe.wait_ge(s["i_y"], freed(e, 2))
                    for t, (at, rows) in enumerate(PARTS):
                        for c in range(CH):
                            last = nc.tensor.matmul(pY[p][0:rows, t * D:(t + 1) * D], h[:, p, c, at:at + rows], w2[:, p, c, :],
                                                    start=(c == 0), stop=(c == CH - 1))
                    last.then_inc(s["i_pY"], 1)


def layer1_combine(nc, sems, H, slot_out, share, YS1, out):
    ctx = ExitStack()
    with ctx:
        def sb(name, shape, dt=F32):
            return ctx.enter_context(nc.sbuf_tensor(name, shape, dt))
        idx = sb("j_idx", [P, 2, QUAD, PICKS1], I32)
        got = sb("j_got", [P, 2, QUAD, PICKS1, D])
        wt = sb("j_wt", [P, 2, QUAD, PICKS1])
        acc = sb("j_acc", [P, 2, QUAD, D])
        s = sems("j_idx j_acck j_acc j_stored j_poolturn", dma="j_got0 j_got1 j_out0 j_out1")
        got_in, store = [s["j_got0"], s["j_got1"]], [s["j_out0"], s["j_out1"]]
        out_v = out.rearrange("i t d -> t i d")
        blk = ctx.enter_context(nc.Block())

        @blk.gpsimd
        def _(pool):
            pool.sem_inc(s["j_idx"], SEED)
            with pool.Fori(0, PAIRS_OF_QUADS) as i:
                for p in range(2):
                    n = 2 * i + p
                    pool.wait_ge(s["j_acc"], freed(n, 2))
                    turn(pool, s["j_poolturn"])
                    nc.gpsimd.tensor_copy(idx[:, p], slot_out[:, bass.ds(n * QUAD, QUAD), :]).then_inc(s["j_idx"], 1)
                    pool.wait_ge(s["j_idx"], made(n))
                    turn(pool, s["j_poolturn"])
                    for j in range(QUAD):
                        for k in range(PICKS1):
                            nc.gpsimd.indirect_dma_start(
                                out=got[:, p, j, k, :], out_offset=None, in_=YS1,
                                in_offset=bass.IndirectOffsetOnAxis(ap=idx[:, p, j, k:k + 1], axis=0)).then_inc(got_in[p], 16)

        @blk.vector
        def _(dve):
            for name in "j_acc j_acck".split():
                dve.sem_inc(s[name], SEED)
            with dve.Fori(0, PAIRS_OF_QUADS) as i:
                for p in range(2):
                    n = 2 * i + p
                    dve.wait_ge(s["j_stored"], freed(n, 2))
                    nc.vector.tensor_copy(wt[:, p], share[:, bass.ds(n * QUAD, QUAD), :])
                    nc.vector.tensor_copy(acc[:, p], H[:, bass.ds(n * QUAD, QUAD), :]).then_inc(s["j_acck"], 1)
                    dve.wait_ge(got_in[p], 16 * QUAD * PICKS1 * (i + 1))
                    for k in range(PICKS1):
                        dve.wait_ge(s["j_acck"], SEED + PICKS1 * n + k + 1)
                        for j in range(QUAD):
                            last = nc.vector.scalar_tensor_tensor(acc[:, p, j, :], got[:, p, j, k, :], wt[:, p, j, k:k + 1],
                                                                  acc[:, p, j, :], ALU.mult, ALU.add)
                        last.then_inc(s["j_acck"] if k < PICKS1 - 1 else s["j_acc"], 1)

        @blk.sync
        def _(sp):
            sp.sem_inc(s["j_stored"], SEED)
            with sp.Fori(0, PAIRS_OF_QUADS) as i:
                for p in range(2):
                    n = 2 * i + p
                    sp.wait_ge(s["j_acc"], made(n))
                    sp.dma_start(out_v[:, bass.ds(n * QUAD, QUAD), :], acc[:, p]).then_inc(store[p], 16)
                for p in range(2):
                    sp.wait_ge(store[p], 16 * i + 16)
                    sp.sem_inc(s["j_stored"], 1)


_INPUTS = ["x", "L0_tok_w", "L0_attn_Wk", "L0_attn_bk", "L0_attn_Wq", "L0_attn_bq", "L0_attn_Wv", "L0_attn_bv",
           "L0_ffn_Wr", "L0_ffn_br", "L0_ffn_Wgate", "L0_ffn_bgate", "L0_ffn_W1", "L0_ffn_W3", "L0_ffn_W2",
           "L1_attn_Wqkv", "L1_attn_Wr", "L1_attn_Wo", "L1_attn_ln_gamma", "L1_attn_ln_beta", "L1_attn_r_w_bias",
           "L1_attn_r_r_bias", "L1_ffn_W_hash", "L1_ffn_W1", "L1_ffn_b1", "L1_ffn_W2", "L1_ffn_b2"]


def kernel(**inputs):
    import concourse.bacc as bacc
    from concourse.bass_utils import run_bass_kernel_spmd

    laid = layout({n: np.asarray(inputs[n]) for n in _INPUTS})
    nc = bacc.Bacc("TRN2", target_bir_lowering=False, num_devices=1)
    arrays, A = {}, {}
    for name, a in laid.items():
        arrays[f"in_{name}"] = a
        A[name] = nc.dram_tensor(f"in_{name}", a.shape, mybir.dt.from_np(a.dtype), kind="ExternalInput").ap()
    out = nc.dram_tensor("out", (TILES, P, D), F32, kind="ExternalOutput").ap()
    tower(nc, A, out)
    return run_bass_kernel_spmd(nc, [arrays], core_ids=[0]).results[0]["out"]
```

```python
from contextlib import ExitStack

import numpy as np
import concourse.bass as bass
from concourse import mybir

F32 = mybir.dt.float32
BF16 = mybir.dt.bfloat16
I32 = mybir.dt.int32
ALU = mybir.AluOpType
ACT = mybir.ActivationFunctionType
AX = mybir.AxisListType

P = 128
D = 128
TILES = 64
TOKENS = TILES * P
QUAD = 4
PAIRS_OF_QUADS = TILES // QUAD // 2
HID = 512
E0, G0, EPG0 = 16, 4, 4
PICKS0 = 4
BLOCKS0 = TOKENS * PICKS0 // P + E0
E1, CAP1, PICKS1 = 64, 320, 2
SLOTS1 = E1 * CAP1
SUPER = 16
QUADS = SUPER // QUAD
SUPERS = TILES // SUPER
REGION0 = TOKENS + P
SPARE0 = E0 * REGION0
ROWS0 = SPARE0 + (E0 + 1) * P
ROW = D + 2
NOWHERE = float(1 << 20)
ROUTE_STEPS = 71
BUCKET_STEPS = 30
HEADS, DH = 8, 16
EPS = 1e-5
MASKED = -1e30
SEED = 2


def made(n):
    return n + SEED + 1


def freed(n, bufs):
    return n + SEED + 1 - bufs


def bc(ap, dim, shape):
    return ap.unsqueeze(dim).to_broadcast(shape)


def live(n, count):
    return not isinstance(n, int) or 0 <= n < count


def wait_free(eng, sem, n, bufs):
    if not (isinstance(n, int) and n < bufs):
        eng.wait_ge(sem, freed(n, bufs))


def pipeline(eng, count, lead, lag, unroll, body):
    for n in range(-lead, unroll):
        body(n, n % unroll, n // unroll)
    with eng.Fori(1, count // unroll - 1) as i:
        for k in range(unroll):
            body(i * unroll + k, k, i)
    for n in range(count - unroll, count + lag):
        body(n, n % unroll, n // unroll)


def turn(eng, tally):
    eng.sem_inc(tally, 1)


class Chain:

    def __init__(self, eng, sem, start=0):
        self.eng, self.sem, self.start, self.n = eng, sem, start, 0

    def __call__(self, ins):
        self.n += 1
        ins.then_inc(self.sem, 1)
        self.eng.wait_ge(self.sem, self.start + self.n)


def positions():
    seq = np.arange(TILES - 1, -1, -1, dtype=np.float32)
    freq = np.float32(1.0) / np.float32(10000.0) ** (np.arange(0, D, 2, dtype=np.float32) / np.float32(D))
    angle = (seq[:, None] * freq[None, :]).astype(np.float32)
    return np.ascontiguousarray(np.concatenate([np.sin(angle), np.cos(angle)], axis=-1).T.astype(np.float32))


TRANSPOSED = ("x", "L1_attn_Wqkv", "L1_attn_Wr", "L1_attn_Wo", "L1_ffn_W_hash")


def layout(inputs):
    laid = {n: np.ascontiguousarray(a.T if n in TRANSPOSED else a) for n, a in inputs.items()}
    b1 = inputs["L1_ffn_b1"].reshape(E1, HID // P, P)
    laid["L1_ffn_b1"] = np.ascontiguousarray(b1.transpose(2, 0, 1))
    laid["positions"] = positions()
    return laid


class Signals:

    def __init__(self, nc, ctx):
        self.nc, self.ctx, self.of_stage = nc, ctx, []

    def __call__(self, names, dma=""):
        own = {n: self.nc.alloc_semaphore(n) for n in names.split()}
        self.of_stage += own.values()
        return own | {n: self.ctx.enter_context(self.nc.semaphore(n)) for n in dma.split()}

    def end_stage(self):
        self.nc.clear_and_free_semaphores(self.of_stage)
        self.of_stage = []
        self.nc.all_engine_barrier()


def tower(nc, A, out, stop=None):
    ctx = ExitStack()

    sems = Signals(nc, ctx)

    def dram(name, shape, dt=F32):
        return nc.dram_tensor(name, shape, dt, kind="Internal").ap()

    XN1 = dram("XN1", (TOKENS, D))
    XS0 = dram("XS0", (ROWS0, ROW))
    YT0 = dram("YT0", (TOKENS * PICKS0, D))
    BD = dram("BD", (P, TILES + 1, HEADS * TILES))
    XN3 = dram("XN3", (TOKENS, D))
    XS1 = dram("XS1", (SLOTS1, ROW))
    YT1 = dram("YT1", (TOKENS * PICKS1, D))

    with ctx:
        def keep(name, shape, dt=F32):
            return ctx.enter_context(nc.sbuf_tensor(name, shape, dt))

        ps = [ctx.enter_context(nc.psum_tensor(f"ps{i}", [P, 512], F32)) for i in range(8)]
        H = keep("H", [P, TILES, D])
        ident = keep("ident", [P, P])
        before = keep("before", [P, P], BF16)
        ones = keep("ones", [P, P], BF16)

        with ExitStack() as c0:
            def sb0(name, shape, dt=F32):
                return c0.enter_context(nc.sbuf_tensor(name, shape, dt))
            block_expert = sb0("block_expert", [1, BLOCKS0], I32)
            block_row = sb0("block_row", [1, BLOCKS0], I32)
            w1 = sb0("w1", [P, E0, HID])
            w3 = sb0("w3", [P, E0, HID])
            w2 = sb0("w2", [P, E0, HID // P, D])
            layer0_attention(nc, A, sems, ps, H, ident, before, ones, w1, w3, w2, block_expert, block_row,
                             XN1, XS0, XS1, YT1)
            sems.end_stage()
            if stop == "A":
                return
            layer0_experts(nc, sems, ps, ident, block_expert, block_row, w1, w3, w2, XS0, YT0)
            sems.end_stage()
            if stop == "C":
                return
        with ExitStack() as c1:
            wnT = c1.enter_context(nc.sbuf_tensor("wnT", [P, P, TILES], F32))
            layer0_combine(nc, A, sems, ps, H, ident, wnT, YT0, BD)
            sems.end_stage()
            if stop == "D":
                return
            readT = c1.enter_context(nc.sbuf_tensor("readT", [P, P, TILES], F32))
            layer1_attention(nc, A, sems, ps, ident, wnT, readT, BD)
            sems.end_stage()
            layer1_project(nc, A, sems, ps, H, ident, before, ones, readT, XN3, XS1)
            sems.end_stage()
            if stop == "E":
                return
        layer1_experts(nc, A, sems, ps, ident, XS1, YT1)
        sems.end_stage()
        layer1_combine(nc, sems, H, YT1, out)
        sems.end_stage()


def route_top2(dve, V, step, s, u, small, prob, rank, first, second, work, pair, picks, logit, total, row, fresh, carry,
               pC, slot, extra, dest):
    flat5 = "p i g e -> p (i g) e"
    group = [P, SUPER * (1 + G0), EPG0]

    def small_(k):
        return small[k][:].rearrange("p i g -> p (i g)")
    step(V.tensor_reduce(small_(0), logit[:].rearrange(flat5), AX.X, ALU.max))
    V.tensor_tensor(work[:].rearrange(flat5), logit[:].rearrange(flat5), bc(small_(0), 2, group),
                    ALU.subtract).then_inc(s["r_max"], 1)
    dve.wait_ge(s["r_exp"], made(u))
    step(V.tensor_reduce(small_(0), prob[:].rearrange(flat5), AX.X, ALU.add))
    step(V.reciprocal(small_(1), small_(0)))
    step(V.tensor_tensor(prob[:].rearrange(flat5), prob[:].rearrange(flat5), bc(small_(1), 2, group), ALU.mult))
    pr, rk = prob[:].rearrange(flat5), rank[:].rearrange(flat5)
    pairs = [(a, b) for a in range(EPG0) for b in range(a + 1, EPG0)]
    for k, (a, b) in enumerate(pairs):
        last = V.tensor_tensor(pair[:, k, :], pr[:, :, a], pr[:, :, b], ALU.is_ge)
    step(last)
    for e in range(EPG0):
        losing = [k for k, (a, b) in enumerate(pairs) if b == e]
        winning = [k for k, (a, b) in enumerate(pairs) if a == e]
        if winning:
            step(V.tensor_scalar(rk[:, :, e], pair[:, winning[0], :], -1.0, float(len(winning)), ALU.mult, ALU.add))
            for k in winning[1:]:
                step(V.tensor_tensor(rk[:, :, e], rk[:, :, e], pair[:, k, :], ALU.subtract))
        else:
            step(V.tensor_copy(rk[:, :, e], pair[:, losing.pop(0), :]))
        for k in losing:
            step(V.tensor_tensor(rk[:, :, e], rk[:, :, e], pair[:, k, :], ALU.add))
    V.tensor_scalar(first[:], rank[:], 0.0, None, ALU.is_equal)
    step(V.tensor_scalar(second[:], rank[:], 1.0, None, ALU.is_equal))
    step(V.tensor_tensor(work[:], first[:], second[:], ALU.add))
    V.tensor_tensor(picks[:].rearrange("p (g e) i -> p i g e", g=G0), work[:, :, 1:, :],
                    bc(work[:, :, 0, :], 3, [P, SUPER, G0, EPG0]), ALU.mult).then_inc(s["r_picks"], 1)
    dve.wait_ge(s["r_picks"], made(u))
    step(V.tensor_tensor(work[:], prob[:], first[:], ALU.mult))
    step(V.tensor_reduce(small_(0), work[:].rearrange(flat5), AX.X, ALU.add))
    step(V.tensor_tensor(work[:], prob[:], second[:], ALU.mult))
    step(V.tensor_reduce(small_(1), work[:].rearrange(flat5), AX.X, ALU.add))
    step(V.tensor_tensor(small[2][:], small[0][:], small[1][:], ALU.add))
    step(V.tensor_scalar(small[2][:], small[2][:], 0.9, None, ALU.is_le))
    step(V.tensor_tensor(small[1][:], small[1][:], small[2][:], ALU.mult))
    step(V.tensor_tensor(small[2][:], small[0][:], small[1][:], ALU.add))
    step(V.tensor_scalar_add(small[2][:], small[2][:], 1e-9))
    step(V.reciprocal(small[3][:], small[2][:]))
    step(V.tensor_tensor(small[0][:], small[0][:], small[3][:], ALU.mult))
    step(V.tensor_tensor(small[1][:], small[1][:], small[3][:], ALU.mult))
    dve.wait_ge(s["r_counted"], made(u))
    flat_row, n = row[:].rearrange("p e i -> p (e i)"), E0 * SUPER
    step(V.tensor_copy(total[:].rearrange("p e i -> p (e i)"), pC[:, n:2 * n]))
    step(V.tensor_tensor_scan(flat_row, fresh[:].rearrange("p e i -> p (e i)"), total[:].rearrange("p e i -> p (e i)"),
                              0.0, ALU.mult, ALU.add))
    step(V.tensor_copy(small[4][:, :, 0], row[:, :, SUPER - 1]))
    step(V.tensor_tensor(row[:], row[:], total[:], ALU.subtract))
    step(V.tensor_tensor(flat_row, flat_row, pC[:, 0:n], ALU.add))
    step(V.tensor_tensor(row[:], row[:], bc(carry[:], 2, [P, E0, SUPER]), ALU.add))
    step(V.tensor_tensor(carry[:], carry[:], small[4][:, :, 0], ALU.add))
    row_v = row[:].rearrange("p (g e) i -> p i g e", g=G0)
    pick16 = work[:].rearrange("p i g e -> p (i g e)")[:, 0:n].rearrange("p (i g e) -> p i g e", i=SUPER, g=G0)
    pick_w = small[4][:, :, G0]
    for a, of_group in enumerate((first, second)):
        for b, of_expert in enumerate((first, second)):
            k = 2 * a + b
            step(V.tensor_tensor(pick16, of_expert[:, :, 1:, :], bc(of_group[:, :, 0, :], 3, [P, SUPER, G0, EPG0]),
                                 ALU.mult))
            step(V.tensor_tensor(pick16, pick16, row_v, ALU.mult))
            step(V.tensor_reduce(pick_w, pick16, AX.XY, ALU.add))
            step(V.tensor_copy(slot[:, :, k], pick_w))
            four = small[4][:, :, 0:G0]
            step(V.tensor_tensor(four, of_group[:, :, 0, :], small[b][:, :, 1:], ALU.mult))
            step(V.tensor_reduce(pick_w, four, AX.X, ALU.add))
            step(V.tensor_tensor(pick_w, pick_w, small[a][:, :, 0], ALU.mult))
            step(V.tensor_scalar_mul(extra[:, :, k, 0], pick_w, float(G0) ** -0.5))
    step(V.tensor_copy(extra[:, :, :, 1], dest[:]))
    V.tensor_scalar_add(dest[:], dest[:], float(SUPER * P * PICKS0)).then_inc(s["r_slots"], 1)
    dve.wait_ge(s["r_slots"], made(u))


def layer0_attention(nc, A, sems, ps, H, ident, before, ones, w1, w3, w2, block_expert, block_row, XN1, XS0, XS1, YT1):
    ctx = ExitStack()
    with ctx:
        def sb(name, shape, dt=F32):
            return ctx.enter_context(nc.sbuf_tensor(name, shape, dt))
        zeros = sb("zeros", [P, 512])
        filler = sb("filler", [P, ROW])
        causal = sb("causal", [P, P])
        power = sb("power", [P, QUAD])
        warm = sb("warm", [P, 1])
        xidx = sb("xidx", [P, TILES], I32)
        wq, wk, wv = sb("wq", [P, D]), sb("wk", [P, D]), sb("wv", [P, D])
        bq, bk, bv = sb("bq", [P, 1]), sb("bk", [P, 1]), sb("bv", [P, D])
        wr = sb("wr", [P, 1 + G0, EPG0])
        br = sb("br", [P, 1 + G0, EPG0])
        idx4 = sb("idx4", [P, 2, QUAD], I32)
        h0 = sb("h0", [P, 2, QUAD, D])
        st = sb("st", [P, 2, QUAD, 6])
        mv = sb("mv", [P, 2, QUAD, 2])
        ve = sb("ve", [P, 2, QUAD])
        rstd = sb("rstd", [P, 2, QUAD])
        xn = sb("xn", [P, 2, QUAD, D])
        xT = sb("xT", [P, 2, QUAD * P])
        qT = sb("qT", [P, 2, QUAD * P])
        kT = sb("kT", [P, 2, QUAD * P])
        v = sb("v", [P, 2, QUAD, D])
        lm = sb("lm", [P, 2, QUAD, P])
        nmx = sb("nmx", [P, 2, QUAD])
        psum = sb("psum", [P, 2, QUAD])
        rsum = sb("rsum", [P, 2, QUAD])
        st1 = sb("st1", [P, 2, QUAD, 6])
        mv1 = sb("mv1", [P, 2, QUAD, 2])
        ve1 = sb("ve1", [P, 2, QUAD])
        rstd1 = sb("rstd1", [P, 2, QUAD])
        xn1 = sb("xn1", [P, 2, QUAD, D])
        logit = sb("r_logit", [P, SUPER, 1 + G0, EPG0])
        prob4 = sb("r_prob", [P, SUPER, 1 + G0, EPG0])
        rank = sb("r_rank", [P, SUPER, 1 + G0, EPG0])
        first = sb("r_first", [P, SUPER, 1 + G0, EPG0])
        second = sb("r_second", [P, SUPER, 1 + G0, EPG0])
        work = sb("r_work", [P, SUPER, 1 + G0, EPG0])
        pair = sb("r_pair", [P, 6, SUPER * (1 + G0)])
        small = [sb(f"r_small{k}", [P, SUPER, 1 + G0]) for k in range(5)]
        picks = sb("r_picks_t", [P, E0, SUPER], BF16)
        total = sb("r_total", [P, E0, SUPER])
        row = sb("r_row", [P, E0, SUPER])
        fresh = sb("r_fresh", [P, E0, SUPER])
        carry = sb("r_carry", [P, E0])
        region = sb("r_region", [P, E0])
        slot = sb("r_slot", [P, SUPER, PICKS0], I32)
        extra = sb("r_extra", [P, SUPER, PICKS0, 2])
        dest = sb("r_dest", [P, SUPER, PICKS0])
        sidx = sb("sidx", [P, 2, QUAD, PICKS0], I32)
        rows = sb("rows", [P, 2, QUAD, PICKS0, ROW])
        count_i = sb("t_count_i", [P, E0], I32)
        padded = sb("t_padded", [1, E0], I32)
        blocks = sb("t_blocks", [P, E0])
        block_end = sb("t_block_end", [P, E0])
        index = sb("t_index", [1, BLOCKS0])
        reached = sb("t_reached", [1, BLOCKS0 // 4, E0], BF16)
        passed = sb("t_passed", [1, BLOCKS0])
        expert_f = sb("t_expert_f", [1, BLOCKS0])
        pT, pQ, pK, pV, pL, pR, pC, pG = ps
        s = sems("a_const a_eye a_idx a_stats a_mv a_ve a_rstd a_xn a_hx a_pT a_xT a_pQ a_pK a_pV a_qT a_kT a_v "
                 "a_pL a_lm a_max a_prob a_rsum a_vs a_pR a_h1 a_stats1 a_mv1 a_ve1 a_rstd1 a_xn1 a_stored a_pT1 "
                 "a_x1T a_pG a_logit a_zero a_p2 a_turn a_poolturn a_staged a_scattered a_fillready a_padded "
                 "r_dve r_max r_exp r_picks r_counted r_slots t_dve t_ready",
                 dma="a_load a_xload a_zeroed a_expw a_gather0 a_gather1 a_store0 a_store1 a_rows0 a_rows1 a_sent0 "
                     "a_sent1 a_filled")
        gather = [s["a_gather0"], s["a_gather1"]]
        store = [s["a_store0"], s["a_store1"]]
        staged = [s["a_rows0"], s["a_rows1"]]
        sent = [s["a_sent0"], s["a_sent1"]]
        n_load = 10
        XN1v = XN1.rearrange("(i t) d -> t i d", t=P)
        z1 = XS1.rearrange("(p a) r -> p a r", p=P)
        zy = YT1.rearrange("(p r) d -> p (r d)", p=P)
        Z1, ZY = 8, 512
        n_zero = z1.shape[1] // Z1 + zy.shape[1] // ZY + (E0 + 1)
        blk = ctx.enter_context(nc.Block())

        def quads(u, half):
            return [(p, u * QUADS + 2 * half + p) for p in range(2)]

        def supers(eng, body, after=0):
            body(0)
            with eng.Fori(1, SUPERS) as u:
                body(u)
            if after:
                body(SUPERS)

        @blk.sync
        def _(sp):
            sp.dma_start(xidx[:], A["x"]).then_inc(s["a_xload"], 16)
            for dst, src in ((wq[:], A["L0_attn_Wq"]), (wk[:], A["L0_attn_Wk"]), (wv[:], A["L0_attn_Wv"]),
                             (bq[:], A["L0_attn_bq"].unsqueeze(1)), (bk[:], A["L0_attn_bk"].unsqueeze(1)),
                             (bv[:], A["L0_attn_bv"].partition_broadcast(P)),
                             (wr[:, 0, :], A["L0_ffn_Wr"]),
                             (wr[:, 1:, :], A["L0_ffn_Wgate"].rearrange("g d e -> d g e")),
                             (br[:, 0, :], A["L0_ffn_br"].partition_broadcast(P)),
                             (br[:, 1:, :], A["L0_ffn_bgate"].partition_broadcast(P))):
                sp.dma_start(dst, src).then_inc(s["a_load"], 16)
            sp.sem_inc(s["a_stored"], SEED)
            sp.wait_ge(s["a_fillready"], 1)
            with sp.Fori(0, E0 + 1) as e:
                sp.dma_start(XS0[bass.ds(SPARE0 + e * P, P), :], filler[:]).then_inc(s["a_zeroed"], 16)

            def background(part):
                with sp.Fori(part * (E0 // 4), (part + 1) * (E0 // 4)) as e:
                    sp.dma_start(w1[:, e, :], A["L0_ffn_W1"][e]).then_inc(s["a_expw"], 16)
                    sp.dma_start(w3[:, e, :], A["L0_ffn_W3"][e]).then_inc(s["a_expw"], 16)
                    sp.dma_start(w2[:, e, :, :], A["L0_ffn_W2"][e].rearrange("(c p) d -> p c d", p=P)).then_inc(s["a_expw"], 16)
                with sp.Fori(part * (z1.shape[1] // Z1 // 4), (part + 1) * (z1.shape[1] // Z1 // 4)) as i:
                    sp.dma_start(z1[:, bass.ds(i * Z1, Z1), :], bc(filler[:], 1, [P, Z1, ROW])).then_inc(s["a_zeroed"], 16)
                with sp.Fori(part * (zy.shape[1] // ZY // 4), (part + 1) * (zy.shape[1] // ZY // 4)) as i:
                    sp.dma_start(zy[:, bass.ts(i, ZY)], zeros[:, 0:ZY]).then_inc(s["a_zeroed"], 16)

            def body(u):
                for half in range(2):
                    if live(u - 1, SUPERS):
                        for p, m in quads(u - 1, half):
                            sp.wait_ge(s["a_scattered"], freed(m, 2))
                            for j in range(QUAD):
                                tile = XN1v[:, bass.ds(m * QUAD + j, 1), :].to_broadcast([P, PICKS0, D])
                                sp.dma_start(rows[:, p, j, :, 0:D], tile).then_inc(staged[p], 16)
                    if live(u, SUPERS):
                        for p, n in quads(u, half):
                            sp.wait_ge(s["a_xn1"], made(n))
                            sp.dma_start(XN1v[:, bass.ds(n * QUAD, QUAD), :], xn1[:, p]).then_inc(store[p], 16)
                        for p in range(2):
                            sp.wait_ge(store[p], 16 * (2 * u + half + 1))
                            sp.sem_inc(s["a_stored"], 1)
            for part in range(4):
                background(part)
            supers(sp, body, after=1)
            sp.wait_ge(s["a_zeroed"], 16 * n_zero)
            sp.wait_ge(s["a_expw"], 48 * E0)
            sp.wait_ge(s["a_padded"], 1)
            with sp.Fori(0, E0) as e:
                at = sp.value_load(padded[0:1, bass.ds(e, 1)], min_val=0, max_val=SPARE0 - P)
                sp.dma_start(XS0[bass.ds(at, P), :], filler[:]).then_inc(s["a_filled"], 16)
            sp.wait_ge(s["a_filled"], 16 * E0)

        @blk.gpsimd
        def _(pool):
            for name in ("a_idx", "a_rstd", "a_rstd1", "a_hx", "a_scattered", "a_staged"):
                pool.sem_inc(s[name], SEED)
            nc.gpsimd.memset(zeros[:], 0.0).then_inc(s["a_zero"], 1)
            nc.gpsimd.memset(filler[:, 0:D + 1], 0.0)
            nc.gpsimd.memset(filler[:, D + 1:ROW], NOWHERE).then_inc(s["a_fillready"], 1)
            nc.gpsimd.memset(ident[:], 0.0)
            nc.gpsimd.memset(causal[:], 0.0)
            nc.gpsimd.memset(ones[:], 1.0)
            nc.gpsimd.memset(before[:], 1.0)
            nc.gpsimd.memset(fresh[:], 1.0)
            nc.gpsimd.memset(power[:], -0.5).then_inc(s["a_eye"], 1)
            pool.wait_ge(s["a_eye"], 1)
            nc.gpsimd.memset(fresh[:, :, 0:1], 0.0)
            nc.gpsimd.iota(carry[:], pattern=[[REGION0, E0]], base=0, channel_multiplier=0,
                           allow_small_or_imprecise_dtypes=True)
            nc.gpsimd.iota(region[:], pattern=[[REGION0, E0]], base=0, channel_multiplier=0,
                           allow_small_or_imprecise_dtypes=True)
            nc.gpsimd.iota(index[:], pattern=[[1, BLOCKS0]], base=0, channel_multiplier=0,
                           allow_small_or_imprecise_dtypes=True)
            nc.gpsimd.iota(dest[:], pattern=[[P * PICKS0, SUPER], [1, PICKS0]], base=0, channel_multiplier=PICKS0,
                           allow_small_or_imprecise_dtypes=True)
            nc.gpsimd.affine_select(out=ident[:], in_=ident[:], compare_op=ALU.not_equal, fill=1.0, base=0,
                                    pattern=[[-1, P]], channel_multiplier=1)
            nc.gpsimd.affine_select(out=causal[:], in_=causal[:], compare_op=ALU.is_ge, fill=MASKED, base=0,
                                    pattern=[[1, P]], channel_multiplier=-1)
            nc.gpsimd.affine_select(out=before[:], in_=before[:], compare_op=ALU.is_gt, fill=0.0, base=0,
                                    pattern=[[1, P]], channel_multiplier=-1).then_inc(s["a_const"], 1)
            pool.wait_ge(s["a_const"], 1)
            pool.wait_ge(s["a_xload"], 16)

            def fetch(n, p):
                pool.wait_ge(s["a_h1"], freed(n, 2))
                turn(pool, s["a_poolturn"])
                nc.gpsimd.tensor_copy(idx4[:, p, :], xidx[:, bass.ds(n * QUAD, QUAD)]).then_inc(s["a_idx"], 1)
                pool.wait_ge(s["a_idx"], made(n))
                turn(pool, s["a_poolturn"])
                for j in range(QUAD):
                    nc.gpsimd.indirect_dma_start(
                        out=h0[:, p, j, :], out_offset=None, in_=A["L0_tok_w"],
                        in_offset=bass.IndirectOffsetOnAxis(ap=idx4[:, p, j:j + 1], axis=0)).then_inc(gather[p], 16)

            def scatter(u, half, p):
                m, i = u * QUADS + 2 * half + p, 2 * half + p
                pool.wait_ge(s["r_slots"], made(u))
                pool.wait_ge(staged[p], 16 * QUAD * (2 * u + half + 1))
                turn(pool, s["a_poolturn"])
                nc.gpsimd.tensor_copy(rows[:, p, :, :, D:ROW], extra[:, i * QUAD:(i + 1) * QUAD])
                nc.gpsimd.tensor_copy(sidx[:, p], slot[:, i * QUAD:(i + 1) * QUAD, :]).then_inc(s["a_staged"], 1)
                pool.wait_ge(s["a_staged"], made(m))
                turn(pool, s["a_poolturn"])
                for j in range(QUAD):
                    for k in range(PICKS0):
                        nc.gpsimd.indirect_dma_start(
                            out=XS0, out_offset=bass.IndirectOffsetOnAxis(ap=sidx[:, p, j, k:k + 1], axis=0),
                            in_=rows[:, p, j, k, :], in_offset=None, bounds_check=ROWS0 - 1,
                            oob_is_err=False).then_inc(sent[p], 16)

            def body(u):
                before_it = not isinstance(u, int) or u > 0
                for half in range(2):
                    if live(u, SUPERS):
                        for p, n in quads(u, half):
                            fetch(n, p)
                    if before_it:
                        scatter(u - 1, half, 0)
                    if live(u, SUPERS):
                        for p, n in quads(u, half):
                            pool.wait_ge(s["a_ve"], made(n))
                            nc.gpsimd.tensor_tensor(rstd[:, p, :], ve[:, p, :], power[:], ALU.pow).then_inc(s["a_rstd"], 1)
                        for p, n in quads(u, half):
                            pool.wait_ge(s["a_xn"], made(n))
                            nc.gpsimd.tensor_tensor(h0[:, p], h0[:, p], xn[:, p], ALU.add).then_inc(s["a_hx"], 1)
                    if before_it:
                        scatter(u - 1, half, 1)
                    if live(u, SUPERS):
                        for p, n in quads(u, half):
                            pool.wait_ge(s["a_ve1"], made(n))
                            nc.gpsimd.tensor_tensor(rstd1[:, p, :], ve1[:, p, :], power[:], ALU.pow).then_inc(s["a_rstd1"], 1)
                    if before_it:
                        for p in range(2):
                            pool.wait_ge(sent[p], 16 * QUAD * PICKS0 * (2 * (u - 1) + half + 1))
                            pool.sem_inc(s["a_scattered"], 1)
            supers(pool, body, after=1)

        @blk.vector
        def _(dve):
            for name in ("a_stats a_mv a_ve a_xn a_v a_lm a_max a_rsum a_vs a_p2 a_h1 a_stats1 a_mv1 a_ve1 a_xn1 "
                         "a_logit r_max r_picks r_slots").split():
                dve.sem_inc(s[name], SEED)
            dve.wait_ge(s["a_load"], 16 * n_load)
            dve.wait_ge(s["a_const"], 1)

            def normalise(n, p, x_of, st, mv, ve, tag):
                turn(dve, s["a_turn"])
                for j in range(QUAD):
                    last = nc.vector.bn_stats(st[:, p, j, :], x_of(j))
                last.then_inc(s["a_stats" + tag], 1)
                dve.wait_ge(s["a_stats" + tag], made(n))
                turn(dve, s["a_turn"])
                for j in range(QUAD):
                    last = nc.vector.bn_aggr(mv[:, p, j, :], st[:, p, j, :])
                last.then_inc(s["a_mv" + tag], 1)
                dve.wait_ge(s["a_mv" + tag], made(n))
                nc.vector.tensor_scalar_add(ve[:, p, :], mv[:, p, :, 1], EPS).then_inc(s["a_ve" + tag], 1)

            def scale(n, p, x_of, mv, rstd, to, tag):
                dve.wait_ge(s["a_rstd" + tag], made(n))
                for j in range(QUAD):
                    last = nc.vector.tensor_scalar(to[:, p, j, :], x_of(j), mv[:, p, j, 0:1], rstd[:, p, j:j + 1],
                                                   ALU.subtract, ALU.mult)
                last.then_inc(s["a_xn" + tag], 1)

            def body(u):
                for half in range(2):
                    ns = [n for _, n in quads(u, half)]
                    for p, n in enumerate(ns):
                        dve.wait_ge(gather[p], 16 * QUAD * (2 * u + half + 1))
                        normalise(n, p, lambda j: h0[:, p, j, :], st, mv, ve, "")
                    for p, n in enumerate(ns):
                        dve.wait_ge(s["a_pT"], freed(n, 2))
                        scale(n, p, lambda j: h0[:, p, j, :], mv, rstd, xn, "")
                    for p, n in enumerate(ns):
                        dve.wait_ge(s["a_pV"], made(n))
                        nc.vector.tensor_tensor(v[:, p], pV[:].rearrange("p (j d) -> p j d", j=QUAD),
                                                bc(bv[:], 1, [P, QUAD, D]), ALU.add).then_inc(s["a_v"], 1)
                    for p, n in enumerate(ns):
                        dve.wait_ge(s["a_pL"], made(n))
                        nc.vector.tensor_tensor(lm[:, p], pL[:].rearrange("p (j t) -> p j t", j=QUAD),
                                                bc(causal[:], 1, [P, QUAD, P]), ALU.add).then_inc(s["a_lm"], 1)
                        dve.wait_ge(s["a_lm"], made(n))
                        nc.vector.tensor_reduce(nmx[:, p, :], lm[:, p], AX.X, ALU.max, negate=True).then_inc(s["a_max"], 1)
                    for p, n in enumerate(ns):
                        dve.wait_ge(s["a_prob"], made(n))
                        nc.vector.tensor_scalar_mul(psum[:, p, :], psum[:, p, :], float(np.sqrt(P))).then_inc(s["a_p2"], 1)
                        dve.wait_ge(s["a_p2"], made(n))
                        nc.vector.reciprocal(rsum[:, p, :], psum[:, p, :]).then_inc(s["a_rsum"], 1)
                        dve.wait_ge(s["a_rsum"], made(n))
                        dve.wait_ge(s["a_v"], made(n))
                        nc.vector.tensor_tensor(v[:, p], v[:, p], bc(rsum[:, p, :], 2, [P, QUAD, D]),
                                                ALU.mult).then_inc(s["a_vs"], 1)
                    for p, n in enumerate(ns):
                        dve.wait_ge(s["a_pR"], made(n))
                        dve.wait_ge(s["a_hx"], made(n))
                        nc.vector.tensor_tensor(H[:, bass.ds(n * QUAD, QUAD), :],
                                                pR[:].rearrange("p (j d) -> p j d", j=QUAD), h0[:, p],
                                                ALU.add).then_inc(s["a_h1"], 1)
                        dve.wait_ge(s["a_h1"], made(n))
                        normalise(n, p, lambda j: H[:, bass.ds(n * QUAD + j, 1), :].rearrange("p o d -> p (o d)"),
                                  st1, mv1, ve1, "1")
                    for p, n in enumerate(ns):
                        dve.wait_ge(s["a_stored"], freed(n, 2))
                        dve.wait_ge(s["a_pT1"], freed(n, 2))
                        scale(n, p, lambda j: H[:, bass.ds(n * QUAD + j, 1), :].rearrange("p o d -> p (o d)"),
                              mv1, rstd1, xn1, "1")
                    for p, n in enumerate(ns):
                        i = 2 * half + p
                        dve.wait_ge(s["a_pG"], made(n))
                        nc.vector.tensor_tensor(
                            logit[:, i * QUAD:(i + 1) * QUAD].rearrange("p i g e -> p i (g e)"),
                            pG[:, 0:QUAD * 20].rearrange("p (i c) -> p i c", i=QUAD),
                            bc(br[:].rearrange("p g e -> p (g e)"), 1, [P, QUAD, 20]), ALU.add).then_inc(s["a_logit"], 1)
                dve.wait_ge(s["a_logit"], made(u * QUADS + QUADS - 1))
                dve.wait_ge(s["a_staged"], made(u * QUADS - 1) if not isinstance(u, int) else SEED)
                route(u)

            def route(u):
                step = Chain(dve, s["r_dve"], u * ROUTE_STEPS)
                route_top2(dve, nc.vector, step, s, u, small, prob4, rank, first, second, work, pair, picks, logit, total,
                           row, fresh, carry, pC, slot, extra, dest)
                assert step.n == ROUTE_STEPS, step.n
            supers(dve, body)
            V = nc.vector
            step = Chain(dve, s["t_dve"])
            step(V.tensor_copy(padded[:], carry[0:1, :]))
            dve.sem_inc(s["a_padded"], 1)
            step(V.scalar_tensor_tensor(count_i[:], carry[:], float(P - 1), region[:], ALU.add, ALU.subtract))
            step(V.tensor_single_scalar(count_i[:], count_i[:], 7, ALU.arith_shift_right))
            step(V.tensor_copy(blocks[:], count_i[:]))
            step(V.memset(region[:], 1.0))
            step(V.tensor_tensor_scan(block_end[:], region[:], blocks[:], 0.0, ALU.mult, ALU.add))
            quarter = [1, BLOCKS0 // 4, E0]
            for c in range(4):
                part = slice(c * BLOCKS0 // 4, (c + 1) * BLOCKS0 // 4)
                step(V.tensor_tensor(reached[:], bc(index[:, part], 2, quarter), bc(block_end[0:1, :], 1, quarter), ALU.is_ge))
                step(V.tensor_reduce(expert_f[:, part], reached[:], AX.X, ALU.add))
                step(V.tensor_tensor(reached[:], reached[:], bc(blocks[0:1, :], 1, quarter), ALU.mult))
                step(V.tensor_reduce(passed[:, part], reached[:], AX.X, ALU.add))
            step(V.tensor_scalar(block_expert[:], expert_f[:], float(E0 - 1), None, ALU.min))
            step(V.tensor_tensor(index[:], index[:], passed[:], ALU.subtract))
            step(V.tensor_scalar_mul(index[:], index[:], float(P)))
            step(V.scalar_tensor_tensor(block_row[:], expert_f[:], float(REGION0), index[:], ALU.mult, ALU.add))

        @blk.tensor
        def _(pe):
            for name in "a_pT a_pQ a_pK a_pV a_pL a_pR a_pT1 a_pG r_counted".split():
                pe.sem_inc(s[name], SEED)
            pe.wait_ge(s["a_load"], 16 * n_load)
            pe.wait_ge(s["a_const"], 1)

            def body(u):
                for half in range(2):
                    ns = [n for _, n in quads(u, half)]
                    for p, n in enumerate(ns):
                        pe.wait_ge(s["a_xn"], made(n))
                        pe.wait_ge(s["a_xT"], freed(n, 1))
                        if p == 0:
                            pe.wait_ge(s["a_x1T"], freed(n, 1))
                        for j in range(QUAD):
                            last = nc.tensor.transpose(pT[:, bass.ts(j, P)], xn[:, p, j, :], ident[:])
                        last.then_inc(s["a_pT"], 1)
                    for p, n in enumerate(ns):
                        pe.wait_ge(s["a_xT"], made(n))
                        pe.wait_ge(s["a_qT"], freed(n, 1))
                        nc.tensor.matmul(pQ[:], wq[:], xT[:, p, :], start=True, stop=True).then_inc(s["a_pQ"], 1)
                        pe.wait_ge(s["a_kT"], freed(n, 1))
                        nc.tensor.matmul(pK[:], wk[:], xT[:, p, :], start=True, stop=True).then_inc(s["a_pK"], 1)
                        pe.wait_ge(s["a_v"], freed(n, 1))
                        for j in range(QUAD):
                            last = nc.tensor.matmul(pV[:, bass.ts(j, D)], xT[:, p, bass.ts(j, P)], wv[:], start=True, stop=True)
                        last.then_inc(s["a_pV"], 1)
                    for p, n in enumerate(ns):
                        pe.wait_ge(s["a_kT"], made(n))
                        pe.wait_ge(s["a_qT"], made(n))
                        pe.wait_ge(s["a_lm"], freed(n, 1))
                        for j in range(QUAD):
                            last = nc.tensor.matmul(pL[:, bass.ts(j, P)], kT[:, p, bass.ts(j, P)], qT[:, p, bass.ts(j, P)],
                                                    start=True, stop=True)
                        last.then_inc(s["a_pL"], 1)
                    for p, n in enumerate(ns):
                        pe.wait_ge(s["a_prob"], made(n))
                        pe.wait_ge(s["a_vs"], made(n))
                        pe.wait_ge(s["a_h1"], freed(n, 1))
                        for j in range(QUAD):
                            last = nc.tensor.matmul(pR[:, bass.ts(j, D)], lm[:, p, j, :], v[:, p, j, :],
                                                    start=True, stop=True)
                        last.then_inc(s["a_pR"], 1)
                    for p, n in enumerate(ns):
                        pe.wait_ge(s["a_xn1"], made(n))
                        if p == 0:
                            pe.wait_ge(s["a_xT"], made(n + 1))
                        pe.wait_ge(s["a_x1T"], freed(n, 1))
                        for j in range(QUAD):
                            last = nc.tensor.transpose(pT[:, bass.ts(j, P)], xn1[:, p, j, :], ident[:])
                        last.then_inc(s["a_pT1"], 1)
                    for p, n in enumerate(ns):
                        pe.wait_ge(s["a_x1T"], made(n))
                        pe.wait_ge(s["a_logit"], freed(n, 1))
                        for j in range(QUAD):
                            last = nc.tensor.matmul(pG[:, j * 20:j * 20 + 20], qT[:, p, bass.ts(j, P)],
                                                    wr[:].rearrange("p g e -> p (g e)"), start=True, stop=True)
                        last.then_inc(s["a_pG"], 1)
                pe.wait_ge(s["r_picks"], made(u))
                flat, n = picks[:].rearrange("p e i -> p (e i)"), E0 * SUPER
                nc.tensor.matmul(pC[:, 0:n], before[:], flat, start=True, stop=True)
                nc.tensor.matmul(pC[:, n:2 * n], ones[:], flat, start=True, stop=True).then_inc(s["r_counted"], 1)
            supers(pe, body)

        @blk.scalar
        def _(act):
            for name in "a_xT a_qT a_kT a_prob a_x1T r_exp".split():
                act.sem_inc(s[name], SEED)
            act.wait_ge(s["a_load"], 16 * n_load)
            act.wait_ge(s["a_zero"], 1)
            nc.scalar.activation(warm[:], zeros[:, 0:1], ACT.Exp)

            def body(u):
                for half in range(2):
                    ns = [n for _, n in quads(u, half)]
                    for p, n in enumerate(ns):
                        act.wait_ge(s["a_pT"], made(n))
                        act.wait_ge(s["a_pV"], freed(n, 2))
                        nc.scalar.copy(xT[:, p, :], pT[:]).then_inc(s["a_xT"], 1)
                    for p, n in enumerate(ns):
                        act.wait_ge(s["a_pG"], freed(n, 2))
                        act.wait_ge(s["a_pQ"], made(n))
                        nc.scalar.activation(qT[:, p, :], pQ[:], ACT.Identity, bias=bq[:, 0:1]).then_inc(s["a_qT"], 1)
                        act.wait_ge(s["a_pK"], made(n))
                        nc.scalar.activation(kT[:, p, :], pK[:], ACT.Identity, bias=bk[:, 0:1]).then_inc(s["a_kT"], 1)
                    for p, n in enumerate(ns):
                        act.wait_ge(s["a_max"], made(n))
                        for j in range(QUAD):
                            last = nc.scalar.activation(lm[:, p, j, :], lm[:, p, j, :], ACT.Exp, bias=nmx[:, p, j:j + 1],
                                                        accum_out=psum[:, p, j:j + 1])
                        last.then_inc(s["a_prob"], 1)
                    for p, n in enumerate(ns):
                        act.wait_ge(s["a_pT1"], made(n))
                        act.wait_ge(s["a_pL"], made(n))
                        nc.scalar.copy(qT[:, p, :], pT[:]).then_inc(s["a_x1T"], 1)
                act.wait_ge(s["r_max"], made(u))
                nc.scalar.activation(prob4[:], work[:], ACT.Exp).then_inc(s["r_exp"], 1)
            supers(act, body)


def layer0_experts(nc, sems, ps, ident, block_expert, block_row, w1, w3, w2, XS0, YT0):
    ctx = ExitStack()
    CH = HID // P
    RING = 4
    with ctx:
        def sb(name, shape, dt=F32):
            return ctx.enter_context(nc.sbuf_tensor(name, shape, dt))
        x = sb("e_x", [P, RING, ROW])
        xT = sb("e_xT", [P, 2, P])
        place = sb("e_place", [P, RING], I32)
        share = sb("e_share", [P, RING])
        gate = sb("e_gate_t", [P, 2, HID])
        g = sb("e_g_t", [P, 2, HID])
        gT = sb("e_gT_t", [P, 2, CH, P])
        y = sb("e_y_t", [P, 2, D])
        warm = sb("e_warm", [P, 1])
        s = sems("e_pT e_xT e_p1 e_p3 e_gate e_g e_pg e_gT e_py e_y e_tags e_sent e_turn",
                 dma="e_x0 e_x1 e_x2 e_x3 e_out0 e_out1")
        landed = [s[f"e_x{r}"] for r in range(RING)]
        out = [s["e_out0"], s["e_out1"]]
        pT, py = ps[0], ps[1]
        p1, p3, pg = [ps[2], ps[3]], [ps[4], ps[5]], [ps[6], ps[7]]
        blk = ctx.enter_context(nc.Block())

        @blk.sync
        def _(sp):
            def body(n, k, i):
                row = sp.value_load(block_row[0:1, bass.ds(n, 1)], min_val=0, max_val=ROWS0 - P)
                wait_free(sp, s["e_pT"], n, RING)
                wait_free(sp, s["e_tags"], n, RING)
                sp.dma_start(x[:, k, :], XS0[bass.ds(row, P), :]).then_inc(landed[k], 16)
            pipeline(sp, BLOCKS0, 0, 0, RING, body)

        @blk.gpsimd
        def _(pool):
            pool.sem_inc(s["e_sent"], SEED)

            def body(n, k, i):
                if live(n, BLOCKS0):
                    pool.wait_ge(s["e_y"], made(n))
                    turn(pool, s["e_turn"])
                    nc.gpsimd.indirect_dma_start(
                        out=YT0, out_offset=bass.IndirectOffsetOnAxis(ap=place[:, k:k + 1], axis=0), in_=y[:, k % 2, :],
                        in_offset=None, bounds_check=TOKENS * PICKS0 - 1, oob_is_err=False).then_inc(out[k % 2], 16)
                if live(n - 1, BLOCKS0):
                    pool.wait_ge(out[(k - 1) % 2], 16 * (2 * i + (k - 1) // 2 + 1))
                    pool.sem_inc(s["e_sent"], 1)
            pipeline(pool, BLOCKS0, 0, 1, RING, body)

        @blk.tensor
        def _(pe):
            for name in "e_pT e_p1 e_p3 e_pg e_py".split():
                pe.sem_inc(s[name], SEED)

            def body(n, k, i):
                if live(n, BLOCKS0):
                    p = k % 2
                    expert = pe.value_load(block_expert[0:1, bass.ds(n, 1)], min_val=0, max_val=E0 - 1)
                    pe.wait_ge(s["e_xT"], made(n))
                    pe.wait_ge(s["e_gate"], freed(n, 2))
                    nc.tensor.matmul(p1[p][:], xT[:, p, :], w1[:, bass.ds(expert, 1), :].rearrange("p o h -> p (o h)"),
                                     start=True, stop=True).then_inc(s["e_p1"], 1)
                    pe.wait_ge(s["e_g"], freed(n, 2))
                    nc.tensor.matmul(p3[p][:], xT[:, p, :], w3[:, bass.ds(expert, 1), :].rearrange("p o h -> p (o h)"),
                                     start=True, stop=True).then_inc(s["e_p3"], 1)
                if live(n - 1, BLOCKS0):
                    m, p = n - 1, (k - 1) % 2
                    pe.wait_ge(s["e_g"], made(m))
                    pe.wait_ge(s["e_gT"], freed(m, 2))
                    for c in range(CH):
                        last = nc.tensor.transpose(pg[p][:, bass.ts(c, P)], g[:, p, bass.ts(c, P)], ident[:])
                    last.then_inc(s["e_pg"], 1)
                if live(n + 1, BLOCKS0):
                    m, r = n + 1, (k + 1) % RING
                    pe.wait_ge(landed[r], 16 * (i + (k + 1) // RING + 1))
                    pe.wait_ge(s["e_xT"], freed(m, 1))
                    nc.tensor.transpose(pT[:, 0:P], x[:, r, 0:D], ident[:]).then_inc(s["e_pT"], 1)
                if live(n - 2, BLOCKS0):
                    m, p = n - 2, k % 2
                    expert = pe.value_load(block_expert[0:1, bass.ds(m, 1)], min_val=0, max_val=E0 - 1)
                    pe.wait_ge(s["e_gT"], made(m))
                    pe.wait_ge(s["e_y"], freed(m, 1))
                    for c in range(CH):
                        last = nc.tensor.matmul(
                            py[:, 0:D], gT[:, p, c, :], w2[:, bass.ds(expert, 1), c, :].rearrange("p o d -> p (o d)"),
                            start=(c == 0), stop=(c == CH - 1))
                    last.then_inc(s["e_py"], 1)
            pipeline(pe, BLOCKS0, 1, 2, RING, body)

        @blk.scalar
        def _(act):
            for name in "e_xT e_gate e_gT".split():
                act.sem_inc(s[name], SEED)
            nc.scalar.activation(warm[:], ident[:, 0:1], ACT.Silu)

            def body(n, k, i):
                if live(n, BLOCKS0):
                    p = k % 2
                    act.wait_ge(s["e_p1"], made(n))
                    act.wait_ge(s["e_g"], freed(n, 2))
                    nc.scalar.activation(gate[:, p, :], p1[p][:], ACT.Silu).then_inc(s["e_gate"], 1)
                if live(n - 1, BLOCKS0):
                    m, p = n - 1, (k - 1) % 2
                    act.wait_ge(s["e_pg"], made(m))
                    act.wait_ge(s["e_py"], freed(m, 2))
                    nc.scalar.copy(gT[:, p].rearrange("p c t -> p (c t)"), pg[p][:]).then_inc(s["e_gT"], 1)
                if live(n + 1, BLOCKS0):
                    m, p = n + 1, (k + 1) % 2
                    act.wait_ge(s["e_pT"], made(m))
                    act.wait_ge(s["e_p3"], freed(m, 2))
                    nc.scalar.copy(xT[:, p, :], pT[:, 0:P]).then_inc(s["e_xT"], 1)
            pipeline(act, BLOCKS0, 1, 2, RING, body)

        @blk.vector
        def _(dve):
            for name in "e_g e_y e_tags".split():
                dve.sem_inc(s[name], SEED)

            def body(n, k, i):
                if live(n, BLOCKS0):
                    p = k % 2
                    dve.wait_ge(s["e_gate"], made(n))
                    dve.wait_ge(s["e_p3"], made(n))
                    dve.wait_ge(s["e_pg"], freed(n, 2))
                    nc.vector.tensor_tensor(g[:, p, :], gate[:, p, :], p3[p][:], ALU.mult).then_inc(s["e_g"], 1)
                if live(n - 1, BLOCKS0):
                    m, r = n - 1, (k - 1) % RING
                    dve.wait_ge(landed[r], 16 * (i + (k - 1) // RING + 1))
                    wait_free(dve, s["e_sent"], m, RING)
                    wait_free(dve, s["e_y"], m, RING)
                    nc.vector.tensor_copy(share[:, r:r + 1], x[:, r, D:D + 1])
                    nc.vector.tensor_copy(place[:, r:r + 1], x[:, r, D + 1:ROW]).then_inc(s["e_tags"], 1)
                if live(n - 2, BLOCKS0):
                    m, p, r = n - 2, k % 2, (k - 2) % RING
                    dve.wait_ge(s["e_py"], made(m))
                    dve.wait_ge(s["e_tags"], made(m))
                    dve.wait_ge(s["e_sent"], freed(m, 2))
                    nc.vector.tensor_scalar(y[:, p, :], py[:, 0:D], share[:, r:r + 1], None, ALU.mult).then_inc(s["e_y"], 1)
            pipeline(dve, BLOCKS0, 0, 2, RING, body)


def layer0_combine(nc, A, sems, ps, H, ident, wnT, YT0, BD):
    ctx = ExitStack()
    with ctx:
        def sb(name, shape, dt=F32):
            return ctx.enter_context(nc.sbuf_tensor(name, shape, dt))
        power = sb("d_power", [P, QUAD])
        gamma, beta, rbias = sb("d_gamma", [P, 1]), sb("d_beta", [P, 1]), sb("d_rbias", [P, 1])
        wq, wr = sb("d_wq", [P, D]), sb("d_wr", [P, D])
        angles = sb("d_angles", [P, TILES])
        headmask = sb("d_headmask", [P, HEADS])
        rk = sb("d_rk", [P, TILES])
        window = sb("d_window", [P, 2, HEADS, 2 * TILES])
        got = sb("d_got", [P, 2, QUAD, PICKS0, D])
        acc = sb("d_acc", [P, 2, QUAD, D])
        st, mv, ve, rstd = (sb("d_st", [P, 2, QUAD, 6]), sb("d_mv", [P, 2, QUAD, 2]), sb("d_ve", [P, 2, QUAD]),
                            sb("d_rstd", [P, 2, QUAD]))
        st2, mv2, ve2, rstd2 = (sb("d_st2", [P, 2, QUAD, 6]), sb("d_mv2", [P, 2, QUAD, 2]),
                                sb("d_ve2", [P, 2, QUAD]), sb("d_rstd2", [P, 2, QUAD]))
        w = sb("d_w", [P, 2, QUAD, D])
        wn = sb("d_wn", [P, 2, QUAD, D])
        wT = sb("d_wT", [P, 2, QUAD, P])
        q = sb("d_q", [P, 2, QUAD, P])
        pos = sb("d_pos", [P, 2, HEADS * TILES])
        s = sems("d_const d_const2 d_rk d_rks d_window d_two d_acc d_acck d_st d_mv d_ve d_rstd d_w d_st2 "
                 "d_mv2 d_ve2 d_rstd2 d_wn d_pT d_wT d_wnT d_h d_pQ d_q d_pB d_pos d_kept d_turn d_poolturn "
                 "d_peturn",
                 dma="d_load d_got0 d_got1 d_out0 d_out1")
        Y = YT0.rearrange("(i t k) d -> t i (k d)", t=P, k=PICKS0)
        got_in, kept = [s["d_got0"], s["d_got1"]], [s["d_out0"], s["d_out1"]]
        pT, pQ, pB, pR = ps[0], ps[1], [ps[2], ps[3]], ps[4]
        n_load = 6
        blk = ctx.enter_context(nc.Block())

        @blk.sync
        def _(sp):
            for dst, src in ((gamma[:], A["L1_attn_ln_gamma"].unsqueeze(1)), (beta[:], A["L1_attn_ln_beta"].unsqueeze(1)),
                             (rbias[:], A["L1_attn_r_r_bias"].rearrange("n (d o) -> (n d) o", o=1)),
                             (wq[:], A["L1_attn_Wqkv"][:, 0:D]), (wr[:], A["L1_attn_Wr"]), (angles[:], A["positions"])):
                sp.dma_start(dst, src).then_inc(s["d_load"], 16)
            sp.sem_inc(s["d_kept"], SEED)

            def load(n, p):
                sp.dma_start(got[:, p].rearrange("t i k d -> t i (k d)"), Y[:, bass.ds(n * QUAD, QUAD), :]).then_inc(got_in[p], 16)

            def store(i):
                for m in range(2 * QUAD):
                    p = m % 2
                    sp.wait_ge(s["d_pos"], made(2 * QUAD * i + m))
                    sp.dma_start(BD[:, bass.ds(2 * QUAD * i + m, 1), :].rearrange("b o c -> b (o c)"),
                                 pos[:, p, :]).then_inc(kept[p], 16)
                    if m % 2:
                        for q_ in range(2):
                            sp.wait_ge(kept[q_], 16 * (QUAD * i + m // 2 + 1))
                            sp.sem_inc(s["d_kept"], 1)
            for p in range(2):
                load(p, p)
            with sp.Fori(0, PAIRS_OF_QUADS - 1) as i:
                for p in range(2):
                    sp.wait_ge(s["d_acc"], made(2 * i + p))
                    load(2 * i + 2 + p, p)
                store(i)
            store(PAIRS_OF_QUADS - 1)
            sp.wait_ge(s["d_pos"], made(TILES))
            sp.dma_start(BD[:, TILES, :], pos[:, 0, :]).then_inc(kept[0], 16)
            sp.wait_ge(kept[0], 16 * (TILES // 2 + 1))

        @blk.gpsimd
        def _(pool):
            for name in "d_two d_rstd d_rstd2 d_h d_wnT".split():
                pool.sem_inc(s[name], SEED)
            nc.gpsimd.memset(power[:], -0.5)
            nc.gpsimd.memset(window[:], 0.0)
            nc.gpsimd.memset(q[:], 0.0)
            nc.gpsimd.memset(headmask[:], 1.0).then_inc(s["d_const"], 1)
            pool.wait_ge(s["d_const"], 1)
            nc.gpsimd.affine_select(out=headmask[:], in_=headmask[:], compare_op=ALU.is_ge, fill=0.0, base=0,
                                    pattern=[[-DH, HEADS]], channel_multiplier=1).then_inc(s["d_const"], 1)
            pool.wait_ge(s["d_const"], 2)
            nc.gpsimd.affine_select(out=headmask[:], in_=headmask[:], compare_op=ALU.is_ge, fill=0.0, base=DH - 1,
                                    pattern=[[DH, HEADS]], channel_multiplier=-1).then_inc(s["d_const"], 1)
            with pool.Fori(0, PAIRS_OF_QUADS) as i:
                ns = [2 * i, 2 * i + 1]
                for p, n in enumerate(ns):
                    pool.wait_ge(got_in[p], 16 * (i + 1))
                    nc.gpsimd.tensor_tensor(got[:, p, :, 0:2, :], got[:, p, :, 0:2, :], got[:, p, :, 2:4, :],
                                            ALU.add).then_inc(s["d_two"], 1)
                for p, n in enumerate(ns):
                    pool.wait_ge(s["d_ve"], made(n))
                    nc.gpsimd.tensor_tensor(rstd[:, p, :], ve[:, p, :], power[:], ALU.pow).then_inc(s["d_rstd"], 1)
                for p, n in enumerate(ns):
                    pool.wait_ge(s["d_w"], made(n))
                    turn(pool, s["d_poolturn"])
                    nc.gpsimd.tensor_tensor(H[:, bass.ds(n * QUAD, QUAD), :], acc[:, p], w[:, p],
                                            ALU.add).then_inc(s["d_h"], 1)
                for p, n in enumerate(ns):
                    pool.wait_ge(s["d_ve2"], made(n))
                    nc.gpsimd.tensor_tensor(rstd2[:, p, :], ve2[:, p, :], power[:], ALU.pow).then_inc(s["d_rstd2"], 1)
                for p, n in enumerate(ns):
                    pool.wait_ge(s["d_wT"], made(n))
                    turn(pool, s["d_poolturn"])
                    nc.gpsimd.tensor_copy(wnT[:, :, bass.ds(n * QUAD, QUAD)],
                                          wT[:, p].rearrange("d i b -> d b i")).then_inc(s["d_wnT"], 1)

        @blk.vector
        def _(dve):
            for name in "d_acc d_acck d_st d_mv d_ve d_w d_st2 d_mv2 d_ve2 d_wn d_pos".split():
                dve.sem_inc(s[name], SEED)
            dve.wait_ge(s["d_const"], 3)
            dve.wait_ge(s["d_rk"], 1)
            nc.vector.tensor_copy(rk[:], pR[:, 0:TILES]).then_inc(s["d_rks"], 1)
            dve.wait_ge(s["d_rks"], 1)
            for k, at in ((0, 0), (1, TILES + 1)):
                width = min(TILES, 2 * TILES - at)
                nc.vector.tensor_tensor(window[:, k, :, at:at + width], bc(rk[:, 0:width], 1, [P, HEADS, width]),
                                        bc(headmask[:], 2, [P, HEADS, width]), ALU.mult).then_inc(s["d_window"], 1)

            def stats(n, p, x, st, mv, ve, tag):
                turn(dve, s["d_turn"])
                for j in range(QUAD):
                    last = nc.vector.bn_stats(st[:, p, j, :], x[:, p, j, :])
                last.then_inc(s["d_st" + tag], 1)
                dve.wait_ge(s["d_st" + tag], made(n))
                turn(dve, s["d_turn"])
                for j in range(QUAD):
                    last = nc.vector.bn_aggr(mv[:, p, j, :], st[:, p, j, :])
                last.then_inc(s["d_mv" + tag], 1)
                dve.wait_ge(s["d_mv" + tag], made(n))
                nc.vector.tensor_scalar_add(ve[:, p, :], mv[:, p, :, 1], EPS).then_inc(s["d_ve" + tag], 1)

            with dve.Fori(0, PAIRS_OF_QUADS) as i:
                ns = [2 * i, 2 * i + 1]
                for p, n in enumerate(ns):
                    dve.wait_ge(s["d_h"], freed(n, 2))
                    dve.wait_ge(s["d_two"], made(n))
                    nc.vector.tensor_tensor(acc[:, p], got[:, p, :, 0, :], got[:, p, :, 1, :], ALU.add).then_inc(s["d_acck"], 1)
                    dve.wait_ge(s["d_acck"], made(n))
                    nc.vector.tensor_tensor(acc[:, p], acc[:, p], H[:, bass.ds(n * QUAD, QUAD), :], ALU.add).then_inc(s["d_acc"], 1)
                    dve.wait_ge(s["d_acc"], made(n))
                    stats(n, p, acc, st, mv, ve, "")
                for p, n in enumerate(ns):
                    dve.wait_ge(s["d_rstd"], made(n))
                    for j in range(QUAD):
                        last = nc.vector.tensor_scalar(w[:, p, j, :], acc[:, p, j, :], mv[:, p, j, 0:1], rstd[:, p, j:j + 1],
                                                       ALU.subtract, ALU.mult)
                    last.then_inc(s["d_w"], 1)
                    dve.wait_ge(s["d_w"], made(n))
                    stats(n, p, w, st2, mv2, ve2, "2")
                for p, n in enumerate(ns):
                    dve.wait_ge(s["d_rstd2"], made(n))
                    dve.wait_ge(s["d_pT"], freed(n, 2))
                    for j in range(QUAD):
                        last = nc.vector.tensor_scalar(wn[:, p, j, :], w[:, p, j, :], mv2[:, p, j, 0:1], rstd2[:, p, j:j + 1],
                                                       ALU.subtract, ALU.mult)
                    last.then_inc(s["d_wn"], 1)
                for p, n in enumerate(ns):
                    for j in range(QUAD):
                        m = n * QUAD + j
                        dve.wait_ge(s["d_pB"], made(m))
                        dve.wait_ge(s["d_kept"], freed(m, 2))
                        nc.vector.tensor_copy(pos[:, j % 2, :], pB[j % 2][:]).then_inc(s["d_pos"], 1)
            dve.wait_ge(s["d_pB"], made(TILES))
            dve.wait_ge(s["d_kept"], freed(TILES, 2))
            nc.vector.tensor_copy(pos[:, 0, :], pB[0][:]).then_inc(s["d_pos"], 1)

        @blk.tensor
        def _(pe):
            for name in "d_pT d_pQ d_pB".split():
                pe.sem_inc(s[name], SEED)
            pe.wait_ge(s["d_load"], 16 * n_load)
            nc.tensor.matmul(pR[:, 0:TILES], wr[:], angles[:], start=True, stop=True).then_inc(s["d_rk"], 1)
            pe.wait_ge(s["d_window"], 2)
            with pe.Fori(0, PAIRS_OF_QUADS) as i:
                ns = [2 * i, 2 * i + 1]
                for p, n in enumerate(ns):
                    pe.wait_ge(s["d_wn"], made(n))
                    pe.wait_ge(s["d_wT"], freed(n, 1))
                    for j in range(QUAD):
                        last = nc.tensor.transpose(pT[:, bass.ts(j, P)], wn[:, p, j, :], ident[:])
                    last.then_inc(s["d_pT"], 1)
                for p, n in enumerate(ns):
                    pe.wait_ge(s["d_wT"], made(n))
                    pe.wait_ge(s["d_q"], freed(n, 1))
                    nc.tensor.matmul(pQ[:], wq[:], wT[:, p].rearrange("d i b -> d (i b)"),
                                     start=True, stop=True).then_inc(s["d_pQ"], 1)
                for p, n in enumerate(ns):
                    pe.wait_ge(s["d_q"], made(n))
                    for j in range(QUAD):
                        m = n * QUAD + j
                        pe.wait_ge(s["d_pos"], freed(m, 2))
                        turn(pe, s["d_peturn"])
                        prev = q[:, p, j - 1, :] if j else q[:, 1 - p, QUAD - 1, :]
                        nc.tensor.matmul(pB[j % 2][:], prev, window[:, 0, :, bass.ds(TILES - m, TILES)],
                                         start=True, stop=False)
                        nc.tensor.matmul(pB[j % 2][:], q[:, p, j, :], window[:, 1, :, bass.ds(TILES - m, TILES)],
                                         start=False, stop=True).then_inc(s["d_pB"], 1)
            pe.wait_ge(s["d_pos"], freed(TILES, 2))
            nc.tensor.matmul(pB[0][:], q[:, 1, QUAD - 1, :], window[:, 0, :, 0:TILES],
                             start=True, stop=True).then_inc(s["d_pB"], 1)

        @blk.scalar
        def _(act):
            for name in "d_wT d_q".split():
                act.sem_inc(s[name], SEED)
            act.wait_ge(s["d_load"], 16 * n_load)
            act.wait_ge(s["d_const"], 3)
            with act.Fori(0, PAIRS_OF_QUADS) as i:
                ns = [2 * i, 2 * i + 1]
                for p, n in enumerate(ns):
                    act.wait_ge(s["d_pT"], made(n))
                    act.wait_ge(s["d_pQ"], freed(n, 2))
                    act.wait_ge(s["d_wnT"], freed(n, 2))
                    nc.scalar.activation(wT[:, p].rearrange("d i b -> d (i b)"), pT[:], ACT.Identity, bias=beta[:, 0:1],
                                         scale=gamma[:, 0:1]).then_inc(s["d_wT"], 1)
                for p, n in enumerate(ns):
                    act.wait_ge(s["d_pQ"], made(n))
                    if p:
                        act.wait_ge(s["d_pB"], made(2 * i * QUAD))
                    nc.scalar.activation(q[:, p].rearrange("d i b -> d (i b)"), pQ[:], ACT.Identity,
                                         bias=rbias[:, 0:1]).then_inc(s["d_q"], 1)


def layer1_attention(nc, A, sems, ps, ident, wnT, readT, BD):
    ctx = ExitStack()
    OCT = 8
    with ctx:
        def sb(name, shape, dt=F32):
            return ctx.enter_context(nc.sbuf_tensor(name, shape, dt))
        wq, wk, wv = sb("f_wq", [P, D]), sb("f_wk", [P, D]), sb("f_wv", [P, D])
        wbias = sb("f_wbias", [P, 1])
        headmask = sb("f_headmask", [P, HEADS])
        halfmask = sb("f_halfmask", [P, 2])
        q = sb("f_q", [P, OCT, TILES])
        kk = sb("f_k", [P, OCT, TILES])
        x = sb("f_x", [P, OCT, 2, TILES])
        kh = sb("f_kh", [P, 2, 2, HEADS, TILES])
        vh = sb("f_vh", [P, 2, 2, HEADS // 2, 2, DH])
        bd = sb("f_bd", [P, 2, HEADS, TILES])
        S = sb("f_S", [P, 2, HEADS, TILES])
        mx = sb("f_mx", [P, 2, HEADS])
        E = sb("f_E", [P, 2, HEADS, TILES])
        den = sb("f_den", [P, 2, HEADS])
        rden = sb("f_rden", [P, 2, HEADS])
        ET = sb("f_ET", [P, 2, HEADS // 2, P])
        O = sb("f_O", [P, 2, D])
        s = sems("f_const f_pQ f_pK f_q f_k f_x f_kh f_pV f_vh f_pS f_S f_mx f_sub f_E f_den f_rden f_pE "
                 "f_ET f_pO f_O f_pOT f_read f_turn f_poolturn",
                 dma="f_load f_bd0 f_bd1")
        bd_in = [s["f_bd0"], s["f_bd1"]]
        pQ, pK, pV, pS, pE, pO = ps[0], ps[1], ps[2], [ps[3], ps[4]], ps[5], ps[6]
        pOT = ps[7]
        n_load = 4
        GROUPS = P // OCT
        PAIRS = OCT // 2
        blk = ctx.enter_context(nc.Block())

        @blk.sync
        def _(sp):
            for dst, src in ((wq[:], A["L1_attn_Wqkv"][:, 0:D]), (wk[:], A["L1_attn_Wqkv"][:, D:2 * D]),
                             (wv[:], A["L1_attn_Wqkv"][:, 2 * D:3 * D]),
                             (wbias[:], A["L1_attn_r_w_bias"].rearrange("n (d o) -> (n d) o", o=1))):
                sp.dma_start(dst, src).then_inc(s["f_load"], 16)
            with sp.Fori(0, GROUPS) as g:
                for r in range(PAIRS):
                    m, p = PAIRS * g + r, r % 2
                    sp.wait_ge(s["f_S"], freed(m, 2))
                    for h in range(2):
                        sp.dma_start(bd[h * TILES:(h + 1) * TILES, p].rearrange("i n j -> i (n j)"),
                                     BD[bass.ds(2 * m + h, 1), 1:, :].rearrange("o i c -> (o i) c")).then_inc(bd_in[p], 16)

        @blk.gpsimd
        def _(pool):
            for name in "f_kh f_sub".split():
                pool.sem_inc(s[name], SEED)
            nc.gpsimd.memset(headmask[:], 1.0)
            nc.gpsimd.memset(halfmask[:], 1.0).then_inc(s["f_const"], 1)
            pool.wait_ge(s["f_const"], 1)
            nc.gpsimd.affine_select(out=headmask[:], in_=headmask[:], compare_op=ALU.is_ge, fill=0.0, base=0,
                                    pattern=[[-DH, HEADS]], channel_multiplier=1)
            nc.gpsimd.affine_select(out=halfmask[:], in_=halfmask[:], compare_op=ALU.is_ge, fill=0.0, base=0,
                                    pattern=[[-TILES, 2]], channel_multiplier=1).then_inc(s["f_const"], 1)
            pool.wait_ge(s["f_const"], 2)
            nc.gpsimd.affine_select(out=headmask[:], in_=headmask[:], compare_op=ALU.is_ge, fill=0.0, base=DH - 1,
                                    pattern=[[DH, HEADS]], channel_multiplier=-1)
            nc.gpsimd.affine_select(out=halfmask[:], in_=halfmask[:], compare_op=ALU.is_ge, fill=0.0, base=TILES - 1,
                                    pattern=[[TILES, 2]], channel_multiplier=-1).then_inc(s["f_const"], 1)
            pool.wait_ge(s["f_const"], 3)
            with pool.Fori(0, GROUPS) as g:
                for r0 in range(0, PAIRS, 2):
                    for r in (r0, r0 + 1):
                        m, p = PAIRS * g + r, r % 2
                        if r == 0:
                            pool.wait_ge(s["f_k"], made(g))
                        pool.wait_ge(s["f_pS"], freed(m, 2))
                        for h in range(2):
                            last = nc.gpsimd.tensor_tensor(kh[:, p, h], bc(kk[:, 2 * r + h, :], 1, [P, HEADS, TILES]),
                                                           bc(headmask[:], 2, [P, HEADS, TILES]), ALU.mult)
                        last.then_inc(s["f_kh"], 1)
                    for r in (r0, r0 + 1):
                        m, p = PAIRS * g + r, r % 2
                        pool.wait_ge(s["f_mx"], made(m))
                        nc.gpsimd.tensor_tensor(S[:, p], S[:, p], bc(mx[:, p, :], 2, [P, HEADS, TILES]),
                                                ALU.subtract).then_inc(s["f_sub"], 1)

        @blk.scalar
        def _(act):
            for name in "f_q f_k f_x f_E f_ET".split():
                act.sem_inc(s[name], SEED)
            act.wait_ge(s["f_load"], 16 * n_load)
            act.wait_ge(s["f_const"], 3)
            nc.scalar.activation(E[:, 0, 0, 0:1], ident[:, 0:1], ACT.Exp)
            with act.Fori(0, GROUPS) as g:
                act.wait_ge(s["f_pV"], freed(2 * g, 1))
                cols = wnT[:, bass.ds(g * OCT, OCT), :]
                nc.scalar.copy(x[:, :, 0, :], cols)
                nc.scalar.copy(x[:, :, 1, :], cols).then_inc(s["f_x"], 1)
                act.wait_ge(s["f_pQ"], made(g))
                act.wait_ge(s["f_pS"], freed(PAIRS * g, 1))
                nc.scalar.activation(q[:].rearrange("d b i -> d (b i)"), pQ[:], ACT.Identity,
                                     bias=wbias[:, 0:1]).then_inc(s["f_q"], 1)
                act.wait_ge(s["f_pK"], made(g))
                act.wait_ge(s["f_kh"], freed(PAIRS * g, 1))
                nc.scalar.copy(kk[:].rearrange("d b i -> d (b i)"), pK[:]).then_inc(s["f_k"], 1)
                for r0 in range(0, PAIRS, 2):
                    for r in (r0, r0 + 1):
                        m, p = PAIRS * g + r, r % 2
                        act.wait_ge(s["f_sub"], made(m))
                        act.wait_ge(s["f_pE"], freed(m, 2))
                        act.wait_ge(s["f_den"], freed(m, 2))
                        nc.scalar.activation(E[:, p], S[:, p], ACT.Exp, scale=DH ** -0.5).then_inc(s["f_E"], 1)
                    for r in (r0, r0 + 1):
                        m, p = PAIRS * g + r, r % 2
                        act.wait_ge(s["f_pE"], made(m))
                        act.wait_ge(s["f_pO"], freed(m, 2))
                        nc.scalar.copy(ET[:, p].rearrange("p c t -> p (c t)"), pE[:]).then_inc(s["f_ET"], 1)

        @blk.vector
        def _(dve):
            for name in "f_vh f_S f_mx f_den f_rden f_O f_read".split():
                dve.sem_inc(s[name], SEED)
            dve.wait_ge(s["f_const"], 3)
            with dve.Fori(0, GROUPS) as g:
                for r0 in range(0, PAIRS, 2):
                    for r in (r0, r0 + 1):
                        m, p = PAIRS * g + r, r % 2
                        dve.wait_ge(s["f_pV"], made(m))
                        dve.wait_ge(s["f_pO"], freed(m, 2))
                        nc.vector.tensor_tensor(vh[:, p].rearrange("p b c h d -> p (b c) h d"),
                                                pV[:, 0:2 * D].rearrange("p (c h d) -> p c h d", h=2, d=DH),
                                                halfmask[:].unsqueeze(1).unsqueeze(3).to_broadcast([P, HEADS, 2, DH]),
                                                ALU.mult).then_inc(s["f_vh"], 1)
                    for r in (r0, r0 + 1):
                        m, p = PAIRS * g + r, r % 2
                        dve.wait_ge(s["f_pS"], made(m))
                        dve.wait_ge(bd_in[p], 32 * (PAIRS // 2 * g + r // 2 + 1))
                        dve.wait_ge(s["f_E"], freed(m, 2))
                        nc.vector.tensor_tensor(S[:, p].rearrange("p n j -> p (n j)"), pS[p][:],
                                                bd[:, p].rearrange("p n j -> p (n j)"), ALU.add).then_inc(s["f_S"], 1)
                        dve.wait_ge(s["f_S"], made(m))
                        dve.wait_ge(s["f_sub"], freed(m, 2))
                        nc.vector.tensor_reduce(mx[:, p, :], S[:, p], AX.X, ALU.max).then_inc(s["f_mx"], 1)
                    for r in (r0, r0 + 1):
                        m, p = PAIRS * g + r, r % 2
                        dve.wait_ge(s["f_E"], made(m))
                        nc.vector.tensor_reduce(den[:, p, :], E[:, p], AX.X, ALU.add).then_inc(s["f_den"], 1)
                        dve.wait_ge(s["f_den"], made(m))
                        nc.vector.reciprocal(rden[:, p, :], den[:, p, :]).then_inc(s["f_rden"], 1)
                    for r in (r0, r0 + 1):
                        m, p = PAIRS * g + r, r % 2
                        dve.wait_ge(s["f_pO"], made(m))
                        dve.wait_ge(s["f_pOT"], freed(m, 2))
                        dve.wait_ge(s["f_rden"], made(m))
                        nc.vector.tensor_tensor(O[:, p].rearrange("p (n d) -> p n d", n=HEADS),
                                                pO[:, 0:D].rearrange("p (n d) -> p n d", n=HEADS),
                                                bc(rden[:, p, :], 2, [P, HEADS, DH]), ALU.mult).then_inc(s["f_O"], 1)
                    for r in (r0, r0 + 1):
                        m, p = PAIRS * g + r, r % 2
                        dve.wait_ge(s["f_pOT"], made(m))
                        nc.vector.tensor_copy(readT[:, bass.ds(2 * m, 2), :].rearrange("p b i -> p (b i)"),
                                              pOT[:, 0:P]).then_inc(s["f_read"], 1)

        @blk.tensor
        def _(pe):
            for name in "f_pQ f_pK f_pV f_pS f_pE f_pO f_pOT".split():
                pe.sem_inc(s[name], SEED)
            pe.wait_ge(s["f_load"], 16 * n_load)
            with pe.Fori(0, GROUPS) as g:
                cols = wnT[:, bass.ds(g * OCT, OCT), :].rearrange("d b i -> d (b i)")
                pe.wait_ge(s["f_q"], freed(g, 1))
                nc.tensor.matmul(pQ[:], wq[:], cols, start=True, stop=True).then_inc(s["f_pQ"], 1)
                pe.wait_ge(s["f_k"], freed(g, 1))
                nc.tensor.matmul(pK[:], wk[:], cols, start=True, stop=True).then_inc(s["f_pK"], 1)
                for r0 in range(0, PAIRS, 2):
                    for r in (r0, r0 + 1):
                        m, p = PAIRS * g + r, r % 2
                        pe.wait_ge(s["f_x"], made(g))
                        pe.wait_ge(s["f_vh"], freed(m, 1))
                        for h in range(2):
                            last = nc.tensor.matmul(pV[:, h * D:(h + 1) * D], x[:, 2 * r + h].rearrange("d a i -> d (a i)"),
                                                    wv[:], start=True, stop=True)
                        last.then_inc(s["f_pV"], 1)
                    for r in (r0, r0 + 1):
                        m, p = PAIRS * g + r, r % 2
                        pe.wait_ge(s["f_q"], made(g))
                        pe.wait_ge(s["f_kh"], made(m))
                        pe.wait_ge(s["f_S"], freed(m, 2))
                        for h in range(2):
                            last = nc.tensor.matmul(pS[p][h * TILES:(h + 1) * TILES, :], q[:, 2 * r + h, :],
                                                    kh[:, p, h].rearrange("d n j -> d (n j)"), start=True, stop=True)
                        last.then_inc(s["f_pS"], 1)
                    for r in (r0, r0 + 1):
                        m, p = PAIRS * g + r, r % 2
                        pe.wait_ge(s["f_E"], made(m))
                        pe.wait_ge(s["f_ET"], freed(m, 1))
                        for c in range(HEADS // 2):
                            last = nc.tensor.transpose(pE[:, bass.ts(c, P)],
                                                       E[:, p, 2 * c:2 * c + 2, :].rearrange("p n j -> p (n j)"), ident[:])
                        last.then_inc(s["f_pE"], 1)
                    for r in (r0, r0 + 1):
                        m, p = PAIRS * g + r, r % 2
                        pe.wait_ge(s["f_ET"], made(m))
                        pe.wait_ge(s["f_vh"], made(m))
                        pe.wait_ge(s["f_O"], freed(m, 1))
                        for h in range(2):
                            for c in range(HEADS // 2):
                                last = nc.tensor.matmul(pO[h * TILES:(h + 1) * TILES, c * 2 * DH:(c + 1) * 2 * DH],
                                                        ET[:, p, c, h * TILES:(h + 1) * TILES],
                                                        vh[:, p, h, c].rearrange("p h d -> p (h d)"), start=True, stop=True)
                        last.then_inc(s["f_pO"], 1)
                    for r in (r0, r0 + 1):
                        m, p = PAIRS * g + r, r % 2
                        pe.wait_ge(s["f_O"], made(m))
                        pe.wait_ge(s["f_read"], freed(m, 1))
                        nc.tensor.transpose(pOT[:, 0:P], O[:, p, :], ident[:]).then_inc(s["f_pOT"], 1)


def route_buckets(V, step, dve, s, u, score, y, low, low_i, over, bucket, expert, hot, count, fresh, total, place, work,
                  at, carry, ps, slot, extra, dest):
    n = E1 * SUPER

    def floor(to, of):
        step(V.tensor_copy(low_i[:], of))
        step(V.tensor_copy(low[:], low_i[:]))
        step(V.tensor_tensor(over[:], low[:], of, ALU.is_gt))
        step(V.tensor_tensor(to, low[:], over[:], ALU.subtract))
    step(V.tensor_scalar_mul(y[:], score[:], 8.0))
    floor(bucket[:], y[:])
    step(V.tensor_scalar_mul(y[:], bucket[:], 1.0 / E1))
    floor(at[:], y[:])
    step(V.scalar_tensor_tensor(bucket[:], at[:], -float(E1), bucket[:], ALU.mult, ALU.add))
    for k in range(PICKS1):
        step(V.tensor_tensor(hot[:, k], bc(bucket[:, :, k], 1, [P, E1, SUPER]), bc(expert[:], 2, [P, E1, SUPER]),
                             ALU.is_equal))
    V.tensor_tensor(count[:], hot[:, 0], hot[:, 1], ALU.add).then_inc(s["h_count"], 1)
    dve.wait_ge(s["h_counted"], made(u))
    flat = place[:].rearrange("p e i -> p (e i)")
    for c in range(n // 512):
        last = V.tensor_copy(total[:].rearrange("p e i -> p (e i)")[:, bass.ts(c, 512)], ps[n // 512 + c][:])
    step(last)
    step(V.tensor_tensor_scan(flat, fresh[:].rearrange("p e i -> p (e i)"), total[:].rearrange("p e i -> p (e i)"),
                              0.0, ALU.mult, ALU.add))
    step(V.tensor_copy(work[:, :, 0], place[:, :, SUPER - 1]))
    step(V.tensor_tensor(place[:], place[:], total[:], ALU.subtract))
    for c in range(n // 512):
        last = V.tensor_tensor(flat[:, bass.ts(c, 512)], flat[:, bass.ts(c, 512)], ps[c][:], ALU.add)
    step(last)
    step(V.tensor_tensor(place[:], place[:], bc(carry[:], 2, [P, E1, SUPER]), ALU.add))
    step(V.tensor_tensor(carry[:], carry[:], work[:, :, 0], ALU.add))
    for k in range(PICKS1):
        step(V.tensor_tensor(work[:], place[:], hot[:, k], ALU.mult))
        step(V.tensor_reduce(at[:, :, k], work[:].rearrange("p e i -> p i e"), AX.X, ALU.add))
    step(V.tensor_tensor(over[:, :, 0], bucket[:, :, 0], bucket[:, :, 1], ALU.is_equal))
    step(V.tensor_tensor(at[:, :, 1], at[:, :, 1], over[:, :, 0], ALU.add))
    step(V.tensor_scalar(over[:], at[:], float(CAP1), None, ALU.is_ge))
    step(V.scalar_tensor_tensor(y[:], bucket[:], float(CAP1), at[:], ALU.mult, ALU.add))
    step(V.scalar_tensor_tensor(slot[:], over[:], NOWHERE, y[:], ALU.mult, ALU.add))
    step(V.tensor_copy(extra[:, :, :, 1], dest[:]))
    V.tensor_scalar_add(dest[:], dest[:], float(SUPER * P * PICKS1)).then_inc(s["h_slots"], 1)
    dve.wait_ge(s["h_slots"], made(u))


def layer1_project(nc, A, sems, ps, H, ident, before, ones, readT, XN3, XS1):
    ctx = ExitStack()
    with ctx:
        def sb(name, shape, dt=F32):
            return ctx.enter_context(nc.sbuf_tensor(name, shape, dt))
        power = sb("g_power", [P, QUAD])
        wo = sb("g_wo", [P, D])
        wh = sb("g_wh", [P, PICKS1])
        r = sb("g_r", [P, 2, QUAD, P])
        st, mv, ve, rstd = (sb("g_st", [P, 2, QUAD, 6]), sb("g_mv", [P, 2, QUAD, 2]), sb("g_ve", [P, 2, QUAD]),
                            sb("g_rstd", [P, 2, QUAD]))
        h = sb("g_h", [P, 2, QUAD, D])
        xn = sb("g_xn", [P, 2, QUAD, D])
        xT = sb("g_xT", [P, 2, QUAD * P])
        score = sb("g_score_t", [P, SUPER, PICKS1])
        y = sb("h_y", [P, SUPER, PICKS1])
        low = sb("h_low", [P, SUPER, PICKS1])
        low_i = sb("h_low_i", [P, SUPER, PICKS1], I32)
        over = sb("h_over", [P, SUPER, PICKS1])
        bucket = sb("h_bucket", [P, SUPER, PICKS1])
        expert = sb("h_expert", [P, E1])
        hot = sb("h_hot", [P, PICKS1, E1, SUPER], BF16)
        count = sb("h_count_t", [P, E1, SUPER], BF16)
        fresh = sb("h_fresh", [P, E1, SUPER])
        total = sb("h_total", [P, E1, SUPER])
        place = sb("h_place", [P, E1, SUPER])
        work = sb("h_work", [P, E1, SUPER])
        at = sb("h_at", [P, SUPER, PICKS1])
        carry = sb("h_carry", [P, E1])
        slot = sb("h_slot", [P, SUPER, PICKS1], I32)
        extra = sb("h_extra", [P, SUPER, PICKS1, 2])
        dest = sb("h_dest", [P, SUPER, PICKS1])
        sidx = sb("g_sidx", [P, 2, QUAD, PICKS1], I32)
        rows = sb("g_rows", [P, 2, QUAD, PICKS1, ROW])
        s = sems("g_const g_r g_pA g_h g_hk g_st g_mv g_ve g_rstd g_xn g_pT g_xT g_pG g_score g_stored g_turn "
                 "g_poolturn g_staged g_scattered h_dve h_const h_count h_counted h_slots",
                 dma="g_load g_store0 g_store1 g_rows0 g_rows1 g_sent0 g_sent1")
        store = [s["g_store0"], s["g_store1"]]
        staged = [s["g_rows0"], s["g_rows1"]]
        sent = [s["g_sent0"], s["g_sent1"]]
        pA, pT, pG, pC = [ps[0], ps[1]], ps[2], ps[3], ps[4:8]
        XN3v = XN3.rearrange("(i t) d -> t i d", t=P)
        blk = ctx.enter_context(nc.Block())

        def quads(u, half):
            return [(p, u * QUADS + 2 * half + p) for p in range(2)]

        def supers(eng, body, after=0):
            body(0)
            with eng.Fori(1, SUPERS) as u:
                body(u)
            if after:
                body(SUPERS)

        @blk.sync
        def _(sp):
            sp.dma_start(wo[:], A["L1_attn_Wo"]).then_inc(s["g_load"], 16)
            sp.dma_start(wh[:], A["L1_ffn_W_hash"][:, 0:PICKS1]).then_inc(s["g_load"], 16)
            sp.sem_inc(s["g_stored"], SEED)

            def body(u):
                for half in range(2):
                    if live(u - 1, SUPERS):
                        for p, m in quads(u - 1, half):
                            sp.wait_ge(s["g_scattered"], freed(m, 2))
                            for j in range(QUAD):
                                tile = XN3v[:, bass.ds(m * QUAD + j, 1), :].to_broadcast([P, PICKS1, D])
                                sp.dma_start(rows[:, p, j, :, 0:D], tile).then_inc(staged[p], 16)
                    if live(u, SUPERS):
                        for p, n in quads(u, half):
                            sp.wait_ge(s["g_xn"], made(n))
                            sp.dma_start(XN3v[:, bass.ds(n * QUAD, QUAD), :], xn[:, p]).then_inc(store[p], 16)
                        for p in range(2):
                            sp.wait_ge(store[p], 16 * (2 * u + half + 1))
                            sp.sem_inc(s["g_stored"], 1)
            supers(sp, body, after=1)

        @blk.gpsimd
        def _(pool):
            for name in "g_rstd g_hk g_scattered g_staged".split():
                pool.sem_inc(s[name], SEED)
            nc.gpsimd.memset(carry[:], 0.0)
            nc.gpsimd.memset(extra[:], 0.0)
            nc.gpsimd.memset(fresh[:], 1.0)
            nc.gpsimd.memset(power[:], -0.5).then_inc(s["g_const"], 1)
            pool.wait_ge(s["g_const"], 1)
            nc.gpsimd.memset(fresh[:, :, 0:1], 0.0)
            nc.gpsimd.iota(dest[:], pattern=[[P * PICKS1, SUPER], [1, PICKS1]], base=0, channel_multiplier=PICKS1,
                           allow_small_or_imprecise_dtypes=True)
            nc.gpsimd.iota(expert[:], pattern=[[1, E1]], base=0, channel_multiplier=0,
                           allow_small_or_imprecise_dtypes=True).then_inc(s["h_const"], 1)

            def scatter(u, half, p):
                m, i = u * QUADS + 2 * half + p, 2 * half + p
                pool.wait_ge(s["h_slots"], made(u))
                pool.wait_ge(staged[p], 16 * QUAD * (2 * u + half + 1))
                turn(pool, s["g_poolturn"])
                nc.gpsimd.tensor_copy(rows[:, p, :, :, D:ROW], extra[:, i * QUAD:(i + 1) * QUAD])
                nc.gpsimd.tensor_copy(sidx[:, p], slot[:, i * QUAD:(i + 1) * QUAD, :]).then_inc(s["g_staged"], 1)
                pool.wait_ge(s["g_staged"], made(m))
                turn(pool, s["g_poolturn"])
                for j in range(QUAD):
                    for k in range(PICKS1):
                        nc.gpsimd.indirect_dma_start(
                            out=XS1, out_offset=bass.IndirectOffsetOnAxis(ap=sidx[:, p, j, k:k + 1], axis=0),
                            in_=rows[:, p, j, k, :], in_offset=None, bounds_check=SLOTS1 - 1,
                            oob_is_err=False).then_inc(sent[p], 16)

            def body(u):
                before_it = not isinstance(u, int) or u > 0
                for half in range(2):
                    if live(u, SUPERS):
                        for p, n in quads(u, half):
                            pool.wait_ge(s["g_ve"], made(n))
                            nc.gpsimd.tensor_tensor(rstd[:, p, :], ve[:, p, :], power[:], ALU.pow).then_inc(s["g_rstd"], 1)
                        for p, n in quads(u, half):
                            nc.gpsimd.tensor_copy(H[:, bass.ds(n * QUAD, QUAD), :], h[:, p]).then_inc(s["g_hk"], 1)
                    if before_it:
                        for p in range(2):
                            scatter(u - 1, half, p)
                        for p in range(2):
                            pool.wait_ge(sent[p], 16 * QUAD * PICKS1 * (2 * (u - 1) + half + 1))
                            pool.sem_inc(s["g_scattered"], 1)
            supers(pool, body, after=1)

        @blk.scalar
        def _(act):
            for name in "g_r g_xT".split():
                act.sem_inc(s[name], SEED)

            def body(u):
                for half in range(2):
                    ns = [n for _, n in quads(u, half)]
                    for p, n in enumerate(ns):
                        act.wait_ge(s["g_pA"], freed(n, 2))
                        nc.scalar.copy(r[:, p], readT[:, :, bass.ds(n * QUAD, QUAD)].rearrange("e b i -> e i b")).then_inc(s["g_r"], 1)
                    for p, n in enumerate(ns):
                        act.wait_ge(s["g_pT"], made(n))
                        act.wait_ge(s["g_pG"], freed(n, 2))
                        nc.scalar.copy(xT[:, p, :], pT[:]).then_inc(s["g_xT"], 1)
            supers(act, body)

        @blk.vector
        def _(dve):
            for name in "g_h g_st g_mv g_ve g_xn g_score h_count h_slots".split():
                dve.sem_inc(s[name], SEED)
            dve.wait_ge(s["h_const"], 1)

            def body(u):
                for half in range(2):
                    ns = [n for _, n in quads(u, half)]
                    for p, n in enumerate(ns):
                        dve.wait_ge(s["g_pA"], made(n))
                        dve.wait_ge(s["g_hk"], freed(n, 2))
                        nc.vector.tensor_tensor(h[:, p], pA[p][:].rearrange("p (j d) -> p j d", j=QUAD),
                                                H[:, bass.ds(n * QUAD, QUAD), :], ALU.add).then_inc(s["g_h"], 1)
                        dve.wait_ge(s["g_h"], made(n))
                        turn(dve, s["g_turn"])
                        for j in range(QUAD):
                            last = nc.vector.bn_stats(st[:, p, j, :], h[:, p, j, :])
                        last.then_inc(s["g_st"], 1)
                        dve.wait_ge(s["g_st"], made(n))
                        turn(dve, s["g_turn"])
                        for j in range(QUAD):
                            last = nc.vector.bn_aggr(mv[:, p, j, :], st[:, p, j, :])
                        last.then_inc(s["g_mv"], 1)
                        dve.wait_ge(s["g_mv"], made(n))
                        nc.vector.tensor_scalar_add(ve[:, p, :], mv[:, p, :, 1], EPS).then_inc(s["g_ve"], 1)
                    for p, n in enumerate(ns):
                        dve.wait_ge(s["g_rstd"], made(n))
                        dve.wait_ge(s["g_stored"], freed(n, 2))
                        dve.wait_ge(s["g_pT"], freed(n, 2))
                        for j in range(QUAD):
                            last = nc.vector.tensor_scalar(xn[:, p, j, :], h[:, p, j, :], mv[:, p, j, 0:1], rstd[:, p, j:j + 1],
                                                           ALU.subtract, ALU.mult)
                        last.then_inc(s["g_xn"], 1)
                    for p, n in enumerate(ns):
                        i = 2 * half + p
                        dve.wait_ge(s["g_pG"], made(n))
                        nc.vector.tensor_copy(score[:, i * QUAD:(i + 1) * QUAD, :],
                                              pG[:, 0:QUAD * PICKS1].rearrange("p (j c) -> p j c", j=QUAD)).then_inc(s["g_score"], 1)
                dve.wait_ge(s["g_score"], made(u * QUADS + QUADS - 1))
                dve.wait_ge(s["g_staged"], made(u * QUADS - 1) if not isinstance(u, int) else SEED)
                step = Chain(dve, s["h_dve"], u * BUCKET_STEPS)
                route_buckets(nc.vector, step, dve, s, u, score, y, low, low_i, over, bucket, expert, hot, count, fresh, total,
                              place, work, at, carry, pC, slot, extra, dest)
                assert step.n == BUCKET_STEPS, step.n
            supers(dve, body)

        @blk.tensor
        def _(pe):
            for name in "g_pA g_pT g_pG h_counted".split():
                pe.sem_inc(s[name], SEED)
            pe.wait_ge(s["g_load"], 32)

            def body(u):
                for half in range(2):
                    ns = [n for _, n in quads(u, half)]
                    for p, n in enumerate(ns):
                        pe.wait_ge(s["g_r"], made(n))
                        pe.wait_ge(s["g_h"], freed(n, 2))
                        for j in range(QUAD):
                            last = nc.tensor.matmul(pA[p][:, bass.ts(j, D)], r[:, p, j, :], wo[:], start=True, stop=True)
                        last.then_inc(s["g_pA"], 1)
                    for p, n in enumerate(ns):
                        pe.wait_ge(s["g_xn"], made(n))
                        pe.wait_ge(s["g_xT"], freed(n, 1))
                        for j in range(QUAD):
                            last = nc.tensor.transpose(pT[:, bass.ts(j, P)], xn[:, p, j, :], ident[:])
                        last.then_inc(s["g_pT"], 1)
                    for p, n in enumerate(ns):
                        pe.wait_ge(s["g_xT"], made(n))
                        pe.wait_ge(s["g_score"], freed(n, 1))
                        for j in range(QUAD):
                            last = nc.tensor.matmul(pG[:, j * PICKS1:(j + 1) * PICKS1], xT[:, p, bass.ts(j, P)], wh[:],
                                                    start=True, stop=True)
                        last.then_inc(s["g_pG"], 1)
                pe.wait_ge(s["h_count"], made(u))
                flat, banks = count[:].rearrange("p e i -> p (e i)"), E1 * SUPER // 512
                for c in range(banks):
                    nc.tensor.matmul(pC[c][:], before[:], flat[:, bass.ts(c, 512)], start=True, stop=True)
                for c in range(banks):
                    last = nc.tensor.matmul(pC[banks + c][:], ones[:], flat[:, bass.ts(c, 512)], start=True, stop=True)
                last.then_inc(s["h_counted"], 1)
            supers(pe, body)


def layer1_experts(nc, A, sems, ps, ident, XS1, YT1):
    ctx = ExitStack()
    CH = HID // P
    RING = 4
    PARTS = [(0, P), (P, P), (2 * P, CAP1 - 2 * P)]
    LAST = CAP1 - 2 * P
    with ctx:
        def sb(name, shape, dt=F32):
            return ctx.enter_context(nc.sbuf_tensor(name, shape, dt))
        w1 = sb("i_w1", [P, RING, HID])
        w2 = sb("i_w2", [P, RING, CH, D])
        b1 = sb("i_b1_t", [P, E1, CH])
        b2 = sb("i_b2", [P, RING, D])
        x = sb("i_x", [P, RING, 3, ROW])
        place = sb("i_place", [P, RING, 3], I32)
        xT = sb("i_xT_t", [P, 2, CAP1])
        h = sb("i_h_t", [P, 2, CH, CAP1])
        y = sb("i_y_t", [P, 2, 3, D])
        warm = sb("i_warm", [P, 1])
        s = sems("i_pT i_xT i_p1 i_h i_pY i_y i_sent i_turn i_place",
                 dma="i_b1 i_w0 i_w1 i_w2 i_w3 i_out0 i_out1")
        landed, out = [s[f"i_w{r}"] for r in range(RING)], [s["i_out0"], s["i_out1"]]
        pT, p1, pY = [ps[0], ps[1]], ps[2:6], [ps[6], ps[7]]
        n_dma = 5
        blk = ctx.enter_context(nc.Block())

        @blk.sync
        def _(sp):
            sp.dma_start(b1[:], A["L1_ffn_b1"]).then_inc(s["i_b1"], 16)

            def body(n, k, i):
                wait_free(sp, s["i_y"], n, RING)
                sp.dma_start(w1[:, k, :], A["L1_ffn_W1"][n]).then_inc(landed[k], 16)
                sp.dma_start(w2[:, k], A["L1_ffn_W2"][n].rearrange("(c p) d -> p c d", p=P)).then_inc(landed[k], 16)
                sp.dma_start(b2[:, k, :], A["L1_ffn_b2"][n].partition_broadcast(P)).then_inc(landed[k], 16)
                sp.dma_start(x[:, k, 0:2, :], XS1[bass.ds(n * CAP1, 2 * P), :].rearrange("(c t) d -> t c d", t=P)).then_inc(landed[k], 16)
                sp.dma_start(x[0:LAST, k, 2, :], XS1[bass.ds(n * CAP1 + 2 * P, LAST), :]).then_inc(landed[k], 16)
            pipeline(sp, E1, 0, 0, RING, body)

        @blk.gpsimd
        def _(pool):
            pool.sem_inc(s["i_sent"], SEED)

            def body(n, k, i):
                p = k % 2
                if live(n, E1):
                    pool.wait_ge(s["i_y"], made(n))
                    pool.wait_ge(s["i_place"], made(n))
                    turn(pool, s["i_turn"])
                    for t, (_, rows) in enumerate(PARTS):
                        nc.gpsimd.indirect_dma_start(
                            out=YT1, out_offset=bass.IndirectOffsetOnAxis(ap=place[0:rows, k, t:t + 1], axis=0),
                            in_=y[0:rows, p, t, :], in_offset=None, bounds_check=TOKENS * PICKS1 - 1,
                            oob_is_err=False).then_inc(out[p], 16)
                if live(n - 1, E1):
                    pool.wait_ge(out[(k - 1) % 2], 48 * (2 * i + (k - 1) // 2 + 1))
                    pool.sem_inc(s["i_sent"], 1)
            pipeline(pool, E1, 0, 1, RING, body)

        @blk.scalar
        def _(act):
            act.sem_inc(s["i_h"], CH)
            act.wait_ge(s["i_b1"], 16)
            nc.scalar.activation(warm[:], ident[:, 0:1], ACT.Gelu)

            def body(n, k, i):
                for c in range(CH):
                    act.wait_ge(s["i_p1"], made(n * CH + c))
                    if c == 0:
                        act.wait_ge(s["i_pY"], freed(n, 2))
                    nc.scalar.activation(h[:, k % 2, c, :], p1[c][:, 0:CAP1], ACT.Gelu,
                                         bias=b1[:, bass.ds(n, 1), c]).then_inc(s["i_h"], 1)
            pipeline(act, E1, 0, 0, RING, body)

        @blk.vector
        def _(dve):
            for name in "i_y i_xT i_place".split():
                dve.sem_inc(s[name], SEED)

            def body(n, k, i):
                if live(n + 1, E1):
                    m, p, r = n + 1, (k + 1) % 2, (k + 1) % RING
                    dve.wait_ge(s["i_pT"], made(m))
                    wait_free(dve, s["i_pY"], m, 2)
                    nc.vector.tensor_copy(xT[:, p, :], pT[p][:, 0:CAP1]).then_inc(s["i_xT"], 1)
                    wait_free(dve, s["i_sent"], m, RING)
                    nc.vector.tensor_copy(place[:, r, 0:2], x[:, r, 0:2, D + 1])
                    nc.vector.tensor_copy(place[0:LAST, r, 2:3], x[0:LAST, r, 2, D + 1:ROW]).then_inc(s["i_place"], 1)
                if live(n - 1, E1):
                    m, p, r = n - 1, (k - 1) % 2, (k - 1) % RING
                    dve.wait_ge(s["i_pY"], made(m))
                    dve.wait_ge(s["i_sent"], freed(m, 2))
                    nc.vector.tensor_tensor(y[:, p, 0:2, :], pY[p][:, 0:2 * D].rearrange("p (c d) -> p c d", c=2),
                                            bc(b2[:, r, :], 1, [P, 2, D]), ALU.add)
                    nc.vector.tensor_tensor(y[0:LAST, p, 2, :], pY[p][0:LAST, 2 * D:3 * D], b2[0:LAST, r, :],
                                            ALU.add).then_inc(s["i_y"], 1)
            pipeline(dve, E1, 1, 1, RING, body)

        @blk.tensor
        def _(pe):
            for name in "i_pT i_p1 i_pY".split():
                pe.sem_inc(s[name], SEED)

            def body(n, k, i):
                if live(n, E1):
                    pe.wait_ge(s["i_xT"], made(n))
                    for c in range(CH):
                        pe.wait_ge(s["i_h"], n * CH + c + 1)
                        nc.tensor.matmul(p1[c][:, 0:CAP1], w1[:, k, bass.ts(c, P)], xT[:, k % 2, :],
                                         start=True, stop=True).then_inc(s["i_p1"], 1)
                if live(n + 1, E1):
                    m, p, r = n + 1, (k + 1) % 2, (k + 1) % RING
                    pe.wait_ge(landed[r], 16 * n_dma * (i + (k + 1) // RING + 1))
                    wait_free(pe, s["i_xT"], m, 2)
                    for t, (_, rows) in enumerate(PARTS):
                        last = nc.tensor.transpose(pT[p][:, t * P:t * P + rows], x[0:rows, r, t, 0:D], ident[0:rows, 0:rows])
                    last.then_inc(s["i_pT"], 1)
                if live(n - 1, E1):
                    m, p, r = n - 1, (k - 1) % 2, (k - 1) % RING
                    pe.wait_ge(s["i_h"], CH * (m + 2))
                    pe.wait_ge(s["i_y"], freed(m, 2))
                    for t, (at, rows) in enumerate(PARTS):
                        for c in range(CH):
                            last = nc.tensor.matmul(pY[p][0:rows, t * D:(t + 1) * D], h[:, p, c, at:at + rows], w2[:, r, c, :],
                                                    start=(c == 0), stop=(c == CH - 1))
                    last.then_inc(s["i_pY"], 1)
            pipeline(pe, E1, 1, 1, RING, body)


def layer1_combine(nc, sems, H, YT1, out):
    ctx = ExitStack()
    RING = 4
    with ctx:
        def sb(name, shape, dt=F32):
            return ctx.enter_context(nc.sbuf_tensor(name, shape, dt))
        got = sb("j_got", [P, RING, QUAD, PICKS1, D])
        acc = sb("j_acc_t", [P, RING, QUAD, D])
        s = sems("j_sum j_acc", dma="j_got0 j_got1 j_got2 j_got3 j_out0 j_out1 j_out2 j_out3")
        got_in, store = [s[f"j_got{r}"] for r in range(RING)], [s[f"j_out{r}"] for r in range(RING)]
        out_v = out.rearrange("i t d -> t i d")
        Y = YT1.rearrange("(i t k) d -> t i (k d)", t=P, k=PICKS1)
        N = TILES // QUAD
        blk = ctx.enter_context(nc.Block())

        @blk.scalar
        def _(act):
            def body(n, k, i):
                wait_free(act, s["j_acc"], n, RING)
                act.dma_start(got[:, k].rearrange("t i k d -> t i (k d)"), Y[:, bass.ds(n * QUAD, QUAD), :]).then_inc(got_in[k], 16)
            pipeline(act, N, 0, 0, RING, body)

        @blk.vector
        def _(dve):
            dve.sem_inc(s["j_sum"], SEED)
            dve.sem_inc(s["j_acc"], SEED)

            def body(n, k, i):
                dve.wait_ge(got_in[k], 16 * (i + 1))
                if not isinstance(i, int) or i > 0:
                    dve.wait_ge(store[k], 16 * i)
                nc.vector.tensor_tensor(acc[:, k], got[:, k, :, 0, :], got[:, k, :, 1, :], ALU.add).then_inc(s["j_sum"], 1)
                dve.wait_ge(s["j_sum"], made(n))
                nc.vector.scalar_tensor_tensor(acc[:, k], acc[:, k], 1.0 / PICKS1, H[:, bass.ds(n * QUAD, QUAD), :],
                                               ALU.mult, ALU.add).then_inc(s["j_acc"], 1)
            pipeline(dve, N, 0, 0, RING, body)

        @blk.sync
        def _(sp):
            def body(n, k, i):
                sp.wait_ge(s["j_acc"], made(n))
                sp.dma_start(out_v[:, bass.ds(n * QUAD, QUAD), :], acc[:, k]).then_inc(store[k], 16)
            pipeline(sp, N, 0, 0, RING, body)
            for r in range(RING):
                sp.wait_ge(store[r], 16 * (N // RING))


_INPUTS = ["x", "L0_tok_w", "L0_attn_Wk", "L0_attn_bk", "L0_attn_Wq", "L0_attn_bq", "L0_attn_Wv", "L0_attn_bv",
           "L0_ffn_Wr", "L0_ffn_br", "L0_ffn_Wgate", "L0_ffn_bgate", "L0_ffn_W1", "L0_ffn_W3", "L0_ffn_W2",
           "L1_attn_Wqkv", "L1_attn_Wr", "L1_attn_Wo", "L1_attn_ln_gamma", "L1_attn_ln_beta", "L1_attn_r_w_bias",
           "L1_attn_r_r_bias", "L1_ffn_W_hash", "L1_ffn_W1", "L1_ffn_b1", "L1_ffn_W2", "L1_ffn_b2"]


def kernel(**inputs):
    import concourse.bacc as bacc
    from concourse.bass_utils import run_bass_kernel_spmd

    laid = layout({n: np.asarray(inputs[n]) for n in _INPUTS})
    nc = bacc.Bacc("TRN2", target_bir_lowering=False, num_devices=1)
    arrays, A = {}, {}
    for name, a in laid.items():
        arrays[f"in_{name}"] = a
        A[name] = nc.dram_tensor(f"in_{name}", a.shape, mybir.dt.from_np(a.dtype), kind="ExternalInput").ap()
    out = nc.dram_tensor("out", (TILES, P, D), F32, kind="ExternalOutput").ap()
    tower(nc, A, out)
    return run_bass_kernel_spmd(nc, [arrays], core_ids=[0]).results[0]["out"]
```

```python
from contextlib import ExitStack

import numpy as np
import concourse.bass as bass
from concourse import mybir

F32 = mybir.dt.float32
BF16 = mybir.dt.bfloat16
I32 = mybir.dt.int32
ALU = mybir.AluOpType
ACT = mybir.ActivationFunctionType
AX = mybir.AxisListType

P = 128
D = 128
TILES = 64
TOKENS = TILES * P
QUAD = 4
PAIRS_OF_QUADS = TILES // QUAD // 2
HID = 512
E0, G0, EPG0 = 16, 4, 4
PICKS0 = 4
BLOCKS0 = TOKENS * PICKS0 // P + E0
E1, CAP1, PICKS1 = 64, 320, 2
SLOTS1 = E1 * CAP1
FILLS = BLOCKS0 // 4
FILL_X = -(-SLOTS1 // (FILLS * P)) * P
FILL_Y = -(-TOKENS * PICKS1 // (FILLS * P)) * P
SUPER = 16
QUADS = SUPER // QUAD
SUPERS = TILES // SUPER
REGION0 = TOKENS + P
SPARE0 = E0 * REGION0
ROWS0 = SPARE0 + (E0 + 1) * P
ROW = D + 2
NOWHERE = float(1 << 20)
ROUTE_STEPS = 71
BUCKET_STEPS = 30
HEADS, DH = 8, 16
EPS = 1e-5
MASKED = -1e30
SEED = 2


def made(n):
    return n + SEED + 1


def freed(n, bufs):
    return n + SEED + 1 - bufs


def bc(ap, dim, shape):
    return ap.unsqueeze(dim).to_broadcast(shape)


def live(n, count):
    return not isinstance(n, int) or 0 <= n < count


def wait_free(eng, sem, n, bufs):
    if not (isinstance(n, int) and n < bufs):
        eng.wait_ge(sem, freed(n, bufs))


def pipeline(eng, count, lead, lag, unroll, body):
    for n in range(-lead, unroll):
        body(n, n % unroll, n // unroll)
    with eng.Fori(1, count // unroll - 1) as i:
        for k in range(unroll):
            body(i * unroll + k, k, i)
    for n in range(count - unroll, count + lag):
        body(n, n % unroll, n // unroll)


def turn(eng, tally):
    eng.sem_inc(tally, 1)


class Chain:

    def __init__(self, eng, sem, start=0):
        self.eng, self.sem, self.start, self.n = eng, sem, start, 0

    def __call__(self, ins):
        self.n += 1
        ins.then_inc(self.sem, 1)
        self.eng.wait_ge(self.sem, self.start + self.n)


def positions():
    seq = np.arange(TILES - 1, -1, -1, dtype=np.float32)
    freq = np.float32(1.0) / np.float32(10000.0) ** (np.arange(0, D, 2, dtype=np.float32) / np.float32(D))
    angle = (seq[:, None] * freq[None, :]).astype(np.float32)
    return np.ascontiguousarray(np.concatenate([np.sin(angle), np.cos(angle)], axis=-1).T.astype(np.float32))


TRANSPOSED = ("x", "L1_attn_Wqkv", "L1_attn_Wr", "L1_attn_Wo", "L1_ffn_W_hash")


def layout(inputs):
    laid = {n: np.ascontiguousarray(a.T if n in TRANSPOSED else a) for n, a in inputs.items()}
    b1 = inputs["L1_ffn_b1"].reshape(E1, HID // P, P)
    laid["L1_ffn_b1"] = np.ascontiguousarray(b1.transpose(2, 0, 1))
    laid["positions"] = positions()
    return laid


class Signals:

    def __init__(self, nc, ctx):
        self.nc, self.ctx, self.of_stage = nc, ctx, []

    def __call__(self, names, dma=""):
        own = {n: self.nc.alloc_semaphore(n) for n in names.split()}
        self.of_stage += own.values()
        return own | {n: self.ctx.enter_context(self.nc.semaphore(n)) for n in dma.split()}

    def end_stage(self):
        self.nc.clear_and_free_semaphores(self.of_stage)
        self.of_stage = []
        self.nc.all_engine_barrier()


def tower(nc, A, out, stop=None):
    ctx = ExitStack()

    sems = Signals(nc, ctx)

    def dram(name, shape, dt=F32):
        return nc.dram_tensor(name, shape, dt, kind="Internal").ap()

    XN1 = dram("XN1", (TOKENS, D))
    XS0 = dram("XS0", (ROWS0, ROW))
    YT0 = dram("YT0", (TOKENS * PICKS0, D))
    BD = dram("BD", (P, TILES + 1, HEADS * TILES))
    XN3 = dram("XN3", (TOKENS, D))
    XS1 = dram("XS1", (FILLS * FILL_X, ROW))
    YT1 = dram("YT1", (FILLS * FILL_Y, D))

    with ctx:
        def keep(name, shape, dt=F32):
            return ctx.enter_context(nc.sbuf_tensor(name, shape, dt))

        ps = [ctx.enter_context(nc.psum_tensor(f"ps{i}", [P, 512], F32)) for i in range(8)]
        H = keep("H", [P, TILES, D])
        ident = keep("ident", [P, P])
        before = keep("before", [P, P], BF16)
        ones = keep("ones", [P, P], BF16)

        with ExitStack() as c0:
            def sb0(name, shape, dt=F32):
                return c0.enter_context(nc.sbuf_tensor(name, shape, dt))
            filler = sb0("filler", [P, ROW])
            block_expert = sb0("block_expert", [1, BLOCKS0], I32)
            block_row = sb0("block_row", [1, BLOCKS0], I32)
            w1 = sb0("w1", [P, E0, HID])
            w3 = sb0("w3", [P, E0, HID])
            w2 = sb0("w2", [P, E0, HID // P, D])
            layer0_attention(nc, A, sems, ps, H, ident, before, ones, filler, w1, w3, w2, block_expert,
                             block_row, XN1, XS0)
            sems.end_stage()
            if stop == "A":
                return
            layer0_experts(nc, sems, ps, ident, filler, block_expert, block_row, w1, w3, w2, XS0, YT0, XS1, YT1)
            sems.end_stage()
            if stop == "C":
                return
        with ExitStack() as c1:
            wnT = c1.enter_context(nc.sbuf_tensor("wnT", [P, P, TILES], F32))
            layer0_combine(nc, A, sems, ps, H, ident, wnT, YT0, BD)
            sems.end_stage()
            if stop == "D":
                return
            readT = c1.enter_context(nc.sbuf_tensor("readT", [P, P, TILES], F32))
            layer1_attention(nc, A, sems, ps, ident, wnT, readT, BD)
            sems.end_stage()
            layer1_project(nc, A, sems, ps, H, ident, before, ones, readT, XN3, XS1)
            sems.end_stage()
            if stop == "E":
                return
        layer1_experts(nc, A, sems, ps, ident, XS1, YT1)
        sems.end_stage()
        layer1_combine(nc, sems, H, YT1, out)
        sems.end_stage()


def route_top2(dve, V, step, s, u, small, prob, rank, first, second, work, pair, picks, logit, total, row, fresh, carry,
               pC, slot_of, extra_of, dest):
    slot = slot_of[:, bass.ds(u, 1)].rearrange("p o i k -> p (o i) k")
    extra = extra_of[:, bass.ds(u, 1)].rearrange("p o i k c -> p (o i) k c")
    flat5 = "p i g e -> p (i g) e"
    group = [P, SUPER * (1 + G0), EPG0]

    def small_(k):
        return small[k][:].rearrange("p i g -> p (i g)")
    step(V.tensor_reduce(small_(0), logit[:].rearrange(flat5), AX.X, ALU.max))
    V.tensor_tensor(work[:].rearrange(flat5), logit[:].rearrange(flat5), bc(small_(0), 2, group),
                    ALU.subtract).then_inc(s["r_max"], 1)
    yield
    dve.wait_ge(s["r_exp"], made(u))
    step(V.tensor_reduce(small_(0), prob[:].rearrange(flat5), AX.X, ALU.add))
    step(V.reciprocal(small_(1), small_(0)))
    step(V.tensor_tensor(prob[:].rearrange(flat5), prob[:].rearrange(flat5), bc(small_(1), 2, group), ALU.mult))
    pr, rk = prob[:].rearrange(flat5), rank[:].rearrange(flat5)
    pairs = [(a, b) for a in range(EPG0) for b in range(a + 1, EPG0)]
    for k, (a, b) in enumerate(pairs):
        last = V.tensor_tensor(pair[:, k, :], pr[:, :, a], pr[:, :, b], ALU.is_ge)
    step(last)
    for e in range(EPG0):
        losing = [k for k, (a, b) in enumerate(pairs) if b == e]
        winning = [k for k, (a, b) in enumerate(pairs) if a == e]
        if winning:
            step(V.tensor_scalar(rk[:, :, e], pair[:, winning[0], :], -1.0, float(len(winning)), ALU.mult, ALU.add))
            for k in winning[1:]:
                step(V.tensor_tensor(rk[:, :, e], rk[:, :, e], pair[:, k, :], ALU.subtract))
        else:
            step(V.tensor_copy(rk[:, :, e], pair[:, losing.pop(0), :]))
        for k in losing:
            step(V.tensor_tensor(rk[:, :, e], rk[:, :, e], pair[:, k, :], ALU.add))
    yield
    V.tensor_scalar(first[:], rank[:], 0.0, None, ALU.is_equal)
    step(V.tensor_scalar(second[:], rank[:], 1.0, None, ALU.is_equal))
    step(V.tensor_tensor(work[:], first[:], second[:], ALU.add))
    V.tensor_tensor(picks[:].rearrange("p (g e) i -> p i g e", g=G0), work[:, :, 1:, :],
                    bc(work[:, :, 0, :], 3, [P, SUPER, G0, EPG0]), ALU.mult).then_inc(s["r_picks"], 1)
    dve.wait_ge(s["r_picks"], made(u))
    step(V.tensor_tensor(work[:], prob[:], first[:], ALU.mult))
    step(V.tensor_reduce(small_(0), work[:].rearrange(flat5), AX.X, ALU.add))
    step(V.tensor_tensor(work[:], prob[:], second[:], ALU.mult))
    step(V.tensor_reduce(small_(1), work[:].rearrange(flat5), AX.X, ALU.add))
    step(V.tensor_tensor(small[2][:], small[0][:], small[1][:], ALU.add))
    step(V.tensor_scalar(small[2][:], small[2][:], 0.9, None, ALU.is_le))
    step(V.tensor_tensor(small[1][:], small[1][:], small[2][:], ALU.mult))
    step(V.tensor_tensor(small[2][:], small[0][:], small[1][:], ALU.add))
    step(V.tensor_scalar_add(small[2][:], small[2][:], 1e-9))
    step(V.reciprocal(small[3][:], small[2][:]))
    step(V.tensor_tensor(small[0][:], small[0][:], small[3][:], ALU.mult))
    step(V.tensor_tensor(small[1][:], small[1][:], small[3][:], ALU.mult))
    yield
    dve.wait_ge(s["r_counted"], made(u))
    flat_row, n = row[:].rearrange("p e i -> p (e i)"), E0 * SUPER
    step(V.tensor_copy(total[:].rearrange("p e i -> p (e i)"), pC[:, n:2 * n]))
    step(V.tensor_tensor_scan(flat_row, fresh[:].rearrange("p e i -> p (e i)"), total[:].rearrange("p e i -> p (e i)"),
                              0.0, ALU.mult, ALU.add))
    step(V.tensor_copy(small[4][:, :, 0], row[:, :, SUPER - 1]))
    step(V.tensor_tensor(row[:], row[:], total[:], ALU.subtract))
    step(V.tensor_tensor(flat_row, flat_row, pC[:, 0:n], ALU.add))
    step(V.tensor_tensor(row[:], row[:], bc(carry[:], 2, [P, E0, SUPER]), ALU.add))
    step(V.tensor_tensor(carry[:], carry[:], small[4][:, :, 0], ALU.add))
    row_v = row[:].rearrange("p (g e) i -> p i g e", g=G0)
    pick16 = work[:].rearrange("p i g e -> p (i g e)")[:, 0:n].rearrange("p (i g e) -> p i g e", i=SUPER, g=G0)
    pick_w = small[4][:, :, G0]
    for a, of_group in enumerate((first, second)):
        for b, of_expert in enumerate((first, second)):
            k = 2 * a + b
            step(V.tensor_tensor(pick16, of_expert[:, :, 1:, :], bc(of_group[:, :, 0, :], 3, [P, SUPER, G0, EPG0]),
                                 ALU.mult))
            step(V.tensor_tensor(pick16, pick16, row_v, ALU.mult))
            step(V.tensor_reduce(pick_w, pick16, AX.XY, ALU.add))
            step(V.tensor_copy(slot[:, :, k], pick_w))
            four = small[4][:, :, 0:G0]
            step(V.tensor_tensor(four, of_group[:, :, 0, :], small[b][:, :, 1:], ALU.mult))
            step(V.tensor_reduce(pick_w, four, AX.X, ALU.add))
            step(V.tensor_tensor(pick_w, pick_w, small[a][:, :, 0], ALU.mult))
            step(V.tensor_scalar_mul(extra[:, :, k, 0], pick_w, float(G0) ** -0.5))
            if k < PICKS0 - 1:
                yield
    step(V.tensor_copy(extra[:, :, :, 1], dest[:]))
    V.tensor_scalar_add(dest[:], dest[:], float(SUPER * P * PICKS0)).then_inc(s["r_slots"], 1)
    dve.wait_ge(s["r_slots"], made(u))


def layer0_attention(nc, A, sems, ps, H, ident, before, ones, filler, w1, w3, w2, block_expert, block_row, XN1, XS0):
    ctx = ExitStack()
    with ctx:
        def sb(name, shape, dt=F32):
            return ctx.enter_context(nc.sbuf_tensor(name, shape, dt))
        causal = sb("causal", [P, P])
        power = sb("power", [P, QUAD])
        warm = sb("warm", [P, 1])
        xidx = sb("xidx", [P, TILES], I32)
        wq, wk, wv = sb("wq", [P, D]), sb("wk", [P, D]), sb("wv", [P, D])
        bq, bk, bv = sb("bq", [P, 1]), sb("bk", [P, 1]), sb("bv", [P, D])
        wr = sb("wr", [P, 1 + G0, EPG0])
        br = sb("br", [P, 1 + G0, EPG0])
        idx4 = sb("idx4", [P, 2, QUAD], I32)
        h0 = sb("h0", [P, 2, 2, QUAD, D])
        st = sb("st", [P, 2, QUAD, 6])
        mv = sb("mv", [P, 2, QUAD, 2])
        ve = sb("ve", [P, 2, QUAD])
        rstd = sb("rstd", [P, 2, QUAD])
        xn = sb("xn", [P, 2, QUAD, D])
        xT = sb("xT", [P, 2, QUAD * P])
        qT = sb("qT", [P, 2, QUAD * P])
        kT = sb("kT", [P, 2, QUAD * P])
        v = sb("v", [P, 2, QUAD, D])
        lm = sb("lm", [P, 2, QUAD, P])
        nmx = sb("nmx", [P, 2, QUAD])
        psum = sb("psum", [P, 2, QUAD])
        rsum = sb("rsum", [P, 2, QUAD])
        st1 = sb("st1", [P, 2, QUAD, 6])
        mv1 = sb("mv1", [P, 2, QUAD, 2])
        ve1 = sb("ve1", [P, 2, QUAD])
        rstd1 = sb("rstd1", [P, 2, QUAD])
        xn1 = sb("xn1", [P, 2, QUAD, D])
        logit = sb("r_logit", [P, SUPER, 1 + G0, EPG0])
        prob4 = sb("r_prob", [P, SUPER, 1 + G0, EPG0])
        rank = sb("r_rank", [P, SUPER, 1 + G0, EPG0])
        first = sb("r_first", [P, SUPER, 1 + G0, EPG0])
        second = sb("r_second", [P, SUPER, 1 + G0, EPG0])
        work = sb("r_work", [P, SUPER, 1 + G0, EPG0])
        pair = sb("r_pair", [P, 6, SUPER * (1 + G0)])
        small = [sb(f"r_small{k}", [P, SUPER, 1 + G0]) for k in range(5)]
        picks = sb("r_picks_t", [P, E0, SUPER], BF16)
        total = sb("r_total", [P, E0, SUPER])
        row = sb("r_row", [P, E0, SUPER])
        fresh = sb("r_fresh", [P, E0, SUPER])
        carry = sb("r_carry", [P, E0])
        region = sb("r_region", [P, E0])
        slot = sb("r_slot", [P, SUPERS, SUPER, PICKS0], I32)
        extra = sb("r_extra", [P, SUPERS, SUPER, PICKS0, 2])
        dest = sb("r_dest", [P, SUPER, PICKS0])
        sidx = sb("sidx", [P, 2, QUAD, PICKS0], I32)
        rows = sb("rows", [P, 2, QUAD, PICKS0, ROW])
        count_i = sb("t_count_i", [P, E0], I32)
        padded = sb("t_padded", [1, E0], I32)
        blocks = sb("t_blocks", [P, E0])
        block_end = sb("t_block_end", [P, E0])
        flat_k, flat_q = (t[0:1].rearrange("p a b -> p (a b)") for t in (kT, qT))
        index, passed, expert_f = (flat_k[:, bass.ts(c, BLOCKS0)] for c in range(3))
        SHARES = 8
        reached = flat_q[:, 0:BLOCKS0 // SHARES * E0].rearrange("p (b e) -> p b e", e=E0)
        pT, pQ, pK, pV, pL, pR, pC, pG = ps
        s = sems("a_const a_eye a_idx a_stats a_mv a_ve a_rstd a_xn a_pT a_xT a_pQ a_pK a_pV a_qT a_kT a_v "
                 "a_pL a_lm a_max a_prob a_rsum a_vs a_pR a_h1 a_stats1 a_mv1 a_ve1 a_rstd1 a_xn1 a_stored a_pT1 "
                 "a_x1T a_pG a_logit a_p2 a_turn a_poolturn a_staged a_scattered a_fillready a_padded a_index "
                 "r_dve r_max r_exp r_picks r_counted r_slots t_dve t_ready",
                 dma="a_load a_xload a_zeroed a_expw a_gather0 a_gather1 a_gather2 a_gather3 a_store0 a_store1 a_rows0 a_rows1 a_sent0 "
                     "a_sent1 a_filled")
        gather = [s[f"a_gather{r}"] for r in range(QUADS)]
        store = [s["a_store0"], s["a_store1"]]
        staged = [s["a_rows0"], s["a_rows1"]]
        sent = [s["a_sent0"], s["a_sent1"]]
        n_load = 10
        XN1v = XN1.rearrange("(i t) d -> t i d", t=P)
        blk = ctx.enter_context(nc.Block())

        def quads(u, half):
            return [(p, u * QUADS + 2 * half + p) for p in range(2)]

        def supers(eng, body, peeled=1, after=1):
            for u in range(peeled):
                body(u)
            with eng.Fori(peeled, SUPERS) as u:
                body(u)
            for u in range(SUPERS, SUPERS + after):
                body(u)

        def lagging(u, half):
            return (u - 1, 0) if half else (u - 2, 1)

        @blk.sync
        def _(sp):
            sp.dma_start(xidx[:], A["x"]).then_inc(s["a_xload"], 16)
            for dst, src in ((wq[:], A["L0_attn_Wq"]), (wk[:], A["L0_attn_Wk"]), (wv[:], A["L0_attn_Wv"]),
                             (bq[:], A["L0_attn_bq"].unsqueeze(1)), (bk[:], A["L0_attn_bk"].unsqueeze(1)),
                             (bv[:], A["L0_attn_bv"].partition_broadcast(P)),
                             (wr[:, 0, :], A["L0_ffn_Wr"]),
                             (wr[:, 1:, :], A["L0_ffn_Wgate"].rearrange("g d e -> d g e")),
                             (br[:, 0, :], A["L0_ffn_br"].partition_broadcast(P)),
                             (br[:, 1:, :], A["L0_ffn_bgate"].partition_broadcast(P))):
                sp.dma_start(dst, src).then_inc(s["a_load"], 16)
            sp.sem_inc(s["a_stored"], SEED)
            sp.wait_ge(s["a_fillready"], 1)
            with sp.Fori(0, E0 + 1) as e:
                sp.dma_start(XS0[bass.ds(SPARE0 + e * P, P), :], filler[:]).then_inc(s["a_zeroed"], 16)

            def weights(u, half):
                for k in range(E0 // SUPERS // 2):
                    e = u * (E0 // SUPERS) + half * (E0 // SUPERS // 2) + k
                    for to, of in ((w1[:, bass.ds(e, 1), :], A["L0_ffn_W1"][bass.ds(e, 1)].rearrange("o d h -> d o h")),
                                   (w3[:, bass.ds(e, 1), :], A["L0_ffn_W3"][bass.ds(e, 1)].rearrange("o d h -> d o h")),
                                   (w2[:, bass.ds(e, 1), :, :].rearrange("p o c d -> p (o c) d"),
                                    A["L0_ffn_W2"][bass.ds(e, 1)].rearrange("o (c p) d -> p (o c) d", p=P))):
                        sp.dma_start(to, of).then_inc(s["a_expw"], 16)

            def body(u):
                for half in range(2):
                    if live(lagging(u, half)[0], SUPERS):
                        for p, m in quads(*lagging(u, half)):
                            wait_free(sp, s["a_scattered"], m, 2)
                            for j in range(QUAD):
                                tile = XN1v[:, bass.ds(m * QUAD + j, 1), :].to_broadcast([P, PICKS0, D])
                                sp.dma_start(rows[:, p, j, :, 0:D], tile).then_inc(staged[p], 16)
                    if live(u, SUPERS):
                        for p, n in quads(u, half):
                            sp.wait_ge(s["a_xn1"], made(n))
                            sp.dma_start(XN1v[:, bass.ds(n * QUAD, QUAD), :], xn1[:, p]).then_inc(store[p], 16)
                        for p in range(2):
                            sp.wait_ge(store[p], 16 * (2 * u + half + 1))
                            sp.sem_inc(s["a_stored"], 1)
                        weights(u, half)
            supers(sp, body, peeled=2, after=2)
            sp.wait_ge(s["a_zeroed"], 16 * (E0 + 1))
            sp.wait_ge(s["a_expw"], 48 * E0)
            sp.wait_ge(s["a_padded"], 1)
            with sp.Fori(0, E0) as e:
                at = sp.value_load(padded[0:1, bass.ds(e, 1)], min_val=0, max_val=SPARE0 - P)
                sp.dma_start(XS0[bass.ds(at, P), :], filler[:]).then_inc(s["a_filled"], 16)
            sp.wait_ge(s["a_filled"], 16 * E0)

        @blk.gpsimd
        def _(pool):
            for name in ("a_idx", "a_rstd", "a_rstd1", "a_scattered", "a_staged"):
                pool.sem_inc(s[name], SEED)
            nc.gpsimd.memset(filler[:, 0:D + 1], 0.0)
            nc.gpsimd.memset(filler[:, D + 1:ROW], NOWHERE).then_inc(s["a_fillready"], 1)
            nc.gpsimd.memset(ident[:], 0.0)
            nc.gpsimd.memset(causal[:], 0.0)
            nc.gpsimd.memset(ones[:], 1.0)
            nc.gpsimd.memset(before[:], 1.0)
            nc.gpsimd.memset(fresh[:], 1.0)
            nc.gpsimd.memset(power[:], -0.5).then_inc(s["a_eye"], 1)
            pool.wait_ge(s["a_eye"], 1)
            nc.gpsimd.memset(fresh[:, :, 0:1], 0.0)
            nc.gpsimd.iota(carry[:], pattern=[[REGION0, E0]], base=0, channel_multiplier=0,
                           allow_small_or_imprecise_dtypes=True)
            nc.gpsimd.iota(region[:], pattern=[[REGION0, E0]], base=0, channel_multiplier=0,
                           allow_small_or_imprecise_dtypes=True)
            nc.gpsimd.iota(dest[:], pattern=[[P * PICKS0, SUPER], [1, PICKS0]], base=0, channel_multiplier=PICKS0,
                           allow_small_or_imprecise_dtypes=True)
            nc.gpsimd.affine_select(out=ident[:], in_=ident[:], compare_op=ALU.not_equal, fill=1.0, base=0,
                                    pattern=[[-1, P]], channel_multiplier=1)
            nc.gpsimd.affine_select(out=causal[:], in_=causal[:], compare_op=ALU.is_ge, fill=MASKED, base=0,
                                    pattern=[[1, P]], channel_multiplier=-1)
            nc.gpsimd.affine_select(out=before[:], in_=before[:], compare_op=ALU.is_gt, fill=0.0, base=0,
                                    pattern=[[1, P]], channel_multiplier=-1).then_inc(s["a_const"], 1)
            pool.wait_ge(s["a_const"], 1)
            pool.wait_ge(s["a_xload"], 16)

            def fetch(u, half):
                for p, n in quads(u, half):
                    wait_free(pool, s["a_h1"], n, QUADS)
                    turn(pool, s["a_poolturn"])
                    nc.gpsimd.tensor_copy(idx4[:, p, :], xidx[:, bass.ds(n * QUAD, QUAD)]).then_inc(s["a_idx"], 1)
                    pool.wait_ge(s["a_idx"], made(n))
                    turn(pool, s["a_poolturn"])
                    for j in range(QUAD):
                        nc.gpsimd.indirect_dma_start(
                            out=h0[:, half, p, j, :], out_offset=None, in_=A["L0_tok_w"],
                            in_offset=bass.IndirectOffsetOnAxis(ap=idx4[:, p, j:j + 1], axis=0)).then_inc(gather[2 * half + p], 16)

            def scatter(u, half, p, tiles):
                if not live(u, SUPERS):
                    return
                m, i = u * QUADS + 2 * half + p, 2 * half + p
                if tiles[0] == 0:
                    pool.wait_ge(s["r_slots"], made(u))
                    pool.wait_ge(staged[p], 16 * QUAD * (2 * u + half + 1))
                    turn(pool, s["a_poolturn"])
                    quad = slice(i * QUAD, (i + 1) * QUAD)
                    nc.gpsimd.tensor_copy(rows[:, p, :, :, D:ROW],
                                          extra[:, bass.ds(u, 1), quad].rearrange("p o i k c -> p (o i) k c"))
                    nc.gpsimd.tensor_copy(sidx[:, p], slot[:, bass.ds(u, 1), quad].rearrange("p o i k -> p (o i) k")
                                          ).then_inc(s["a_staged"], 1)
                    pool.wait_ge(s["a_staged"], made(m))
                    turn(pool, s["a_poolturn"])
                for j in tiles:
                    for k in range(PICKS0):
                        nc.gpsimd.indirect_dma_start(
                            out=XS0, out_offset=bass.IndirectOffsetOnAxis(ap=sidx[:, p, j, k:k + 1], axis=0),
                            in_=rows[:, p, j, k, :], in_offset=None, bounds_check=ROWS0 - 1,
                            oob_is_err=False).then_inc(sent[p], 16)

            def body(u):
                for half in range(2):
                    v, of = lagging(u, half)
                    pass
                    if live(u, SUPERS):
                        for p, n in quads(u, half):
                            pool.wait_ge(s["a_ve"], made(n))
                            nc.gpsimd.tensor_tensor(rstd[:, p, :], ve[:, p, :], power[:], ALU.pow).then_inc(s["a_rstd"], 1)
                    scatter(v, of, 0, (0, 1, 2, 3))
                    if live(u, SUPERS):
                        if half == 0:
                            fetch(u, 1)
                        elif not isinstance(u, int):
                            fetch(u + 1, 0)
                        elif u + 1 < SUPERS:
                            fetch(u + 1, 0)
                    scatter(v, of, 1, (0, 1))
                    if live(u, SUPERS):
                        for p, n in quads(u, half):
                            pool.wait_ge(s["a_ve1"], made(n))
                            nc.gpsimd.tensor_tensor(rstd1[:, p, :], ve1[:, p, :], power[:], ALU.pow).then_inc(s["a_rstd1"], 1)
                    scatter(v, of, 1, (2, 3))
                    if live(v, SUPERS):
                        for p in range(2):
                            pool.wait_ge(sent[p], 16 * QUAD * PICKS0 * (2 * v + of + 1))
                            pool.sem_inc(s["a_scattered"], 1)
            fetch(0, 0)
            body(0)
            body(1)
            with pool.Fori(2, SUPERS - 1) as u:
                body(u)
            body(SUPERS - 1)
            pool.wait_ge(s["a_logit"], made(TILES // QUAD - 1))
            nc.gpsimd.iota(index, pattern=[[1, BLOCKS0]], base=0, channel_multiplier=0,
                           allow_small_or_imprecise_dtypes=True).then_inc(s["a_index"], 1)
            body(SUPERS)
            body(SUPERS + 1)

        @blk.vector
        def _(dve):
            for name in ("a_stats a_mv a_ve a_xn a_v a_lm a_max a_rsum a_vs a_p2 a_h1 a_stats1 a_mv1 a_ve1 a_xn1 "
                         "a_logit r_max r_picks r_slots").split():
                dve.sem_inc(s[name], SEED)
            dve.wait_ge(s["a_load"], 16 * n_load)
            dve.wait_ge(s["a_const"], 1)

            def normalise(n, p, x_of, st, mv, ve, tag):
                turn(dve, s["a_turn"])
                for j in range(QUAD):
                    last = nc.vector.bn_stats(st[:, p, j, :], x_of(j))
                last.then_inc(s["a_stats" + tag], 1)
                dve.wait_ge(s["a_stats" + tag], made(n))
                turn(dve, s["a_turn"])
                for j in range(QUAD):
                    last = nc.vector.bn_aggr(mv[:, p, j, :], st[:, p, j, :])
                last.then_inc(s["a_mv" + tag], 1)
                dve.wait_ge(s["a_mv" + tag], made(n))
                nc.vector.tensor_scalar_add(ve[:, p, :], mv[:, p, :, 1], EPS).then_inc(s["a_ve" + tag], 1)

            def scale(n, p, x_of, mv, rstd, to, tag):
                dve.wait_ge(s["a_rstd" + tag], made(n))
                for j in range(QUAD):
                    last = nc.vector.tensor_scalar(to[:, p, j, :], x_of(j), mv[:, p, j, 0:1], rstd[:, p, j:j + 1],
                                                   ALU.subtract, ALU.mult)
                last.then_inc(s["a_xn" + tag], 1)

            def body(u):
                routing = iter(route(u - 1)) if live(u - 1, SUPERS) else iter(())
                if not live(u, SUPERS):
                    for _ in routing:
                        pass
                    return
                for half in range(2):
                    ns = [n for _, n in quads(u, half)]
                    for p, n in enumerate(ns):
                        dve.wait_ge(gather[2 * half + p], 16 * QUAD * (u + 1))
                        normalise(n, p, lambda j: h0[:, half, p, j, :], st, mv, ve, "")
                    next(routing, None)
                    for p, n in enumerate(ns):
                        wait_free(dve, s["a_pR"], n, 2)
                        scale(n, p, lambda j: h0[:, half, p, j, :], mv, rstd, xn, "")
                    next(routing, None)
                    for p, n in enumerate(ns):
                        dve.wait_ge(s["a_pV"], made(n))
                        nc.vector.tensor_tensor(v[:, p], pV[:].rearrange("p (j d) -> p j d", j=QUAD),
                                                bc(bv[:], 1, [P, QUAD, D]), ALU.add).then_inc(s["a_v"], 1)
                    next(routing, None)
                    for p, n in enumerate(ns):
                        dve.wait_ge(s["a_pL"], made(n))
                        nc.vector.tensor_tensor(lm[:, p], pL[:].rearrange("p (j t) -> p j t", j=QUAD),
                                                bc(causal[:], 1, [P, QUAD, P]), ALU.add).then_inc(s["a_lm"], 1)
                        dve.wait_ge(s["a_lm"], made(n))
                        nc.vector.tensor_reduce(nmx[:, p, :], lm[:, p], AX.X, ALU.max, negate=True).then_inc(s["a_max"], 1)
                    next(routing, None)
                    for p, n in enumerate(ns):
                        dve.wait_ge(s["a_prob"], made(n))
                        nc.vector.tensor_scalar_mul(psum[:, p, :], psum[:, p, :], float(np.sqrt(P))).then_inc(s["a_p2"], 1)
                        dve.wait_ge(s["a_p2"], made(n))
                        nc.vector.reciprocal(rsum[:, p, :], psum[:, p, :]).then_inc(s["a_rsum"], 1)
                        dve.wait_ge(s["a_rsum"], made(n))
                        dve.wait_ge(s["a_v"], made(n))
                        nc.vector.tensor_tensor(v[:, p], v[:, p], bc(rsum[:, p, :], 2, [P, QUAD, D]),
                                                ALU.mult).then_inc(s["a_vs"], 1)
                    next(routing, None)
                    for p, n in enumerate(ns):
                        dve.wait_ge(s["a_pR"], made(n))
                        nc.vector.tensor_tensor(H[:, bass.ds(n * QUAD, QUAD), :],
                                                pR[:].rearrange("p (j d) -> p j d", j=QUAD), h0[:, half, p],
                                                ALU.add).then_inc(s["a_h1"], 1)
                        dve.wait_ge(s["a_h1"], made(n))
                        normalise(n, p, lambda j: H[:, bass.ds(n * QUAD + j, 1), :].rearrange("p o d -> p (o d)"),
                                  st1, mv1, ve1, "1")
                    next(routing, None)
                    for p, n in enumerate(ns):
                        dve.wait_ge(s["a_stored"], freed(n, 2))
                        dve.wait_ge(s["a_pT1"], freed(n, 2))
                        scale(n, p, lambda j: H[:, bass.ds(n * QUAD + j, 1), :].rearrange("p o d -> p (o d)"),
                              mv1, rstd1, xn1, "1")
                    next(routing, None)
                    for p, n in enumerate(ns):
                        i = 2 * half + p
                        dve.wait_ge(s["a_pG"], made(n))
                        nc.vector.tensor_tensor(
                            logit[:, i * QUAD:(i + 1) * QUAD].rearrange("p i g e -> p i (g e)"),
                            pG[:, 0:QUAD * 20].rearrange("p (i c) -> p i c", i=QUAD),
                            bc(br[:].rearrange("p g e -> p (g e)"), 1, [P, QUAD, 20]), ALU.add).then_inc(s["a_logit"], 1)
                    next(routing, None)

            def route(u):
                dve.wait_ge(s["a_logit"], made(u * QUADS + QUADS - 1))
                step = Chain(dve, s["r_dve"], u * ROUTE_STEPS)
                yield from route_top2(dve, nc.vector, step, s, u, small, prob4, rank, first, second, work, pair, picks,
                                      logit, total, row, fresh, carry, pC, slot, extra, dest)
                assert step.n == ROUTE_STEPS, step.n
            supers(dve, body)
            V = nc.vector
            step = Chain(dve, s["t_dve"])
            step(V.tensor_copy(padded[:], carry[0:1, :]))
            dve.sem_inc(s["a_padded"], 1)
            step(V.scalar_tensor_tensor(count_i[:], carry[:], float(P - 1), region[:], ALU.add, ALU.subtract))
            step(V.tensor_single_scalar(count_i[:], count_i[:], 7, ALU.arith_shift_right))
            step(V.tensor_copy(blocks[:], count_i[:]))
            step(V.memset(region[:], 1.0))
            step(V.tensor_tensor_scan(block_end[:], region[:], blocks[:], 0.0, ALU.mult, ALU.add))
            dve.wait_ge(s["a_index"], 1)
            share = [1, BLOCKS0 // SHARES, E0]
            for c in range(SHARES):
                part = bass.ts(c, BLOCKS0 // SHARES)
                step(V.tensor_tensor(reached, bc(index[:, part], 2, share), bc(block_end[0:1, :], 1, share), ALU.is_ge))
                step(V.tensor_reduce(expert_f[:, part], reached, AX.X, ALU.add))
                step(V.tensor_tensor(reached, reached, bc(blocks[0:1, :], 1, share), ALU.mult))
                step(V.tensor_reduce(passed[:, part], reached, AX.X, ALU.add))
            step(V.tensor_scalar(block_expert[:], expert_f, float(E0 - 1), None, ALU.min))
            step(V.tensor_tensor(index, index, passed, ALU.subtract))
            step(V.tensor_scalar_mul(index, index, float(P)))
            step(V.scalar_tensor_tensor(block_row[:], expert_f, float(REGION0), index, ALU.mult, ALU.add))

        @blk.tensor
        def _(pe):
            for name in "a_pT a_pQ a_pK a_pV a_pL a_pR a_pT1 a_pG r_counted".split():
                pe.sem_inc(s[name], SEED)
            pe.wait_ge(s["a_load"], 16 * n_load)
            pe.wait_ge(s["a_const"], 1)

            def count(u):
                if live(u, SUPERS):
                    pe.wait_ge(s["r_picks"], made(u))
                    flat, n = picks[:].rearrange("p e i -> p (e i)"), E0 * SUPER
                    nc.tensor.matmul(pC[:, 0:n], before[:], flat, start=True, stop=True)
                    nc.tensor.matmul(pC[:, n:2 * n], ones[:], flat, start=True, stop=True).then_inc(s["r_counted"], 1)

            def body(u):
                for half in range(2):
                    ns = [n for _, n in quads(u, half)]
                    for p, n in enumerate(ns):
                        pe.wait_ge(s["a_xn"], made(n))
                        pe.wait_ge(s["a_xT"], freed(n, 1))
                        if p == 0:
                            pe.wait_ge(s["a_x1T"], freed(n, 1))
                        for j in range(QUAD):
                            last = nc.tensor.transpose(pT[:, bass.ts(j, P)], xn[:, p, j, :], ident[:])
                        last.then_inc(s["a_pT"], 1)
                    for p, n in enumerate(ns):
                        pe.wait_ge(s["a_xT"], made(n))
                        pe.wait_ge(s["a_qT"], freed(n, 1))
                        nc.tensor.matmul(pQ[:], wq[:], xT[:, p, :], start=True, stop=True).then_inc(s["a_pQ"], 1)
                        pe.wait_ge(s["a_kT"], freed(n, 1))
                        nc.tensor.matmul(pK[:], wk[:], xT[:, p, :], start=True, stop=True).then_inc(s["a_pK"], 1)
                        pe.wait_ge(s["a_v"], freed(n, 1))
                        for j in range(QUAD):
                            last = nc.tensor.matmul(pV[:, bass.ts(j, D)], xT[:, p, bass.ts(j, P)], wv[:], start=True, stop=True)
                        last.then_inc(s["a_pV"], 1)
                    for p, n in enumerate(ns):
                        pe.wait_ge(s["a_kT"], made(n))
                        pe.wait_ge(s["a_qT"], made(n))
                        pe.wait_ge(s["a_lm"], freed(n, 1))
                        for j in range(QUAD):
                            last = nc.tensor.matmul(pL[:, bass.ts(j, P)], kT[:, p, bass.ts(j, P)], qT[:, p, bass.ts(j, P)],
                                                    start=True, stop=True)
                        last.then_inc(s["a_pL"], 1)
                    if half == 0:
                        count(u - 1)
                    for p, n in enumerate(ns):
                        pe.wait_ge(s["a_prob"], made(n))
                        pe.wait_ge(s["a_vs"], made(n))
                        pe.wait_ge(s["a_h1"], freed(n, 1))
                        for j in range(QUAD):
                            nc.tensor.matmul(pR[:, bass.ts(j, D)], ident[:], xn[:, p, j, :], start=True, stop=False)
                            last = nc.tensor.matmul(pR[:, bass.ts(j, D)], lm[:, p, j, :], v[:, p, j, :],
                                                    start=False, stop=True)
                        last.then_inc(s["a_pR"], 1)
                    for p, n in enumerate(ns):
                        pe.wait_ge(s["a_xn1"], made(n))
                        if p == 0:
                            pe.wait_ge(s["a_xT"], made(n + 1))
                        pe.wait_ge(s["a_x1T"], freed(n, 1))
                        for j in range(QUAD):
                            last = nc.tensor.transpose(pT[:, bass.ts(j, P)], xn1[:, p, j, :], ident[:])
                        last.then_inc(s["a_pT1"], 1)
                    for p, n in enumerate(ns):
                        pe.wait_ge(s["a_x1T"], made(n))
                        pe.wait_ge(s["a_logit"], freed(n, 1))
                        for j in range(QUAD):
                            last = nc.tensor.matmul(pG[:, j * 20:j * 20 + 20], qT[:, p, bass.ts(j, P)],
                                                    wr[:].rearrange("p g e -> p (g e)"), start=True, stop=True)
                        last.then_inc(s["a_pG"], 1)
            supers(pe, body, after=0)
            count(SUPERS - 1)

        @blk.scalar
        def _(act):
            for name in "a_xT a_qT a_kT a_prob a_x1T r_exp".split():
                act.sem_inc(s[name], SEED)
            act.wait_ge(s["a_load"], 16 * n_load)
            act.wait_ge(s["a_fillready"], 1)
            nc.scalar.activation(warm[:], filler[:, 0:1], ACT.Exp)

            def exponentials(u):
                if live(u, SUPERS):
                    act.wait_ge(s["r_max"], made(u))
                    nc.scalar.activation(prob4[:], work[:], ACT.Exp).then_inc(s["r_exp"], 1)

            def body(u):
                exponentials(u - 1)
                for half in range(2):
                    ns = [n for _, n in quads(u, half)]
                    for p, n in enumerate(ns):
                        act.wait_ge(s["a_pT"], made(n))
                        act.wait_ge(s["a_pV"], freed(n, 2))
                        nc.scalar.copy(xT[:, p, :], pT[:]).then_inc(s["a_xT"], 1)
                    for p, n in enumerate(ns):
                        act.wait_ge(s["a_pG"], freed(n, 2))
                        act.wait_ge(s["a_pQ"], made(n))
                        nc.scalar.activation(qT[:, p, :], pQ[:], ACT.Identity, bias=bq[:, 0:1]).then_inc(s["a_qT"], 1)
                        act.wait_ge(s["a_pK"], made(n))
                        nc.scalar.activation(kT[:, p, :], pK[:], ACT.Identity, bias=bk[:, 0:1]).then_inc(s["a_kT"], 1)
                    for p, n in enumerate(ns):
                        act.wait_ge(s["a_max"], made(n))
                        for j in range(QUAD):
                            last = nc.scalar.activation(lm[:, p, j, :], lm[:, p, j, :], ACT.Exp, bias=nmx[:, p, j:j + 1],
                                                        accum_out=psum[:, p, j:j + 1])
                        last.then_inc(s["a_prob"], 1)
                    for p, n in enumerate(ns):
                        act.wait_ge(s["a_pT1"], made(n))
                        act.wait_ge(s["a_pL"], made(n))
                        nc.scalar.copy(qT[:, p, :], pT[:]).then_inc(s["a_x1T"], 1)
            supers(act, body, after=0)
            exponentials(SUPERS - 1)


def layer0_experts(nc, sems, ps, ident, filler, block_expert, block_row, w1, w3, w2, XS0, YT0, XS1, YT1):
    ctx = ExitStack()
    CH = HID // P
    RING = 4
    with ctx:
        def sb(name, shape, dt=F32):
            return ctx.enter_context(nc.sbuf_tensor(name, shape, dt))
        x = sb("e_x", [P, RING, ROW])
        xT = sb("e_xT", [P, 2, P])
        w1s = sb("e_w1s", [P, 2, HID])
        w3s = sb("e_w3s", [P, 2, HID])
        place = sb("e_place", [P, RING], I32)
        share = sb("e_share", [P, RING])
        gate = sb("e_gate_t", [P, 2, CH, P])
        g = sb("e_g_t", [P, 2, CH, P])
        y = sb("e_y_t", [P, 2, D])
        warm = sb("e_warm", [P, 1])
        s = sems("e_pT e_xT e_w1s e_w3s e_p1 e_p3 e_gate e_g e_py e_y e_tags e_sent e_turn",
                 dma="e_x0 e_x1 e_x2 e_x3 e_filled e_out0 e_out1")
        landed = [s[f"e_x{r}"] for r in range(RING)]
        out = [s["e_out0"], s["e_out1"]]
        pT, py = ps[0], ps[1]
        p1, p3 = [ps[2], ps[3]], [ps[4], ps[5]]
        blk = ctx.enter_context(nc.Block())

        @blk.sync
        def _(sp):
            def body(n, k, i):
                row = sp.value_load(block_row[0:1, bass.ds(n, 1)], min_val=0, max_val=ROWS0 - P)
                wait_free(sp, s["e_pT"], n, RING)
                wait_free(sp, s["e_tags"], n, RING)
                sp.dma_start(x[:, k, :], XS0[bass.ds(row, P), :]).then_inc(landed[k], 16)
                if k == RING - 1:
                    for buffer, share, width in ((XS1, FILL_X, ROW), (YT1, FILL_Y, D)):
                        sp.dma_start(buffer[bass.ds(i * share, share), :].rearrange("(p a) r -> p a r", p=P),
                                     bc(filler[:, 0:width], 1, [P, share // P, width])).then_inc(s["e_filled"], 16)
            pipeline(sp, BLOCKS0, 0, 0, RING, body)
            sp.wait_ge(s["e_filled"], 2 * 16 * FILLS)

        @blk.gpsimd
        def _(pool):
            pool.sem_inc(s["e_sent"], SEED)

            def body(n, k, i):
                if live(n, BLOCKS0):
                    pool.wait_ge(s["e_y"], made(n))
                    turn(pool, s["e_turn"])
                    nc.gpsimd.indirect_dma_start(
                        out=YT0, out_offset=bass.IndirectOffsetOnAxis(ap=place[:, k:k + 1], axis=0), in_=y[:, k % 2, :],
                        in_offset=None, bounds_check=TOKENS * PICKS0 - 1, oob_is_err=False).then_inc(out[k % 2], 16)
                if live(n - 1, BLOCKS0):
                    pool.wait_ge(out[(k - 1) % 2], 16 * (2 * i + (k - 1) // 2 + 1))
                    pool.sem_inc(s["e_sent"], 1)
            pipeline(pool, BLOCKS0, 0, 1, RING, body)

        @blk.tensor
        def _(pe):
            for name in "e_pT e_p1 e_p3 e_py".split():
                pe.sem_inc(s[name], SEED)

            def body(n, k, i):
                if live(n, BLOCKS0):
                    p = k % 2
                    pe.wait_ge(s["e_xT"], made(n))
                    pe.wait_ge(s["e_w1s"], made(n))
                    wait_free(pe, s["e_gate"], n, 2)
                    for c in range(CH):
                        last = nc.tensor.matmul(p1[p][:, bass.ts(c, P)], w1s[:, p, bass.ts(c, P)], xT[:, p, :],
                                                start=True, stop=True)
                    last.then_inc(s["e_p1"], 1)
                    pe.wait_ge(s["e_w3s"], made(n))
                    wait_free(pe, s["e_g"], n, 2)
                    for c in range(CH):
                        last = nc.tensor.matmul(p3[p][:, bass.ts(c, P)], w3s[:, p, bass.ts(c, P)], xT[:, p, :],
                                                start=True, stop=True)
                    last.then_inc(s["e_p3"], 1)
                if live(n + 1, BLOCKS0):
                    m, r = n + 1, (k + 1) % RING
                    pe.wait_ge(landed[r], 16 * (i + (k + 1) // RING + 1))
                    wait_free(pe, s["e_xT"], m, 1)
                    nc.tensor.transpose(pT[:, 0:P], x[:, r, 0:D], ident[:]).then_inc(s["e_pT"], 1)
                if live(n - 1, BLOCKS0):
                    m, p = n - 1, (k - 1) % 2
                    expert = pe.value_load(block_expert[0:1, bass.ds(m, 1)], min_val=0, max_val=E0 - 1)
                    pe.wait_ge(s["e_g"], made(m))
                    wait_free(pe, s["e_y"], m, 1)
                    for c in range(CH):
                        last = nc.tensor.matmul(
                            py[:, 0:D], g[:, p, c, :], w2[:, bass.ds(expert, 1), c, :].rearrange("p o d -> p (o d)"),
                            start=(c == 0), stop=(c == CH - 1))
                    last.then_inc(s["e_py"], 1)
            pipeline(pe, BLOCKS0, 1, 1, RING, body)

        @blk.scalar
        def _(act):
            for name in "e_xT e_w1s e_gate".split():
                act.sem_inc(s[name], SEED)
            nc.scalar.activation(warm[:], ident[:, 0:1], ACT.Silu)

            def body(n, k, i):
                if live(n + 1, BLOCKS0):
                    m, p = n + 1, (k + 1) % 2
                    expert = act.value_load(block_expert[0:1, bass.ds(m, 1)], min_val=0, max_val=E0 - 1)
                    wait_free(act, s["e_p1"], m, 2)
                    nc.scalar.copy(w1s[:, p, :], w1[:, bass.ds(expert, 1), :].rearrange("p o h -> p (o h)")).then_inc(s["e_w1s"], 1)
                if live(n, BLOCKS0):
                    p = k % 2
                    act.wait_ge(s["e_p1"], made(n))
                    wait_free(act, s["e_g"], n, 2)
                    nc.scalar.activation(gate[:, p].rearrange("p c t -> p (c t)"), p1[p][:], ACT.Silu).then_inc(s["e_gate"], 1)
                if live(n + 1, BLOCKS0):
                    act.wait_ge(s["e_pT"], made(m))
                    wait_free(act, s["e_p3"], m, 2)
                    nc.scalar.copy(xT[:, 1 - k % 2, :], pT[:, 0:P]).then_inc(s["e_xT"], 1)
            pipeline(act, BLOCKS0, 1, 0, RING, body)

        @blk.vector
        def _(dve):
            for name in "e_w3s e_g e_y e_tags".split():
                dve.sem_inc(s[name], SEED)

            def body(n, k, i):
                if live(n + 1, BLOCKS0):
                    m, p = n + 1, (k + 1) % 2
                    expert = dve.value_load(block_expert[0:1, bass.ds(m, 1)], min_val=0, max_val=E0 - 1)
                    wait_free(dve, s["e_p3"], m, 2)
                    nc.vector.tensor_copy(w3s[:, p, :], w3[:, bass.ds(expert, 1), :].rearrange("p o h -> p (o h)")).then_inc(s["e_w3s"], 1)
                if live(n - 1, BLOCKS0):
                    m, p, r = n - 1, (k - 1) % 2, (k - 1) % RING
                    dve.wait_ge(landed[r], 16 * (i + (k - 1) // RING + 1))
                    wait_free(dve, s["e_sent"], m, RING)
                    wait_free(dve, s["e_y"], m, RING)
                    nc.vector.tensor_copy(share[:, r:r + 1], x[:, r, D:D + 1])
                    nc.vector.tensor_copy(place[:, r:r + 1], x[:, r, D + 1:ROW]).then_inc(s["e_tags"], 1)
                if live(n, BLOCKS0):
                    p = k % 2
                    dve.wait_ge(s["e_gate"], made(n))
                    dve.wait_ge(s["e_p3"], made(n))
                    wait_free(dve, s["e_py"], n, 2)
                    nc.vector.tensor_tensor(g[:, p].rearrange("p c t -> p (c t)"), gate[:, p].rearrange("p c t -> p (c t)"),
                                            p3[p][:], ALU.mult).then_inc(s["e_g"], 1)
                if live(n - 1, BLOCKS0):
                    dve.wait_ge(s["e_py"], made(m))
                    dve.wait_ge(s["e_tags"], made(m))
                    wait_free(dve, s["e_sent"], m, 2)
                    nc.vector.tensor_scalar(y[:, 1 - k % 2, :], py[:, 0:D], share[:, r:r + 1], None, ALU.mult).then_inc(s["e_y"], 1)
            pipeline(dve, BLOCKS0, 1, 1, RING, body)


def layer0_combine(nc, A, sems, ps, H, ident, wnT, YT0, BD):
    ctx = ExitStack()
    RING = 4
    with ctx:
        def sb(name, shape, dt=F32):
            return ctx.enter_context(nc.sbuf_tensor(name, shape, dt))
        power = sb("d_power", [P, QUAD])
        gamma, beta, rbias = sb("d_gamma", [P, 1]), sb("d_beta", [P, 1]), sb("d_rbias", [P, 1])
        wq, wr = sb("d_wq", [P, D]), sb("d_wr", [P, D])
        angles = sb("d_angles", [P, TILES])
        headmask = sb("d_headmask", [P, HEADS])
        rk = sb("d_rk", [P, TILES])
        window = sb("d_window", [P, 2, HEADS, 2 * TILES])
        got = sb("d_got", [P, RING, QUAD, PICKS0, D])
        acc = sb("d_acc", [P, 2, QUAD, D])
        st, mv, ve, rstd = (sb("d_st", [P, 2, QUAD, 6]), sb("d_mv", [P, 2, QUAD, 2]), sb("d_ve", [P, 2, QUAD]),
                            sb("d_rstd", [P, 2, QUAD]))
        st2, mv2, ve2, rstd2 = (sb("d_st2", [P, 2, QUAD, 6]), sb("d_mv2", [P, 2, QUAD, 2]),
                                sb("d_ve2", [P, 2, QUAD]), sb("d_rstd2", [P, 2, QUAD]))
        w = sb("d_w", [P, 2, QUAD, D])
        wn = sb("d_wn", [P, 2, QUAD, D])
        wT = sb("d_wT", [P, 2, QUAD, P])
        q = sb("d_q", [P, 2, QUAD, P])
        pos = sb("d_pos", [P, QUAD, HEADS * TILES])
        s = sems("d_const d_const2 d_rk d_rks d_window d_two d_acc d_acck d_st d_mv d_ve d_rstd d_w d_st2 "
                 "d_mv2 d_ve2 d_rstd2 d_wn d_pT d_wT d_wnT d_h d_pQ d_q d_pB d_pos d_pos_odd d_turn d_poolturn "
                 "d_peturn",
                 dma="d_load d_got0 d_got1 d_got2 d_got3 d_out0 d_out1 d_out2 d_out3")
        Y = YT0.rearrange("(i t k) d -> t i (k d)", t=P, k=PICKS0)
        got_in, kept = [s[f"d_got{r}"] for r in range(RING)], [s[f"d_out{r}"] for r in range(QUAD)]
        pT, pQ, pR, pB = ps[0], ps[1], ps[2], ps[4:8]
        COUNT = TILES // QUAD
        n_load = 6
        blk = ctx.enter_context(nc.Block())

        @blk.sync
        def _(sp):
            for dst, src in ((gamma[:], A["L1_attn_ln_gamma"].unsqueeze(1)), (beta[:], A["L1_attn_ln_beta"].unsqueeze(1)),
                             (rbias[:], A["L1_attn_r_r_bias"].rearrange("n (d o) -> (n d) o", o=1)),
                             (wq[:], A["L1_attn_Wqkv"][:, 0:D]), (wr[:], A["L1_attn_Wr"]), (angles[:], A["positions"])):
                sp.dma_start(dst, src).then_inc(s["d_load"], 16)

            def body(n, k, i):
                m = n + RING - 1
                if live(m, COUNT):
                    r = (k + RING - 1) % RING
                    wait_free(sp, s["d_acc"], m, RING)
                    sp.dma_start(got[:, r].rearrange("t i k d -> t i (k d)"),
                                 Y[:, bass.ds(m * QUAD, QUAD), :]).then_inc(got_in[r], 16)
                if live(n - 1, COUNT):
                    for j in range(QUAD):
                        made_by = s["d_pos_odd"] if j % 2 else s["d_pos"]
                        sp.wait_ge(made_by, made(2 * (n - 1) + j // 2))
                        sp.dma_start(BD[:, bass.ds((n - 1) * QUAD + j, 1), :].rearrange("b o c -> b (o c)"),
                                     pos[:, j, :]).then_inc(kept[j], 16)
            for n in range(-(RING - 1), RING):
                body(n, n % RING, n // RING)
            with sp.Fori(1, COUNT // RING - 1) as i:
                for k in range(RING):
                    body(i * RING + k, k, i)
            for n in range(COUNT - RING, COUNT + 1):
                body(n, n % RING, n // RING)
            sp.wait_ge(s["d_pos"], made(TILES // 2))
            sp.dma_start(BD[:, TILES, :], pos[:, 0, :]).then_inc(kept[0], 16)
            for j in range(QUAD):
                sp.wait_ge(kept[j], 16 * (COUNT + (j == 0)))

        @blk.gpsimd
        def _(pool):
            for name in "d_two d_rstd d_rstd2 d_h d_wnT".split():
                pool.sem_inc(s[name], SEED)
            nc.gpsimd.memset(power[:], -0.5)
            nc.gpsimd.memset(window[:], 0.0)
            nc.gpsimd.memset(q[:], 0.0)
            nc.gpsimd.memset(headmask[:], 1.0).then_inc(s["d_const"], 1)
            pool.wait_ge(s["d_const"], 1)
            nc.gpsimd.affine_select(out=headmask[:], in_=headmask[:], compare_op=ALU.is_ge, fill=0.0, base=0,
                                    pattern=[[-DH, HEADS]], channel_multiplier=1).then_inc(s["d_const"], 1)
            pool.wait_ge(s["d_const"], 2)
            nc.gpsimd.affine_select(out=headmask[:], in_=headmask[:], compare_op=ALU.is_ge, fill=0.0, base=DH - 1,
                                    pattern=[[DH, HEADS]], channel_multiplier=-1).then_inc(s["d_const"], 1)

            def body(n, k, i):
                p = k % 2
                if live(n - 1, COUNT):
                    pool.wait_ge(s["d_wT"], made(n - 1))
                    turn(pool, s["d_poolturn"])
                    nc.gpsimd.tensor_copy(wnT[:, :, bass.ds((n - 1) * QUAD, QUAD)],
                                          wT[:, 1 - p].rearrange("d i b -> d b i")).then_inc(s["d_wnT"], 1)
                if live(n, COUNT):
                    pool.wait_ge(s["d_ve"], made(n))
                    nc.gpsimd.tensor_tensor(rstd[:, p, :], ve[:, p, :], power[:], ALU.pow).then_inc(s["d_rstd"], 1)
                if live(n + 1, COUNT):
                    r = (k + 1) % RING
                    pool.wait_ge(got_in[r], 16 * (i + (k + 1) // RING + 1))
                    nc.gpsimd.tensor_tensor(got[:, r, :, 0:2, :], got[:, r, :, 0:2, :], got[:, r, :, 2:4, :],
                                            ALU.add).then_inc(s["d_two"], 1)
                if live(n, COUNT):
                    pool.wait_ge(s["d_ve2"], made(n))
                    nc.gpsimd.tensor_tensor(rstd2[:, p, :], ve2[:, p, :], power[:], ALU.pow).then_inc(s["d_rstd2"], 1)
                    pool.wait_ge(s["d_w"], made(n))
                    turn(pool, s["d_poolturn"])
                    nc.gpsimd.tensor_tensor(H[:, bass.ds(n * QUAD, QUAD), :], acc[:, p], w[:, p],
                                            ALU.add).then_inc(s["d_h"], 1)
            pipeline(pool, COUNT, 1, 1, RING, body)

        @blk.vector
        def _(dve):
            for name in "d_acc d_acck d_st d_mv d_ve d_w d_st2 d_mv2 d_ve2 d_wn d_pos".split():
                dve.sem_inc(s[name], SEED)
            dve.wait_ge(s["d_const"], 3)
            dve.wait_ge(s["d_rk"], 1)
            nc.vector.tensor_copy(rk[:], pR[:, 0:TILES]).then_inc(s["d_rks"], 1)
            dve.wait_ge(s["d_rks"], 1)
            for k, at in ((0, 0), (1, TILES + 1)):
                width = min(TILES, 2 * TILES - at)
                nc.vector.tensor_tensor(window[:, k, :, at:at + width], bc(rk[:, 0:width], 1, [P, HEADS, width]),
                                        bc(headmask[:], 2, [P, HEADS, width]), ALU.mult).then_inc(s["d_window"], 1)

            def stats(n, p, x, st, mv, ve, tag):
                turn(dve, s["d_turn"])
                for j in range(QUAD):
                    last = nc.vector.bn_stats(st[:, p, j, :], x[:, p, j, :])
                last.then_inc(s["d_st" + tag], 1)
                dve.wait_ge(s["d_st" + tag], made(n))
                turn(dve, s["d_turn"])
                for j in range(QUAD):
                    last = nc.vector.bn_aggr(mv[:, p, j, :], st[:, p, j, :])
                last.then_inc(s["d_mv" + tag], 1)
                dve.wait_ge(s["d_mv" + tag], made(n))
                nc.vector.tensor_scalar_add(ve[:, p, :], mv[:, p, :, 1], EPS).then_inc(s["d_ve" + tag], 1)

            def even_row(n, i, j):
                if live(n - 1, COUNT):
                    dve.wait_ge(s["d_pB"], made((n - 1) * QUAD + j))
                    if not isinstance(n, int) or n > 1:
                        dve.wait_ge(kept[j], 16 * (n - 1))
                    nc.vector.tensor_copy(pos[:, j, :], pB[j][:]).then_inc(s["d_pos"], 1)

            def body(n, k, i):
                p = k % 2
                if live(n, COUNT):
                    wait_free(dve, s["d_h"], n, 2)
                    dve.wait_ge(s["d_two"], made(n))
                    nc.vector.tensor_tensor(acc[:, p], got[:, k, :, 0, :], got[:, k, :, 1, :], ALU.add).then_inc(s["d_acck"], 1)
                    dve.wait_ge(s["d_acck"], made(n))
                    nc.vector.tensor_tensor(acc[:, p], acc[:, p], H[:, bass.ds(n * QUAD, QUAD), :], ALU.add).then_inc(s["d_acc"], 1)
                    dve.wait_ge(s["d_acc"], made(n))
                    stats(n, p, acc, st, mv, ve, "")
                even_row(n, i, 0)
                if live(n, COUNT):
                    dve.wait_ge(s["d_rstd"], made(n))
                    for j in range(QUAD):
                        last = nc.vector.tensor_scalar(w[:, p, j, :], acc[:, p, j, :], mv[:, p, j, 0:1], rstd[:, p, j:j + 1],
                                                       ALU.subtract, ALU.mult)
                    last.then_inc(s["d_w"], 1)
                    dve.wait_ge(s["d_w"], made(n))
                    stats(n, p, w, st2, mv2, ve2, "2")
                even_row(n, i, 2)
                if live(n, COUNT):
                    dve.wait_ge(s["d_rstd2"], made(n))
                    wait_free(dve, s["d_pT"], n, 2)
                    for j in range(QUAD):
                        last = nc.vector.tensor_scalar(wn[:, p, j, :], w[:, p, j, :], mv2[:, p, j, 0:1], rstd2[:, p, j:j + 1],
                                                       ALU.subtract, ALU.mult)
                    last.then_inc(s["d_wn"], 1)
            pipeline(dve, COUNT, 0, 1, RING, body)
            dve.wait_ge(s["d_pB"], made(TILES))
            dve.wait_ge(kept[0], 16 * COUNT)
            nc.vector.tensor_copy(pos[:, 0, :], pB[0][:]).then_inc(s["d_pos"], 1)

        @blk.tensor
        def _(pe):
            for name in "d_pT d_pQ d_pB".split():
                pe.sem_inc(s[name], SEED)
            pe.wait_ge(s["d_load"], 16 * n_load)
            nc.tensor.matmul(pR[:, 0:TILES], wr[:], angles[:], start=True, stop=True).then_inc(s["d_rk"], 1)
            pe.wait_ge(s["d_window"], 2)

            def body(n, k, i):
                p = k % 2
                if live(n - 1, COUNT):
                    pe.wait_ge(s["d_q"], made(n - 1))
                    for j in range(QUAD):
                        m = (n - 1) * QUAD + j
                        wait_free(pe, s["d_pos_odd"] if j % 2 else s["d_pos"], 2 * (n - 1) + j // 2, 2)
                        turn(pe, s["d_peturn"])
                        prev = q[:, 1 - p, j - 1, :] if j else q[:, p, QUAD - 1, :]
                        nc.tensor.matmul(pB[j][:], prev, window[:, 0, :, bass.ds(TILES - m, TILES)],
                                         start=True, stop=False)
                        nc.tensor.matmul(pB[j][:], q[:, 1 - p, j, :], window[:, 1, :, bass.ds(TILES - m, TILES)],
                                         start=False, stop=True).then_inc(s["d_pB"], 1)
                if live(n, COUNT):
                    pe.wait_ge(s["d_wn"], made(n))
                    wait_free(pe, s["d_wT"], n, 1)
                    for j in range(QUAD):
                        last = nc.tensor.transpose(pT[:, bass.ts(j, P)], wn[:, p, j, :], ident[:])
                    last.then_inc(s["d_pT"], 1)
                    pe.wait_ge(s["d_wT"], made(n))
                    wait_free(pe, s["d_q"], n, 1)
                    nc.tensor.matmul(pQ[:], wq[:], wT[:, p].rearrange("d i b -> d (i b)"),
                                     start=True, stop=True).then_inc(s["d_pQ"], 1)
            pipeline(pe, COUNT, 0, 1, RING, body)
            pe.wait_ge(s["d_pos"], freed(TILES // 2, 2))
            nc.tensor.matmul(pB[0][:], q[:, 1, QUAD - 1, :], window[:, 0, :, 0:TILES],
                             start=True, stop=True).then_inc(s["d_pB"], 1)

        @blk.scalar
        def _(act):
            for name in "d_wT d_q d_pos_odd".split():
                act.sem_inc(s[name], SEED)
            act.wait_ge(s["d_load"], 16 * n_load)
            act.wait_ge(s["d_const"], 3)

            def body(n, k, i):
                p = k % 2
                if live(n - 1, COUNT):
                    for j in (1, 3):
                        act.wait_ge(s["d_pB"], made((n - 1) * QUAD + j))
                        if not isinstance(n, int) or n > 1:
                            act.wait_ge(kept[j], 16 * (n - 1))
                        nc.scalar.copy(pos[:, j, :], pB[j][:]).then_inc(s["d_pos_odd"], 1)
                if live(n, COUNT):
                    act.wait_ge(s["d_pT"], made(n))
                    wait_free(act, s["d_pQ"], n, 2)
                    wait_free(act, s["d_wnT"], n, 2)
                    nc.scalar.activation(wT[:, p].rearrange("d i b -> d (i b)"), pT[:], ACT.Identity, bias=beta[:, 0:1],
                                         scale=gamma[:, 0:1]).then_inc(s["d_wT"], 1)
                    act.wait_ge(s["d_pQ"], made(n))
                    if not isinstance(n, int) or n > 0:
                        act.wait_ge(s["d_pB"], made((n - 1) * QUAD))
                    nc.scalar.activation(q[:, p].rearrange("d i b -> d (i b)"), pQ[:], ACT.Identity,
                                         bias=rbias[:, 0:1]).then_inc(s["d_q"], 1)
            pipeline(act, COUNT, 0, 1, RING, body)


def layer1_attention(nc, A, sems, ps, ident, wnT, readT, BD):
    ctx = ExitStack()
    OCT = 8
    LEAD = 4
    with ctx:
        def sb(name, shape, dt=F32):
            return ctx.enter_context(nc.sbuf_tensor(name, shape, dt))
        wq, wk, wv = sb("f_wq", [P, D]), sb("f_wk", [P, D]), sb("f_wv", [P, D])
        wbias = sb("f_wbias", [P, 1])
        headmask = sb("f_headmask", [P, HEADS])
        halfmask = sb("f_halfmask", [P, 2])
        q = sb("f_q", [P, 2, OCT, TILES])
        kk = sb("f_k", [P, 2, OCT, TILES])
        x = sb("f_x", [P, 2, OCT, 2, TILES])
        kh = sb("f_kh", [P, 2, 2, HEADS, TILES])
        vh = sb("f_vh", [P, 2, 2, HEADS // 2, 2, DH])
        bd = sb("f_bd", [P, 4, HEADS, TILES])
        S = sb("f_S", [P, 2, HEADS, TILES])
        warm = sb("f_warm", [P, 1])
        mx = sb("f_mx", [P, 2, HEADS])
        E = sb("f_E", [P, 2, HEADS, TILES])
        den = sb("f_den", [P, 2, HEADS])
        rden = sb("f_rden", [P, 2, HEADS])
        ET = sb("f_ET", [P, 2, HEADS // 2, P])
        O = sb("f_O", [P, 2, D])
        s = sems("f_const f_pQ f_pK f_q f_k f_x f_kh f_pV f_vh f_pS f_S f_mx f_sub f_E f_den f_rden f_pE "
                 "f_ET f_pO f_O f_pOT f_read",
                 dma="f_load f_bd0 f_bd1 f_bd2 f_bd3")
        bd_in = [s[f"f_bd{r}"] for r in range(4)]
        pQ, pK, pV, pS, pE, pO = ps[0], ps[1], ps[2], [ps[3], ps[4]], ps[5], ps[6]
        pOT = ps[7]
        n_load = 4
        PAIRS = OCT // 2
        COUNT = P // 2
        TWO = 2 * PAIRS
        blk = ctx.enter_context(nc.Block())

        def shifted(n, k, i, by):
            slot = (k + by) % TWO
            turn_ = i + (k + by) // TWO
            return n + by, slot, 2 * turn_ + slot // PAIRS, slot % 2

        @blk.sync
        def _(sp):
            for dst, src in ((wq[:], A["L1_attn_Wqkv"][:, 0:D]), (wk[:], A["L1_attn_Wqkv"][:, D:2 * D]),
                             (wv[:], A["L1_attn_Wqkv"][:, 2 * D:3 * D]),
                             (wbias[:], A["L1_attn_r_w_bias"].rearrange("n (d o) -> (n d) o", o=1))):
                sp.dma_start(dst, src).then_inc(s["f_load"], 16)

            def body(n, k, i):
                p = k % 4
                wait_free(sp, s["f_S"], n, 4)
                for h in range(2):
                    sp.dma_start(bd[h * TILES:(h + 1) * TILES, p].rearrange("i n j -> i (n j)"),
                                 BD[bass.ds(2 * n + h, 1), 1:, :].rearrange("o i c -> (o i) c")).then_inc(bd_in[p], 16)
            pipeline(sp, COUNT, 0, 0, TWO, body)

        @blk.gpsimd
        def _(pool):
            for name in "f_kh f_sub".split():
                pool.sem_inc(s[name], SEED)
            nc.gpsimd.memset(headmask[:], 1.0)
            nc.gpsimd.memset(halfmask[:], 1.0).then_inc(s["f_const"], 1)
            pool.wait_ge(s["f_const"], 1)
            nc.gpsimd.affine_select(out=headmask[:], in_=headmask[:], compare_op=ALU.is_ge, fill=0.0, base=0,
                                    pattern=[[-DH, HEADS]], channel_multiplier=1)
            nc.gpsimd.affine_select(out=halfmask[:], in_=halfmask[:], compare_op=ALU.is_ge, fill=0.0, base=0,
                                    pattern=[[-TILES, 2]], channel_multiplier=1).then_inc(s["f_const"], 1)
            pool.wait_ge(s["f_const"], 2)
            nc.gpsimd.affine_select(out=headmask[:], in_=headmask[:], compare_op=ALU.is_ge, fill=0.0, base=DH - 1,
                                    pattern=[[DH, HEADS]], channel_multiplier=-1)
            nc.gpsimd.affine_select(out=halfmask[:], in_=halfmask[:], compare_op=ALU.is_ge, fill=0.0, base=TILES - 1,
                                    pattern=[[TILES, 2]], channel_multiplier=-1).then_inc(s["f_const"], 1)
            pool.wait_ge(s["f_const"], 3)

            def body(n, k, i):
                m, slot, grp, p = shifted(n, k, i, 2)
                if live(m, COUNT):
                    if slot % PAIRS == 0:
                        pool.wait_ge(s["f_k"], made(grp))
                    wait_free(pool, s["f_pS"], m, 2)
                    for h in range(2):
                        last = nc.gpsimd.tensor_tensor(
                            kh[:, p, h], bc(kk[:, slot // PAIRS, 2 * (slot % PAIRS) + h, :], 1, [P, HEADS, TILES]),
                            bc(headmask[:], 2, [P, HEADS, TILES]), ALU.mult)
                    last.then_inc(s["f_kh"], 1)
                m, slot, grp, p = shifted(n, k, i, 1)
                if live(m, COUNT):
                    pool.wait_ge(s["f_mx"], made(m))
                    nc.gpsimd.tensor_tensor(S[:, p], S[:, p], bc(mx[:, p, :], 2, [P, HEADS, TILES]),
                                            ALU.subtract).then_inc(s["f_sub"], 1)
            pipeline(pool, COUNT, 2, 0, TWO, body)

        @blk.scalar
        def _(act):
            for name in "f_q f_k f_x f_E f_ET".split():
                act.sem_inc(s[name], SEED)
            act.wait_ge(s["f_load"], 16 * n_load)
            nc.scalar.activation(warm[:], ident[:, 0:1], ACT.Exp)

            def body(n, k, i):
                m, slot, grp, p = shifted(n, k, i, 0)
                if live(m, COUNT):
                    act.wait_ge(s["f_pE"], made(m))
                    wait_free(act, s["f_pO"], m, 2)
                    nc.scalar.copy(ET[:, p].rearrange("p c t -> p (c t)"), pE[:]).then_inc(s["f_ET"], 1)
                m, slot, grp, p = shifted(n, k, i, LEAD)
                if live(m, COUNT) and slot % PAIRS == 0:
                    two = slot // PAIRS
                    pairs_before = m
                    act.wait_ge(s["f_pQ"], made(grp))
                    wait_free(act, s["f_pS"], pairs_before, TWO - PAIRS + 1)
                    nc.scalar.activation(q[:, two].rearrange("d b i -> d (b i)"), pQ[:], ACT.Identity,
                                         bias=wbias[:, 0:1]).then_inc(s["f_q"], 1)
                    act.wait_ge(s["f_pK"], made(grp))
                    wait_free(act, s["f_kh"], pairs_before, TWO - PAIRS + 1)
                    nc.scalar.copy(kk[:, two].rearrange("d b i -> d (b i)"), pK[:]).then_inc(s["f_k"], 1)
                    wait_free(act, s["f_pV"], pairs_before, TWO - PAIRS + 1)
                    cols = wnT[:, bass.ds(grp * OCT, OCT), :]
                    nc.scalar.copy(x[:, two, :, 0, :], cols)
                    nc.scalar.copy(x[:, two, :, 1, :], cols).then_inc(s["f_x"], 1)
                m, slot, grp, p = shifted(n, k, i, 1)
                if live(m, COUNT):
                    act.wait_ge(s["f_sub"], made(m))
                    wait_free(act, s["f_pE"], m, 2)
                    wait_free(act, s["f_den"], m, 2)
                    nc.scalar.activation(E[:, p], S[:, p], ACT.Exp, scale=DH ** -0.5).then_inc(s["f_E"], 1)
            pipeline(act, COUNT, LEAD, 0, TWO, body)

        @blk.vector
        def _(dve):
            for name in "f_vh f_S f_mx f_den f_rden f_O f_read".split():
                dve.sem_inc(s[name], SEED)
            dve.wait_ge(s["f_const"], 3)

            def body(n, k, i):
                m, slot, grp, p = shifted(n, k, i, 1)
                if live(m, COUNT):
                    dve.wait_ge(s["f_pS"], made(m))
                    dve.wait_ge(bd_in[slot % 4], 32 * (TWO // 4 * (i + (k + 1) // TWO) + slot // 4 + 1))
                    wait_free(dve, s["f_E"], m, 2)
                    nc.vector.tensor_tensor(S[:, p].rearrange("p n j -> p (n j)"), pS[p][:],
                                            bd[:, slot % 4].rearrange("p n j -> p (n j)"), ALU.add).then_inc(s["f_S"], 1)
                    dve.wait_ge(s["f_S"], made(m))
                    wait_free(dve, s["f_sub"], m, 2)
                    nc.vector.tensor_reduce(mx[:, p, :], S[:, p], AX.X, ALU.max).then_inc(s["f_mx"], 1)
                m, slot, grp, p = shifted(n, k, i, -1)
                if live(m, COUNT):
                    dve.wait_ge(s["f_pO"], made(m))
                    wait_free(dve, s["f_pOT"], m, 2)
                    dve.wait_ge(s["f_rden"], made(m))
                    nc.vector.tensor_tensor(O[:, p].rearrange("p (n d) -> p n d", n=HEADS),
                                            pO[:, 0:D].rearrange("p (n d) -> p n d", n=HEADS),
                                            bc(rden[:, p, :], 2, [P, HEADS, DH]), ALU.mult).then_inc(s["f_O"], 1)
                m, slot, grp, p = shifted(n, k, i, 0)
                if live(m, COUNT):
                    dve.wait_ge(s["f_pV"], made(m))
                    wait_free(dve, s["f_pO"], m, 2)
                    nc.vector.tensor_tensor(vh[:, p].rearrange("p b c h d -> p (b c) h d"),
                                            pV[:, 0:2 * D].rearrange("p (c h d) -> p c h d", h=2, d=DH),
                                            halfmask[:].unsqueeze(1).unsqueeze(3).to_broadcast([P, HEADS, 2, DH]),
                                            ALU.mult).then_inc(s["f_vh"], 1)
                    dve.wait_ge(s["f_E"], made(m))
                    wait_free(dve, s["f_rden"], m, 2)
                    nc.vector.tensor_reduce(den[:, p, :], E[:, p], AX.X, ALU.add).then_inc(s["f_den"], 1)
                    dve.wait_ge(s["f_den"], made(m))
                    wait_free(dve, s["f_O"], m, 2)
                    nc.vector.reciprocal(rden[:, p, :], den[:, p, :]).then_inc(s["f_rden"], 1)
                m, slot, grp, p = shifted(n, k, i, -2)
                if live(m, COUNT):
                    dve.wait_ge(s["f_pOT"], made(m))
                    nc.vector.tensor_copy(readT[:, bass.ds(2 * m, 2), :].rearrange("p b i -> p (b i)"),
                                          pOT[:, 0:P]).then_inc(s["f_read"], 1)
            pipeline(dve, COUNT, 1, 2, TWO, body)

        @blk.tensor
        def _(pe):
            for name in "f_pQ f_pK f_pV f_pS f_pE f_pO f_pOT".split():
                pe.sem_inc(s[name], SEED)
            pe.wait_ge(s["f_load"], 16 * n_load)

            def body(n, k, i):
                m, slot, grp, p = shifted(n, k, i, 1)
                if live(m, COUNT):
                    if slot % PAIRS == 0:
                        pe.wait_ge(s["f_q"], made(grp))
                    pe.wait_ge(s["f_kh"], made(m))
                    wait_free(pe, s["f_S"], m, 2)
                    for h in range(2):
                        last = nc.tensor.matmul(pS[p][h * TILES:(h + 1) * TILES, :],
                                                q[:, slot // PAIRS, 2 * (slot % PAIRS) + h, :],
                                                kh[:, p, h].rearrange("d n j -> d (n j)"), start=True, stop=True)
                    last.then_inc(s["f_pS"], 1)
                m, slot, grp, p = shifted(n, k, i, LEAD + 1)
                if live(m, COUNT) and slot % PAIRS == 0:
                    cols = wnT[:, bass.ds(grp * OCT, OCT), :].rearrange("d b i -> d (b i)")
                    wait_free(pe, s["f_q"], grp, 1)
                    nc.tensor.matmul(pQ[:], wq[:], cols, start=True, stop=True).then_inc(s["f_pQ"], 1)
                    wait_free(pe, s["f_k"], grp, 1)
                    nc.tensor.matmul(pK[:], wk[:], cols, start=True, stop=True).then_inc(s["f_pK"], 1)
                m, slot, grp, p = shifted(n, k, i, 0)
                if live(m, COUNT):
                    if slot % PAIRS == 0:
                        pe.wait_ge(s["f_x"], made(grp))
                    wait_free(pe, s["f_vh"], m, 1)
                    for h in range(2):
                        last = nc.tensor.matmul(pV[:, h * D:(h + 1) * D],
                                                x[:, slot // PAIRS, 2 * (slot % PAIRS) + h].rearrange("d a i -> d (a i)"),
                                                wv[:], start=True, stop=True)
                    last.then_inc(s["f_pV"], 1)
                m, slot, grp, p = shifted(n, k, i, -1)
                if live(m, COUNT):
                    pe.wait_ge(s["f_ET"], made(m))
                    pe.wait_ge(s["f_vh"], made(m))
                    wait_free(pe, s["f_O"], m, 1)
                    for h in range(2):
                        for c in range(HEADS // 2):
                            last = nc.tensor.matmul(pO[h * TILES:(h + 1) * TILES, c * 2 * DH:(c + 1) * 2 * DH],
                                                    ET[:, p, c, h * TILES:(h + 1) * TILES],
                                                    vh[:, p, h, c].rearrange("p h d -> p (h d)"), start=True, stop=True)
                    last.then_inc(s["f_pO"], 1)
                m, slot, grp, p = shifted(n, k, i, 0)
                if live(m, COUNT):
                    pe.wait_ge(s["f_E"], made(m))
                    wait_free(pe, s["f_ET"], m, 1)
                    for c in range(HEADS // 2):
                        last = nc.tensor.transpose(pE[:, bass.ts(c, P)],
                                                   E[:, p, 2 * c:2 * c + 2, :].rearrange("p n j -> p (n j)"), ident[:])
                    last.then_inc(s["f_pE"], 1)
                m, slot, grp, p = shifted(n, k, i, -2)
                if live(m, COUNT):
                    pe.wait_ge(s["f_O"], made(m))
                    wait_free(pe, s["f_read"], m, 1)
                    nc.tensor.transpose(pOT[:, 0:P], O[:, p, :], ident[:]).then_inc(s["f_pOT"], 1)
            pipeline(pe, COUNT, LEAD + 1, 2, TWO, body)


def route_buckets(V, step, dve, s, u, score, y, low, low_i, over, bucket, expert, hot, count, fresh, total, place, work,
                  at, carry, ps, slot_of, extra_of, dest):
    slot = slot_of[:, bass.ds(u, 1)].rearrange("p o i k -> p (o i) k")
    extra = extra_of[:, bass.ds(u, 1)].rearrange("p o i k c -> p (o i) k c")
    n = E1 * SUPER

    def floor(to, of):
        step(V.tensor_copy(low_i[:], of))
        step(V.tensor_copy(low[:], low_i[:]))
        step(V.tensor_tensor(over[:], low[:], of, ALU.is_gt))
        step(V.tensor_tensor(to, low[:], over[:], ALU.subtract))
    step(V.tensor_scalar_mul(y[:], score[:], 8.0))
    floor(bucket[:], y[:])
    step(V.tensor_scalar_mul(y[:], bucket[:], 1.0 / E1))
    floor(at[:], y[:])
    step(V.scalar_tensor_tensor(bucket[:], at[:], -float(E1), bucket[:], ALU.mult, ALU.add))
    for k in range(PICKS1):
        step(V.tensor_tensor(hot[:, k], bc(bucket[:, :, k], 1, [P, E1, SUPER]), bc(expert[:], 2, [P, E1, SUPER]),
                             ALU.is_equal))
    V.tensor_tensor(count[:], hot[:, 0], hot[:, 1], ALU.add).then_inc(s["h_count"], 1)
    yield
    dve.wait_ge(s["h_counted"], made(u))
    flat = place[:].rearrange("p e i -> p (e i)")
    for c in range(n // 512):
        last = V.tensor_copy(total[:].rearrange("p e i -> p (e i)")[:, bass.ts(c, 512)], ps[n // 512 + c][:])
    step(last)
    step(V.tensor_tensor_scan(flat, fresh[:].rearrange("p e i -> p (e i)"), total[:].rearrange("p e i -> p (e i)"),
                              0.0, ALU.mult, ALU.add))
    step(V.tensor_copy(work[:, :, 0], place[:, :, SUPER - 1]))
    step(V.tensor_tensor(place[:], place[:], total[:], ALU.subtract))
    for c in range(n // 512):
        last = V.tensor_tensor(flat[:, bass.ts(c, 512)], flat[:, bass.ts(c, 512)], ps[c][:], ALU.add)
    step(last)
    step(V.tensor_tensor(place[:], place[:], bc(carry[:], 2, [P, E1, SUPER]), ALU.add))
    step(V.tensor_tensor(carry[:], carry[:], work[:, :, 0], ALU.add))
    yield
    for k in range(PICKS1):
        step(V.tensor_tensor(work[:], place[:], hot[:, k], ALU.mult))
        step(V.tensor_reduce(at[:, :, k], work[:].rearrange("p e i -> p i e"), AX.X, ALU.add))
    step(V.tensor_tensor(over[:, :, 0], bucket[:, :, 0], bucket[:, :, 1], ALU.is_equal))
    step(V.tensor_tensor(at[:, :, 1], at[:, :, 1], over[:, :, 0], ALU.add))
    step(V.tensor_scalar(over[:], at[:], float(CAP1), None, ALU.is_ge))
    step(V.scalar_tensor_tensor(y[:], bucket[:], float(CAP1), at[:], ALU.mult, ALU.add))
    step(V.scalar_tensor_tensor(slot[:], over[:], NOWHERE, y[:], ALU.mult, ALU.add))
    step(V.tensor_copy(extra[:, :, :, 1], dest[:]))
    V.tensor_scalar_add(dest[:], dest[:], float(SUPER * P * PICKS1)).then_inc(s["h_slots"], 1)
    dve.wait_ge(s["h_slots"], made(u))


def layer1_project(nc, A, sems, ps, H, ident, before, ones, readT, XN3, XS1):
    ctx = ExitStack()
    with ctx:
        def sb(name, shape, dt=F32):
            return ctx.enter_context(nc.sbuf_tensor(name, shape, dt))
        power = sb("g_power", [P, QUAD])
        wo = sb("g_wo", [P, D])
        wh = sb("g_wh", [P, PICKS1])
        r = sb("g_r", [P, 2, QUAD, P])
        st, mv, ve, rstd = (sb("g_st", [P, 2, QUAD, 6]), sb("g_mv", [P, 2, QUAD, 2]), sb("g_ve", [P, 2, QUAD]),
                            sb("g_rstd", [P, 2, QUAD]))
        xn = sb("g_xn", [P, 2, QUAD, D])
        xT = sb("g_xT", [P, 2, QUAD * P])
        score = sb("g_score_t", [P, SUPER, PICKS1])
        y = sb("h_y", [P, SUPER, PICKS1])
        low = sb("h_low", [P, SUPER, PICKS1])
        low_i = sb("h_low_i", [P, SUPER, PICKS1], I32)
        over = sb("h_over", [P, SUPER, PICKS1])
        bucket = sb("h_bucket", [P, SUPER, PICKS1])
        expert = sb("h_expert", [P, E1])
        hot = sb("h_hot", [P, PICKS1, E1, SUPER], BF16)
        count = sb("h_count_t", [P, E1, SUPER], BF16)
        fresh = sb("h_fresh", [P, E1, SUPER])
        total = sb("h_total", [P, E1, SUPER])
        place = sb("h_place", [P, E1, SUPER])
        work = sb("h_work", [P, E1, SUPER])
        at = sb("h_at", [P, SUPER, PICKS1])
        carry = sb("h_carry", [P, E1])
        slot = sb("h_slot", [P, SUPERS, SUPER, PICKS1], I32)
        extra = sb("h_extra", [P, SUPERS, SUPER, PICKS1, 2])
        dest = sb("h_dest", [P, SUPER, PICKS1])
        sidx = sb("g_sidx", [P, 2, QUAD, PICKS1], I32)
        rows = sb("g_rows", [P, 2, QUAD, PICKS1, ROW])
        s = sems("g_const g_r g_pA g_h g_st g_mv g_ve g_rstd g_xn g_pT g_xT g_pG g_score g_stored g_turn "
                 "g_poolturn g_staged g_scattered h_dve h_const h_count h_counted h_slots",
                 dma="g_load g_store0 g_store1 g_rows0 g_rows1 g_sent0 g_sent1")
        store = [s["g_store0"], s["g_store1"]]
        staged = [s["g_rows0"], s["g_rows1"]]
        sent = [s["g_sent0"], s["g_sent1"]]
        pA, pT, pG, pC = [ps[0], ps[1]], ps[2], ps[3], ps[4:8]
        XN3v = XN3.rearrange("(i t) d -> t i d", t=P)
        blk = ctx.enter_context(nc.Block())

        def quads(u, half):
            return [(p, u * QUADS + 2 * half + p) for p in range(2)]

        def supers(eng, body, peeled=1, after=1):
            for u in range(peeled):
                body(u)
            with eng.Fori(peeled, SUPERS) as u:
                body(u)
            for u in range(SUPERS, SUPERS + after):
                body(u)

        def lagging(u, half):
            return (u - 1, 0) if half else (u - 2, 1)

        @blk.sync
        def _(sp):
            sp.dma_start(wo[:], A["L1_attn_Wo"]).then_inc(s["g_load"], 16)
            sp.dma_start(wh[:], A["L1_ffn_W_hash"][:, 0:PICKS1]).then_inc(s["g_load"], 16)
            sp.sem_inc(s["g_stored"], SEED)

            def body(u):
                for half in range(2):
                    if live(lagging(u, half)[0], SUPERS):
                        for p, m in quads(*lagging(u, half)):
                            wait_free(sp, s["g_scattered"], m, 2)
                            for j in range(QUAD):
                                tile = XN3v[:, bass.ds(m * QUAD + j, 1), :].to_broadcast([P, PICKS1, D])
                                sp.dma_start(rows[:, p, j, :, 0:D], tile).then_inc(staged[p], 16)
                    if live(u, SUPERS):
                        for p, n in quads(u, half):
                            sp.wait_ge(s["g_xn"], made(n))
                            sp.dma_start(XN3v[:, bass.ds(n * QUAD, QUAD), :], xn[:, p]).then_inc(store[p], 16)
                        for p in range(2):
                            sp.wait_ge(store[p], 16 * (2 * u + half + 1))
                            sp.sem_inc(s["g_stored"], 1)
            supers(sp, body, peeled=2, after=2)

        @blk.gpsimd
        def _(pool):
            for name in "g_rstd g_scattered g_staged".split():
                pool.sem_inc(s[name], SEED)
            nc.gpsimd.memset(carry[:], 0.0)
            nc.gpsimd.memset(extra[:], 0.0)
            nc.gpsimd.memset(fresh[:], 1.0)
            nc.gpsimd.memset(power[:], -0.5).then_inc(s["g_const"], 1)
            pool.wait_ge(s["g_const"], 1)
            nc.gpsimd.memset(fresh[:, :, 0:1], 0.0)
            nc.gpsimd.iota(dest[:], pattern=[[P * PICKS1, SUPER], [1, PICKS1]], base=0, channel_multiplier=PICKS1,
                           allow_small_or_imprecise_dtypes=True)
            nc.gpsimd.iota(expert[:], pattern=[[1, E1]], base=0, channel_multiplier=0,
                           allow_small_or_imprecise_dtypes=True).then_inc(s["h_const"], 1)

            def scatter(u, half, p):
                m, i = u * QUADS + 2 * half + p, 2 * half + p
                pool.wait_ge(s["h_slots"], made(u))
                pool.wait_ge(staged[p], 16 * QUAD * (2 * u + half + 1))
                turn(pool, s["g_poolturn"])
                quad = slice(i * QUAD, (i + 1) * QUAD)
                nc.gpsimd.tensor_copy(rows[:, p, :, :, D:ROW],
                                      extra[:, bass.ds(u, 1), quad].rearrange("p o i k c -> p (o i) k c"))
                nc.gpsimd.tensor_copy(sidx[:, p], slot[:, bass.ds(u, 1), quad].rearrange("p o i k -> p (o i) k")
                                      ).then_inc(s["g_staged"], 1)
                pool.wait_ge(s["g_staged"], made(m))
                turn(pool, s["g_poolturn"])
                for j in range(QUAD):
                    for k in range(PICKS1):
                        nc.gpsimd.indirect_dma_start(
                            out=XS1, out_offset=bass.IndirectOffsetOnAxis(ap=sidx[:, p, j, k:k + 1], axis=0),
                            in_=rows[:, p, j, k, :], in_offset=None, bounds_check=SLOTS1 - 1,
                            oob_is_err=False).then_inc(sent[p], 16)

            def body(u):
                for half in range(2):
                    if live(u, SUPERS):
                        for p, n in quads(u, half):
                            pool.wait_ge(s["g_ve"], made(n))
                            nc.gpsimd.tensor_tensor(rstd[:, p, :], ve[:, p, :], power[:], ALU.pow).then_inc(s["g_rstd"], 1)
                    v, of = lagging(u, half)
                    if live(v, SUPERS):
                        for p in range(2):
                            scatter(v, of, p)
                        for p in range(2):
                            pool.wait_ge(sent[p], 16 * QUAD * PICKS1 * (2 * v + of + 1))
                            pool.sem_inc(s["g_scattered"], 1)
            supers(pool, body, peeled=2, after=2)

        @blk.scalar
        def _(act):
            for name in "g_r g_xT".split():
                act.sem_inc(s[name], SEED)

            def body(u):
                for half in range(2):
                    ns = [n for _, n in quads(u, half)]
                    for p, n in enumerate(ns):
                        act.wait_ge(s["g_pA"], freed(n, 2))
                        nc.scalar.copy(r[:, p], readT[:, :, bass.ds(n * QUAD, QUAD)].rearrange("e b i -> e i b")).then_inc(s["g_r"], 1)
                    for p, n in enumerate(ns):
                        act.wait_ge(s["g_pT"], made(n))
                        act.wait_ge(s["g_pG"], freed(n, 2))
                        nc.scalar.copy(xT[:, p, :], pT[:]).then_inc(s["g_xT"], 1)
            supers(act, body, after=0)

        @blk.vector
        def _(dve):
            for name in "g_h g_st g_mv g_ve g_xn g_score h_count h_slots".split():
                dve.sem_inc(s[name], SEED)
            dve.wait_ge(s["h_const"], 1)

            def body(u):
                routing = iter(route(u - 1)) if live(u - 1, SUPERS) else iter(())
                if not live(u, SUPERS):
                    for _ in routing:
                        pass
                    return
                for half in range(2):
                    ns = [n for _, n in quads(u, half)]
                    for p, n in enumerate(ns):
                        rows_of = H[:, bass.ds(n * QUAD, QUAD), :]
                        dve.wait_ge(s["g_pA"], made(n))
                        nc.vector.tensor_tensor(rows_of, pA[p][:].rearrange("p (j d) -> p j d", j=QUAD),
                                                rows_of, ALU.add).then_inc(s["g_h"], 1)
                        dve.wait_ge(s["g_h"], made(n))
                        turn(dve, s["g_turn"])
                        for j in range(QUAD):
                            last = nc.vector.bn_stats(st[:, p, j, :], H[:, bass.ds(n * QUAD + j, 1), :].rearrange("p o d -> p (o d)"))
                        last.then_inc(s["g_st"], 1)
                        dve.wait_ge(s["g_st"], made(n))
                        turn(dve, s["g_turn"])
                        for j in range(QUAD):
                            last = nc.vector.bn_aggr(mv[:, p, j, :], st[:, p, j, :])
                        last.then_inc(s["g_mv"], 1)
                        dve.wait_ge(s["g_mv"], made(n))
                        nc.vector.tensor_scalar_add(ve[:, p, :], mv[:, p, :, 1], EPS).then_inc(s["g_ve"], 1)
                    next(routing, None)
                    for p, n in enumerate(ns):
                        dve.wait_ge(s["g_rstd"], made(n))
                        wait_free(dve, s["g_stored"], n, 2)
                        wait_free(dve, s["g_pT"], n, 2)
                        for j in range(QUAD):
                            last = nc.vector.tensor_scalar(xn[:, p, j, :], H[:, bass.ds(n * QUAD + j, 1), :].rearrange("p o d -> p (o d)"),
                                                           mv[:, p, j, 0:1], rstd[:, p, j:j + 1], ALU.subtract, ALU.mult)
                        last.then_inc(s["g_xn"], 1)
                    next(routing, None)
                    for p, n in enumerate(ns):
                        i = 2 * half + p
                        dve.wait_ge(s["g_pG"], made(n))
                        nc.vector.tensor_copy(score[:, i * QUAD:(i + 1) * QUAD, :],
                                              pG[:, 0:QUAD * PICKS1].rearrange("p (j c) -> p j c", j=QUAD)).then_inc(s["g_score"], 1)
                    next(routing, None)

            def route(u):
                dve.wait_ge(s["g_score"], made(u * QUADS + QUADS - 1))
                step = Chain(dve, s["h_dve"], u * BUCKET_STEPS)
                yield from route_buckets(nc.vector, step, dve, s, u, score, y, low, low_i, over, bucket, expert, hot, count,
                                         fresh, total, place, work, at, carry, pC, slot, extra, dest)
                assert step.n == BUCKET_STEPS, step.n
            supers(dve, body)

        @blk.tensor
        def _(pe):
            for name in "g_pA g_pT g_pG h_counted".split():
                pe.sem_inc(s[name], SEED)
            pe.wait_ge(s["g_load"], 32)

            def count_picks(u):
                if live(u, SUPERS):
                    pe.wait_ge(s["h_count"], made(u))
                    flat, banks = count[:].rearrange("p e i -> p (e i)"), E1 * SUPER // 512
                    for c in range(banks):
                        nc.tensor.matmul(pC[c][:], before[:], flat[:, bass.ts(c, 512)], start=True, stop=True)
                    for c in range(banks):
                        last = nc.tensor.matmul(pC[banks + c][:], ones[:], flat[:, bass.ts(c, 512)], start=True, stop=True)
                    last.then_inc(s["h_counted"], 1)

            def body(u):
                for half in range(2):
                    ns = [n for _, n in quads(u, half)]
                    for p, n in enumerate(ns):
                        pe.wait_ge(s["g_r"], made(n))
                        pe.wait_ge(s["g_h"], freed(n, 2))
                        for j in range(QUAD):
                            last = nc.tensor.matmul(pA[p][:, bass.ts(j, D)], r[:, p, j, :], wo[:], start=True, stop=True)
                        last.then_inc(s["g_pA"], 1)
                    if half == 0:
                        count_picks(u - 1)
                    for p, n in enumerate(ns):
                        pe.wait_ge(s["g_xn"], made(n))
                        pe.wait_ge(s["g_xT"], freed(n, 1))
                        for j in range(QUAD):
                            last = nc.tensor.transpose(pT[:, bass.ts(j, P)], xn[:, p, j, :], ident[:])
                        last.then_inc(s["g_pT"], 1)
                    for p, n in enumerate(ns):
                        pe.wait_ge(s["g_xT"], made(n))
                        pe.wait_ge(s["g_score"], freed(n, 1))
                        for j in range(QUAD):
                            last = nc.tensor.matmul(pG[:, j * PICKS1:(j + 1) * PICKS1], xT[:, p, bass.ts(j, P)], wh[:],
                                                    start=True, stop=True)
                        last.then_inc(s["g_pG"], 1)
            supers(pe, body, after=0)
            count_picks(SUPERS - 1)


def layer1_experts(nc, A, sems, ps, ident, XS1, YT1):
    ctx = ExitStack()
    CH = HID // P
    RING = 4
    PARTS = [(0, P), (P, P), (2 * P, CAP1 - 2 * P)]
    LAST = CAP1 - 2 * P
    with ctx:
        def sb(name, shape, dt=F32):
            return ctx.enter_context(nc.sbuf_tensor(name, shape, dt))
        w1 = sb("i_w1", [P, RING, HID])
        w2 = sb("i_w2", [P, RING, CH, D])
        b1 = sb("i_b1_t", [P, E1, CH])
        b2 = sb("i_b2", [P, RING, D])
        x = sb("i_x", [P, RING, 3, ROW])
        place = sb("i_place", [P, RING, 3], I32)
        xT = sb("i_xT_t", [P, 2, CAP1])
        h = sb("i_h_t", [P, 2, CH, CAP1])
        y = sb("i_y_t", [P, 2, 3, D])
        warm = sb("i_warm", [P, 1])
        s = sems("i_pT i_xT i_p1 i_h i_pY i_y i_sent i_turn i_place",
                 dma="i_b1 i_w0 i_w1 i_w2 i_w3 i_out0 i_out1")
        landed, out = [s[f"i_w{r}"] for r in range(RING)], [s["i_out0"], s["i_out1"]]
        pT, p1, pY = [ps[0], ps[1]], ps[2:6], [ps[6], ps[7]]
        n_dma = 5
        blk = ctx.enter_context(nc.Block())

        @blk.sync
        def _(sp):
            sp.dma_start(b1[:], A["L1_ffn_b1"]).then_inc(s["i_b1"], 16)

            def body(n, k, i):
                wait_free(sp, s["i_y"], n, RING)
                sp.dma_start(w1[:, k, :], A["L1_ffn_W1"][n]).then_inc(landed[k], 16)
                sp.dma_start(w2[:, k], A["L1_ffn_W2"][n].rearrange("(c p) d -> p c d", p=P)).then_inc(landed[k], 16)
                sp.dma_start(b2[:, k, :], A["L1_ffn_b2"][n].partition_broadcast(P)).then_inc(landed[k], 16)
                sp.dma_start(x[:, k, 0:2, :], XS1[bass.ds(n * CAP1, 2 * P), :].rearrange("(c t) d -> t c d", t=P)).then_inc(landed[k], 16)
                sp.dma_start(x[0:LAST, k, 2, :], XS1[bass.ds(n * CAP1 + 2 * P, LAST), :]).then_inc(landed[k], 16)
            pipeline(sp, E1, 0, 0, RING, body)

        @blk.gpsimd
        def _(pool):
            pool.sem_inc(s["i_sent"], SEED)

            def body(n, k, i):
                p = k % 2
                if live(n, E1):
                    pool.wait_ge(s["i_y"], made(n))
                    pool.wait_ge(s["i_place"], made(n))
                    turn(pool, s["i_turn"])
                    for t, (_, rows) in enumerate(PARTS):
                        nc.gpsimd.indirect_dma_start(
                            out=YT1, out_offset=bass.IndirectOffsetOnAxis(ap=place[0:rows, k, t:t + 1], axis=0),
                            in_=y[0:rows, p, t, :], in_offset=None, bounds_check=TOKENS * PICKS1 - 1,
                            oob_is_err=False).then_inc(out[p], 16)
                if live(n - 1, E1):
                    pool.wait_ge(out[(k - 1) % 2], 48 * (2 * i + (k - 1) // 2 + 1))
                    pool.sem_inc(s["i_sent"], 1)
            pipeline(pool, E1, 0, 1, RING, body)

        @blk.scalar
        def _(act):
            act.sem_inc(s["i_h"], CH)
            act.wait_ge(s["i_b1"], 16)
            nc.scalar.activation(warm[:], ident[:, 0:1], ACT.Gelu)

            def body(n, k, i):
                for c in range(CH):
                    act.wait_ge(s["i_p1"], made(n * CH + c))
                    if c == 0:
                        act.wait_ge(s["i_pY"], freed(n, 2))
                    nc.scalar.activation(h[:, k % 2, c, :], p1[c][:, 0:CAP1], ACT.Gelu,
                                         bias=b1[:, bass.ds(n, 1), c]).then_inc(s["i_h"], 1)
            pipeline(act, E1, 0, 0, RING, body)

        @blk.vector
        def _(dve):
            for name in "i_y i_xT i_place".split():
                dve.sem_inc(s[name], SEED)

            def body(n, k, i):
                if live(n + 1, E1):
                    m, p, r = n + 1, (k + 1) % 2, (k + 1) % RING
                    dve.wait_ge(s["i_pT"], made(m))
                    wait_free(dve, s["i_pY"], m, 2)
                    nc.vector.tensor_copy(xT[:, p, :], pT[p][:, 0:CAP1]).then_inc(s["i_xT"], 1)
                    wait_free(dve, s["i_sent"], m, RING)
                    nc.vector.tensor_copy(place[:, r, 0:2], x[:, r, 0:2, D + 1])
                    nc.vector.tensor_copy(place[0:LAST, r, 2:3], x[0:LAST, r, 2, D + 1:ROW]).then_inc(s["i_place"], 1)
                if live(n - 1, E1):
                    m, p, r = n - 1, (k - 1) % 2, (k - 1) % RING
                    dve.wait_ge(s["i_pY"], made(m))
                    dve.wait_ge(s["i_sent"], freed(m, 2))
                    nc.vector.tensor_tensor(y[:, p, 0:2, :], pY[p][:, 0:2 * D].rearrange("p (c d) -> p c d", c=2),
                                            bc(b2[:, r, :], 1, [P, 2, D]), ALU.add)
                    nc.vector.tensor_tensor(y[0:LAST, p, 2, :], pY[p][0:LAST, 2 * D:3 * D], b2[0:LAST, r, :],
                                            ALU.add).then_inc(s["i_y"], 1)
            pipeline(dve, E1, 1, 1, RING, body)

        @blk.tensor
        def _(pe):
            for name in "i_pT i_p1 i_pY".split():
                pe.sem_inc(s[name], SEED)

            def body(n, k, i):
                if live(n, E1):
                    pe.wait_ge(s["i_xT"], made(n))
                    for c in range(CH):
                        pe.wait_ge(s["i_h"], n * CH + c + 1)
                        nc.tensor.matmul(p1[c][:, 0:CAP1], w1[:, k, bass.ts(c, P)], xT[:, k % 2, :],
                                         start=True, stop=True).then_inc(s["i_p1"], 1)
                if live(n + 1, E1):
                    m, p, r = n + 1, (k + 1) % 2, (k + 1) % RING
                    pe.wait_ge(landed[r], 16 * n_dma * (i + (k + 1) // RING + 1))
                    wait_free(pe, s["i_xT"], m, 2)
                    for t, (_, rows) in enumerate(PARTS):
                        last = nc.tensor.transpose(pT[p][:, t * P:t * P + rows], x[0:rows, r, t, 0:D], ident[0:rows, 0:rows])
                    last.then_inc(s["i_pT"], 1)
                if live(n - 1, E1):
                    m, p, r = n - 1, (k - 1) % 2, (k - 1) % RING
                    pe.wait_ge(s["i_h"], CH * (m + 2))
                    pe.wait_ge(s["i_y"], freed(m, 2))
                    for t, (at, rows) in enumerate(PARTS):
                        for c in range(CH):
                            last = nc.tensor.matmul(pY[p][0:rows, t * D:(t + 1) * D], h[:, p, c, at:at + rows], w2[:, r, c, :],
                                                    start=(c == 0), stop=(c == CH - 1))
                    last.then_inc(s["i_pY"], 1)
            pipeline(pe, E1, 1, 1, RING, body)


def layer1_combine(nc, sems, H, YT1, out):
    ctx = ExitStack()
    RING = 4
    with ctx:
        def sb(name, shape, dt=F32):
            return ctx.enter_context(nc.sbuf_tensor(name, shape, dt))
        got = sb("j_got", [P, RING, QUAD, PICKS1, D])
        acc = sb("j_acc_t", [P, RING, QUAD, D])
        s = sems("j_sum j_acc", dma="j_got0 j_got1 j_got2 j_got3 j_out0 j_out1 j_out2 j_out3")
        got_in, store = [s[f"j_got{r}"] for r in range(RING)], [s[f"j_out{r}"] for r in range(RING)]
        out_v = out.rearrange("i t d -> t i d")
        Y = YT1[0:TOKENS * PICKS1, :].rearrange("(i t k) d -> t i (k d)", t=P, k=PICKS1)
        N = TILES // QUAD
        blk = ctx.enter_context(nc.Block())

        @blk.scalar
        def _(act):
            def body(n, k, i):
                wait_free(act, s["j_acc"], n, RING)
                act.dma_start(got[:, k].rearrange("t i k d -> t i (k d)"), Y[:, bass.ds(n * QUAD, QUAD), :]).then_inc(got_in[k], 16)
            pipeline(act, N, 0, 0, RING, body)

        @blk.vector
        def _(dve):
            dve.sem_inc(s["j_sum"], SEED)
            dve.sem_inc(s["j_acc"], SEED)

            def body(n, k, i):
                dve.wait_ge(got_in[k], 16 * (i + 1))
                if not isinstance(i, int) or i > 0:
                    dve.wait_ge(store[k], 16 * i)
                nc.vector.tensor_tensor(acc[:, k], got[:, k, :, 0, :], got[:, k, :, 1, :], ALU.add).then_inc(s["j_sum"], 1)
                dve.wait_ge(s["j_sum"], made(n))
                nc.vector.scalar_tensor_tensor(acc[:, k], acc[:, k], 1.0 / PICKS1, H[:, bass.ds(n * QUAD, QUAD), :],
                                               ALU.mult, ALU.add).then_inc(s["j_acc"], 1)
            pipeline(dve, N, 0, 0, RING, body)

        @blk.sync
        def _(sp):
            def body(n, k, i):
                sp.wait_ge(s["j_acc"], made(n))
                sp.dma_start(out_v[:, bass.ds(n * QUAD, QUAD), :], acc[:, k]).then_inc(store[k], 16)
            pipeline(sp, N, 0, 0, RING, body)
            for r in range(RING):
                sp.wait_ge(store[r], 16 * (N // RING))


_INPUTS = ["x", "L0_tok_w", "L0_attn_Wk", "L0_attn_bk", "L0_attn_Wq", "L0_attn_bq", "L0_attn_Wv", "L0_attn_bv",
           "L0_ffn_Wr", "L0_ffn_br", "L0_ffn_Wgate", "L0_ffn_bgate", "L0_ffn_W1", "L0_ffn_W3", "L0_ffn_W2",
           "L1_attn_Wqkv", "L1_attn_Wr", "L1_attn_Wo", "L1_attn_ln_gamma", "L1_attn_ln_beta", "L1_attn_r_w_bias",
           "L1_attn_r_r_bias", "L1_ffn_W_hash", "L1_ffn_W1", "L1_ffn_b1", "L1_ffn_W2", "L1_ffn_b2"]


def kernel(**inputs):
    import concourse.bacc as bacc
    from concourse.bass_utils import run_bass_kernel_spmd

    laid = layout({n: np.asarray(inputs[n]) for n in _INPUTS})
    nc = bacc.Bacc("TRN2", target_bir_lowering=False, num_devices=1)
    arrays, A = {}, {}
    for name, a in laid.items():
        arrays[f"in_{name}"] = a
        A[name] = nc.dram_tensor(f"in_{name}", a.shape, mybir.dt.from_np(a.dtype), kind="ExternalInput").ap()
    out = nc.dram_tensor("out", (TILES, P, D), F32, kind="ExternalOutput").ap()
    tower(nc, A, out)
    return run_bass_kernel_spmd(nc, [arrays], core_ids=[0]).results[0]["out"]
```
